# Optimizing a Trainium2 kernel written in Bass

```python
import numpy as np
import jax
import jax.numpy as jnp

def _softmax(x, axis=-1):
    return jax.nn.softmax(x, axis=axis)

def _gelu(x):
    return jax.nn.gelu(x, approximate=True)

def _silu(x):
    return jax.nn.silu(x)

def _sigmoid(x):
    return jax.nn.sigmoid(x)

def _layernorm(x, axis=-1, eps=1e-05):
    m = jnp.mean(x, axis=axis, keepdims=True)
    v = jnp.var(x, axis=axis, keepdims=True)
    return (x - m) / jnp.sqrt(v + eps)

def _scatter_add(tgt, idx, src, axis=0):
    return tgt.at[idx].add(src)

def _segment_sum(src, seg, n):
    return jax.ops.segment_sum(src, seg, n)
kernel_name = 'mk_recurrent_d1_jaxref_r8_2f67fb'

def setup_inputs(seed: int=0):
    np.random.seed(seed)
    _w = jnp.asarray

    def _L0_attn_setup():
        import jax, jax.numpy as jnp
        import numpy as np
        B, L = (2, 128)
        D_MODEL, D_CKV, D_CQ = (128, 32, 64)
        N_HEAD, D_HEAD, D_ROPE = (8, 64, 32)
        N_IDX_HEAD = 4
        K_TS, LW = (96, 64)
        ROPE_BASE = 10000.0

        def _pope(x, angles):
            cos, sin = (jnp.cos(angles), jnp.sin(angles))
            mu1, mu2 = jnp.split(jax.nn.softplus(x), 2, axis=-1)
            return jnp.concatenate([mu1 * cos - mu2 * sin, mu1 * sin + mu2 * cos], axis=-1)

        def _forward(x, W_dkv, W_uk, W_uv, W_dq, W_uq, W_qr, W_kr, W_out, idx_wq, idx_wk, idx_w, raw_delta):
            B_, L_, _ = x.shape
            c_kv = x @ W_dkv
            q_i = (x @ idx_wq).reshape(B_, L_, N_IDX_HEAD, D_HEAD)
            k_i = x @ idx_wk
            s_i = jax.nn.relu(jnp.einsum('bthd,bsd->bths', q_i, k_i))
            I = jnp.einsum('bths,h->bts', s_i, idx_w)
            qpos = jnp.arange(L_)[:, None]
            kpos = jnp.arange(L_)[None, :]
            local = (kpos >= qpos - LW + 1) & (kpos <= qpos)
            causal = kpos > qpos
            I = jnp.where(local[None], jnp.inf, I)
            I = jnp.where(causal[None], -jnp.inf, I)
            kk = min(K_TS, L_)
            _, idx = jax.lax.top_k(I, kk)
            bi = jnp.arange(B_)[:, None, None]
            key_c = (c_kv @ W_uk)[bi, idx].reshape(B_, L_, kk, N_HEAD, D_HEAD)
            value = (c_kv @ W_uv)[bi, idx].reshape(B_, L_, kk, N_HEAD, D_HEAD)
            c_q = x @ W_dq
            query_c = (c_q @ W_uq).reshape(B_, L_, N_HEAD, D_HEAD)
            half = D_ROPE // 2
            theta = 1.0 / ROPE_BASE ** (2.0 * jnp.arange(half, dtype=jnp.float32) / D_ROPE)
            delta = -2.0 * jnp.pi * jax.nn.sigmoid(raw_delta)
            angles_q = jnp.arange(L_, dtype=jnp.float32)[:, None] * theta[None, :] + delta
            query_r = _pope((c_q @ W_qr).reshape(B_, L_, N_HEAD, D_ROPE), angles_q[None, :, None, :])
            kr_sel = (x @ W_kr)[bi, idx]
            angles_k = jnp.arange(kk, dtype=jnp.float32)[:, None] * theta[None, :] + delta
            key_r = _pope(kr_sel, angles_k[None, None, :, :])
            scale = (D_HEAD + D_ROPE) ** (-0.5)
            q_c = query_c.transpose(0, 2, 1, 3)
            q_r = query_r.transpose(0, 2, 1, 3)
            k_c = key_c.transpose(0, 3, 1, 2, 4)
            v = value.transpose(0, 3, 1, 2, 4)
            scores = (jnp.einsum('bhld,bhlkd->bhlk', q_c, k_c) + jnp.einsum('bhld,blkd->bhlk', q_r, key_r)) * scale
            attn = jax.nn.softmax(scores.astype(jnp.float32), axis=-1).astype(v.dtype)
            out = jnp.einsum('bhlk,bhlkd->bhld', attn, v)
            out = out.transpose(0, 2, 1, 3).reshape(B_, L_, N_HEAD * D_HEAD)
            return out @ W_out
        key = jax.random.key(seed)
        ks = jax.random.split(key, 14)

        def w(k, shape, fan_in):
            return jax.random.normal(k, shape, dtype=jnp.float32) * fan_in ** (-0.5)
        return {'x': jax.random.normal(ks[0], (B, L, D_MODEL), dtype=jnp.float32), 'W_dkv': w(ks[1], (D_MODEL, D_CKV), D_MODEL), 'W_uk': w(ks[2], (D_CKV, N_HEAD * D_HEAD), D_CKV), 'W_uv': w(ks[3], (D_CKV, N_HEAD * D_HEAD), D_CKV), 'W_dq': w(ks[4], (D_MODEL, D_CQ), D_MODEL), 'W_uq': w(ks[5], (D_CQ, N_HEAD * D_HEAD), D_CQ), 'W_qr': w(ks[6], (D_CQ, N_HEAD * D_ROPE), D_CQ), 'W_kr': w(ks[7], (D_MODEL, D_ROPE), D_MODEL), 'W_out': w(ks[8], (N_HEAD * D_HEAD, D_MODEL), N_HEAD * D_HEAD), 'idx_wq': w(ks[9], (D_MODEL, N_IDX_HEAD * D_HEAD), D_MODEL), 'idx_wk': w(ks[10], (D_MODEL, D_HEAD), D_MODEL), 'idx_w': jnp.ones((N_IDX_HEAD,), dtype=jnp.float32), 'raw_delta': jax.random.normal(ks[11], (D_ROPE // 2,), dtype=jnp.float32) * 0.1}
    _L0_attn_in = _L0_attn_setup()

    def _L0_ffn_setup():
        import jax, jax.numpy as jnp
        import numpy as np
        DIM = 128
        DEPTH = 2
        HEADS = 8
        DIM_HEAD = 64
        WINDOW = 64
        INNER = HEADS * DIM_HEAD
        HID = int(DIM * 4 * 2 / 3)
        B, N = (2, 1024)
        QK_SCALE = 8.0

        def shift_token(t):
            t1, t2 = jnp.split(t, 2, axis=-1)
            t2 = jnp.pad(t2, ((0, 0), (1, 0), (0, 0)))[:, :-1]
            return jnp.concatenate([t1, t2], axis=-1)

        def l2norm(t):
            return t / jnp.clip(jnp.linalg.norm(t, axis=-1, keepdims=True), 1e-12)

        def rotate_half(x):
            x1, x2 = jnp.split(x, 2, axis=-1)
            return jnp.concatenate([-x2, x1], axis=-1)

        def rotary_xpos(q, k):
            n = q.shape[-2]
            half_idx = jnp.arange(0, DIM_HEAD, 2, dtype=jnp.float32)
            inv_freq = 1.0 / 10000.0 ** (half_idx / DIM_HEAD)
            t = jnp.arange(n, dtype=jnp.float32)
            freqs = t[:, None] * inv_freq[None, :]
            freqs = jnp.concatenate([freqs, freqs], axis=-1)
            base = (half_idx + 0.4 * DIM_HEAD) / (1.4 * DIM_HEAD)
            power = (t - n // 2) / float(WINDOW // 2)
            scale = base[None, :] ** power[:, None]
            scale = jnp.concatenate([scale, scale], axis=-1)
            cos, sin = (jnp.cos(freqs), jnp.sin(freqs))
            q = q * cos * scale + rotate_half(q) * sin * scale
            k = k * cos / scale + rotate_half(k) * sin / scale
            return (q, k)

        def local_attention(q, k, v):
            b, h, n, d = q.shape
            w = n // WINDOW
            bq = q.reshape(b, h, w, WINDOW, d) * QK_SCALE
            bk = k.reshape(b, h, w, WINDOW, d)
            bv = v.reshape(b, h, w, WINDOW, d)

            def look_around(t):
                p = jnp.pad(t, ((0, 0), (0, 0), (1, 0), (0, 0), (0, 0)))
                return jnp.concatenate([p[:, :, :w], p[:, :, 1:]], axis=3)
            bk, bv = (look_around(bk), look_around(bv))
            bt = jnp.arange(n).reshape(w, WINDOW)
            btp = jnp.pad(bt, ((1, 0), (0, 0)), constant_values=-1)
            btk = jnp.concatenate([btp[:w], btp[1:]], axis=1)
            sim = jnp.einsum('bhwid,bhwjd->bhwij', bq, bk)
            i = bt[:, :, None]
            j = btk[:, None, :]
            mask = (i < j) | (i > j + WINDOW) | (j == -1)
            sim = jnp.where(mask, -jnp.finfo(sim.dtype).max, sim)
            attn = jax.nn.softmax(sim, axis=-1)
            out = jnp.einsum('bhwij,bhwjd->bhwid', attn, bv)
            return out.reshape(b, h, n, d)

        def _layer(x, wqkv, qs, ksc, wo, lg, lb, w1, b1, w2, b2):
            b, n, _ = x.shape
            h = shift_token(x)
            qkv = h @ wqkv
            q, k, v = jnp.split(qkv, 3, axis=-1)
            to_heads = lambda t: t.reshape(b, n, HEADS, DIM_HEAD).transpose(0, 2, 1, 3)
            q, k, v = (to_heads(q), to_heads(k), to_heads(v))
            q = l2norm(q) * qs
            k = l2norm(k) * ksc
            q, k = rotary_xpos(q, k)
            o = local_attention(q, k, v)
            o = o.transpose(0, 2, 1, 3).reshape(b, n, INNER)
            x = x + o @ wo
            h = shift_token(x)
            mu = h.mean(-1, keepdims=True)
            var = h.var(-1, keepdims=True)
            h = (h - mu) / jnp.sqrt(var + 1e-05) * lg + lb
            h = h @ w1 + b1
            a, g = jnp.split(h, 2, axis=-1)
            h = a * jax.nn.gelu(g, approximate=False)
            x = x + h @ w2 + b2
            return x
        key = jax.random.key(seed)
        ks = jax.random.split(key, 6)
        return {'x': jax.random.normal(ks[0], (B, N, DIM), jnp.float32), 'wqkv': jax.random.normal(ks[1], (DEPTH, DIM, 3 * INNER), jnp.float32) * 0.02, 'q_scale': jnp.ones((DEPTH, DIM_HEAD), jnp.float32), 'k_scale': jnp.ones((DEPTH, DIM_HEAD), jnp.float32), 'wo': jax.random.normal(ks[2], (DEPTH, INNER, DIM), jnp.float32) * 0.02, 'ln_g': jnp.ones((DEPTH, DIM), jnp.float32), 'ln_b': jnp.zeros((DEPTH, DIM), jnp.float32), 'w1': jax.random.normal(ks[3], (DEPTH, DIM, 2 * HID), jnp.float32) * 0.02, 'b1': jnp.zeros((DEPTH, 2 * HID), jnp.float32), 'w2': jax.random.normal(ks[4], (DEPTH, HID, DIM), jnp.float32) * 0.02, 'b2': jnp.zeros((DEPTH, DIM), jnp.float32)}
    _L0_ffn_in = _L0_ffn_setup()
    _d = {'L0_attn_x': _L0_attn_in['x'], 'L0_attn_W_dkv': _L0_attn_in['W_dkv'], 'L0_attn_W_uk': _L0_attn_in['W_uk'], 'L0_attn_W_uv': _L0_attn_in['W_uv'], 'L0_attn_W_dq': _L0_attn_in['W_dq'], 'L0_attn_W_uq': _L0_attn_in['W_uq'], 'L0_attn_W_qr': _L0_attn_in['W_qr'], 'L0_attn_W_kr': _L0_attn_in['W_kr'], 'L0_attn_W_out': _L0_attn_in['W_out'], 'L0_attn_idx_wq': _L0_attn_in['idx_wq'], 'L0_attn_idx_wk': _L0_attn_in['idx_wk'], 'L0_attn_idx_w': _L0_attn_in['idx_w'], 'L0_attn_raw_delta': _L0_attn_in['raw_delta'], 'L0_ffn_wqkv': _L0_ffn_in['wqkv'], 'L0_ffn_q_scale': _L0_ffn_in['q_scale'], 'L0_ffn_k_scale': _L0_ffn_in['k_scale'], 'L0_ffn_wo': _L0_ffn_in['wo'], 'L0_ffn_ln_g': _L0_ffn_in['ln_g'], 'L0_ffn_ln_b': _L0_ffn_in['ln_b'], 'L0_ffn_w1': _L0_ffn_in['w1'], 'L0_ffn_b1': _L0_ffn_in['b1'], 'L0_ffn_w2': _L0_ffn_in['w2'], 'L0_ffn_b2': _L0_ffn_in['b2']}
    _x0 = _d['L0_attn_x']
    _d['L0_attn_x'] = jax.random.normal(jax.random.fold_in(jax.random.key(seed), 1), (4, 512, 128), dtype=_x0.dtype)
    del _x0
    return _d

def reference(L0_attn_x, L0_attn_W_dkv, L0_attn_W_uk, L0_attn_W_uv, L0_attn_W_dq, L0_attn_W_uq, L0_attn_W_qr, L0_attn_W_kr, L0_attn_W_out, L0_attn_idx_wq, L0_attn_idx_wk, L0_attn_idx_w, L0_attn_raw_delta, L0_ffn_wqkv, L0_ffn_q_scale, L0_ffn_k_scale, L0_ffn_wo, L0_ffn_ln_g, L0_ffn_ln_b, L0_ffn_w1, L0_ffn_b1, L0_ffn_w2, L0_ffn_b2):

    def _L0_attn_ref(x, W_dkv, W_uk, W_uv, W_dq, W_uq, W_qr, W_kr, W_out, idx_wq, idx_wk, idx_w, raw_delta):
        import jax, jax.numpy as jnp
        import numpy as np
        B, L = (2, 128)
        D_MODEL, D_CKV, D_CQ = (128, 32, 64)
        N_HEAD, D_HEAD, D_ROPE = (8, 64, 32)
        N_IDX_HEAD = 4
        K_TS, LW = (96, 64)
        ROPE_BASE = 10000.0

        def _pope(x, angles):
            cos, sin = (jnp.cos(angles), jnp.sin(angles))
            mu1, mu2 = jnp.split(jax.nn.softplus(x), 2, axis=-1)
            return jnp.concatenate([mu1 * cos - mu2 * sin, mu1 * sin + mu2 * cos], axis=-1)

        def _forward(x, W_dkv, W_uk, W_uv, W_dq, W_uq, W_qr, W_kr, W_out, idx_wq, idx_wk, idx_w, raw_delta):
            B_, L_, _ = x.shape
            c_kv = x @ W_dkv
            q_i = (x @ idx_wq).reshape(B_, L_, N_IDX_HEAD, D_HEAD)
            k_i = x @ idx_wk
            s_i = jax.nn.relu(jnp.einsum('bthd,bsd->bths', q_i, k_i))
            I = jnp.einsum('bths,h->bts', s_i, idx_w)
            qpos = jnp.arange(L_)[:, None]
            kpos = jnp.arange(L_)[None, :]
            local = (kpos >= qpos - LW + 1) & (kpos <= qpos)
            causal = kpos > qpos
            I = jnp.where(local[None], jnp.inf, I)
            I = jnp.where(causal[None], -jnp.inf, I)
            kk = min(K_TS, L_)
            _, idx = jax.lax.top_k(I, kk)
            bi = jnp.arange(B_)[:, None, None]
            key_c = (c_kv @ W_uk)[bi, idx].reshape(B_, L_, kk, N_HEAD, D_HEAD)
            value = (c_kv @ W_uv)[bi, idx].reshape(B_, L_, kk, N_HEAD, D_HEAD)
            c_q = x @ W_dq
            query_c = (c_q @ W_uq).reshape(B_, L_, N_HEAD, D_HEAD)
            half = D_ROPE // 2
            theta = 1.0 / ROPE_BASE ** (2.0 * jnp.arange(half, dtype=jnp.float32) / D_ROPE)
            delta = -2.0 * jnp.pi * jax.nn.sigmoid(raw_delta)
            angles_q = jnp.arange(L_, dtype=jnp.float32)[:, None] * theta[None, :] + delta
            query_r = _pope((c_q @ W_qr).reshape(B_, L_, N_HEAD, D_ROPE), angles_q[None, :, None, :])
            kr_sel = (x @ W_kr)[bi, idx]
            angles_k = jnp.arange(kk, dtype=jnp.float32)[:, None] * theta[None, :] + delta
            key_r = _pope(kr_sel, angles_k[None, None, :, :])
            scale = (D_HEAD + D_ROPE) ** (-0.5)
            q_c = query_c.transpose(0, 2, 1, 3)
            q_r = query_r.transpose(0, 2, 1, 3)
            k_c = key_c.transpose(0, 3, 1, 2, 4)
            v = value.transpose(0, 3, 1, 2, 4)
            scores = (jnp.einsum('bhld,bhlkd->bhlk', q_c, k_c) + jnp.einsum('bhld,blkd->bhlk', q_r, key_r)) * scale
            attn = jax.nn.softmax(scores.astype(jnp.float32), axis=-1).astype(v.dtype)
            out = jnp.einsum('bhlk,bhlkd->bhld', attn, v)
            out = out.transpose(0, 2, 1, 3).reshape(B_, L_, N_HEAD * D_HEAD)
            return out @ W_out
        return _forward(x, W_dkv, W_uk, W_uv, W_dq, W_uq, W_qr, W_kr, W_out, idx_wq, idx_wk, idx_w, raw_delta)

    def _L0_ffn_ref(x, wqkv, q_scale, k_scale, wo, ln_g, ln_b, w1, b1, w2, b2):
        import jax, jax.numpy as jnp
        import numpy as np
        DIM = 128
        DEPTH = 2
        HEADS = 8
        DIM_HEAD = 64
        WINDOW = 64
        INNER = HEADS * DIM_HEAD
        HID = int(DIM * 4 * 2 / 3)
        B, N = (2, 1024)
        QK_SCALE = 8.0

        def shift_token(t):
            t1, t2 = jnp.split(t, 2, axis=-1)
            t2 = jnp.pad(t2, ((0, 0), (1, 0), (0, 0)))[:, :-1]
            return jnp.concatenate([t1, t2], axis=-1)

        def l2norm(t):
            return t / jnp.clip(jnp.linalg.norm(t, axis=-1, keepdims=True), 1e-12)

        def rotate_half(x):
            x1, x2 = jnp.split(x, 2, axis=-1)
            return jnp.concatenate([-x2, x1], axis=-1)

        def rotary_xpos(q, k):
            n = q.shape[-2]
            half_idx = jnp.arange(0, DIM_HEAD, 2, dtype=jnp.float32)
            inv_freq = 1.0 / 10000.0 ** (half_idx / DIM_HEAD)
            t = jnp.arange(n, dtype=jnp.float32)
            freqs = t[:, None] * inv_freq[None, :]
            freqs = jnp.concatenate([freqs, freqs], axis=-1)
            base = (half_idx + 0.4 * DIM_HEAD) / (1.4 * DIM_HEAD)
            power = (t - n // 2) / float(WINDOW // 2)
            scale = base[None, :] ** power[:, None]
            scale = jnp.concatenate([scale, scale], axis=-1)
            cos, sin = (jnp.cos(freqs), jnp.sin(freqs))
            q = q * cos * scale + rotate_half(q) * sin * scale
            k = k * cos / scale + rotate_half(k) * sin / scale
            return (q, k)

        def local_attention(q, k, v):
            b, h, n, d = q.shape
            w = n // WINDOW
            bq = q.reshape(b, h, w, WINDOW, d) * QK_SCALE
            bk = k.reshape(b, h, w, WINDOW, d)
            bv = v.reshape(b, h, w, WINDOW, d)

            def look_around(t):
                p = jnp.pad(t, ((0, 0), (0, 0), (1, 0), (0, 0), (0, 0)))
                return jnp.concatenate([p[:, :, :w], p[:, :, 1:]], axis=3)
            bk, bv = (look_around(bk), look_around(bv))
            bt = jnp.arange(n).reshape(w, WINDOW)
            btp = jnp.pad(bt, ((1, 0), (0, 0)), constant_values=-1)
            btk = jnp.concatenate([btp[:w], btp[1:]], axis=1)
            sim = jnp.einsum('bhwid,bhwjd->bhwij', bq, bk)
            i = bt[:, :, None]
            j = btk[:, None, :]
            mask = (i < j) | (i > j + WINDOW) | (j == -1)
            sim = jnp.where(mask, -jnp.finfo(sim.dtype).max, sim)
            attn = jax.nn.softmax(sim, axis=-1)
            out = jnp.einsum('bhwij,bhwjd->bhwid', attn, bv)
            return out.reshape(b, h, n, d)

        def _layer(x, wqkv, qs, ksc, wo, lg, lb, w1, b1, w2, b2):
            b, n, _ = x.shape
            h = shift_token(x)
            qkv = h @ wqkv
            q, k, v = jnp.split(qkv, 3, axis=-1)
            to_heads = lambda t: t.reshape(b, n, HEADS, DIM_HEAD).transpose(0, 2, 1, 3)
            q, k, v = (to_heads(q), to_heads(k), to_heads(v))
            q = l2norm(q) * qs
            k = l2norm(k) * ksc
            q, k = rotary_xpos(q, k)
            o = local_attention(q, k, v)
            o = o.transpose(0, 2, 1, 3).reshape(b, n, INNER)
            x = x + o @ wo
            h = shift_token(x)
            mu = h.mean(-1, keepdims=True)
            var = h.var(-1, keepdims=True)
            h = (h - mu) / jnp.sqrt(var + 1e-05) * lg + lb
            h = h @ w1 + b1
            a, g = jnp.split(h, 2, axis=-1)
            h = a * jax.nn.gelu(g, approximate=False)
            x = x + h @ w2 + b2
            return x
        for l in range(DEPTH):
            x = _layer(x, wqkv[l], q_scale[l], k_scale[l], wo[l], ln_g[l], ln_b[l], w1[l], b1[l], w2[l], b2[l])
        return x
    x = L0_attn_x
    xn = _layernorm(x, axis=-1)
    s = _L0_attn_ref(xn, L0_attn_W_dkv, L0_attn_W_uk, L0_attn_W_uv, L0_attn_W_dq, L0_attn_W_uq, L0_attn_W_qr, L0_attn_W_kr, L0_attn_W_out, L0_attn_idx_wq, L0_attn_idx_wk, L0_attn_idx_w, L0_attn_raw_delta)
    g = _silu(_L0_ffn_ref(xn, L0_ffn_wqkv, L0_ffn_q_scale, L0_ffn_k_scale, L0_ffn_wo, L0_ffn_ln_g, L0_ffn_ln_b, L0_ffn_w1, L0_ffn_b1, L0_ffn_w2, L0_ffn_b2))
    x = x + s * g
    return x

_drawn_inputs = setup_inputs


def setup_inputs(seed=0):
    import zlib

    import numpy as np

    out = dict(_drawn_inputs(seed))
    spreads = {'L0_attn_idx_w': (1.0, 0.6),
     'L0_ffn_q_scale': (1.0, 0.6),
     'L0_ffn_k_scale': (1.0, 0.6),
     'L0_ffn_ln_g': (1.0, 0.6),
     'L0_ffn_ln_b': (0.0, 0.8),
     'L0_ffn_b1': (0.0, 0.8),
     'L0_ffn_b2': (0.0, 0.416)}
    factors = {'L0_attn_raw_delta': 8.0,
     'L0_ffn_wqkv': 8.0,
     'L0_ffn_wo': 8.0,
     'L0_ffn_w1': 8.0,
     'L0_ffn_w2': 8.0}
    for name, (base, spread) in spreads.items():
        noise = np.random.default_rng([zlib.crc32(name.encode()), seed]).standard_normal(out[name].shape)
        drawn = base * np.exp(spread * noise) if base else spread * noise
        out[name] = jnp.asarray(drawn.astype(out[name].dtype))
    for name, factor in factors.items():
        out[name] = (out[name] * factor).astype(out[name].dtype)
    return out
```

```python
from contextlib import ExitStack

import numpy as np

import concourse.bass as bass
from concourse import mybir

B, L, D = 4, 512, 128
P = 128
TILES = L // P
WIN = 64
NW_T = P // WIN
CKV, CQ, ROPE, HALF = 32, 64, 32, 16
HEADS, DH = 8, 64
IDX_HEADS = 4
TOPK = 96
FAR = TOPK - WIN
LAYERS = 2
INNER = HEADS * DH
HID = 341
HCH = [(0, 128), (128, 128), (256, HID - 256)]
PAIRS = HEADS // 2
SLOTS = 2 * WIN
SCALE = float((DH + ROPE) ** -0.5)
NEG = -1.0e30
RB = 8
GR = P // 32
LN_SHIFT = 24


class Columns:

    def __init__(self):
        self.at, self.n = {}, 0

    def add(self, name, width):
        self.at[name] = (self.n, self.n + width)
        self.n += width


def layout():
    c = Columns()
    for name, width in (("ident", P), ("pair_ones", P), ("mean_ones", P), ("istack", 32),
                        ("cos_q", L), ("sin_q", L), ("cos_k", L), ("sin_k", L),
                        ("tab_a_c", L), ("tab_a_s", L), ("tab_b_c", L), ("tab_b_s", L),
                        ("mask_f0", P), ("mask_f", P), ("mask_a0", P), ("mask_a", P), ("far_mask", P),
                        ("keep0", FAR), ("fill0", FAR), ("iota", TILES), ("sgn", 1), ("eps", 1),
                        ("tiny", 1), ("shift", 1), ("negpi", 1)):
        c.add(name, width)
    r = Columns()
    for name, width in (("rot_c", FAR * 32), ("rot_s", FAR * 32)):
        r.add(name, width)
    w = Columns()
    for name, width in (("dkv4", 128), ("dq", CQ), ("kr4", 128), ("kr4p", 128), ("idxq", IDX_HEADS * DH),
                        ("idxk2", 128), ("qr", 256), ("qrp", 256), ("qkv", LAYERS * 3 * INNER),
                        ("rot", LAYERS * 2 * INNER), ("wo", LAYERS * 4 * D), ("w1", LAYERS * 2 * HID),
                        ("w2", LAYERS * 3 * D), ("qks", LAYERS * 4), ("lng", LAYERS), ("lnb", LAYERS),
                        ("b1a", LAYERS * 3), ("b1g", LAYERS * 3), ("b2", LAYERS), ("idxw", IDX_HEADS),
                        ("delta", 1)):
        w.add(name, width)
    s = Columns()
    for name, width in (("uqT", HEADS * CQ), ("ukT", HEADS * CKV), ("uvT", HEADS * CKV), ("out", HEADS * D)):
        s.add(name, width)
    return c, r, w, s


def constants():
    c, r, _, _ = layout()
    a = np.zeros((P, c.n), np.float32)

    def put(name, v):
        a[:, c.at[name][0]:c.at[name][1]] = v
    p = np.arange(P)
    put("ident", np.eye(P))
    put("pair_ones", (p[:, None] // DH == p[None, :] // DH))
    put("mean_ones", 1.0 / D)
    put("istack", (p[:, None] % 32 == np.arange(32)[None, :]) & (p[:, None] < 96))
    t = np.arange(L, dtype=np.float32)
    half = np.arange(0, DH, 2, dtype=np.float32)
    inv = (1.0 / np.float32(10000.0) ** (half / np.float32(DH))).astype(np.float32)
    fr = (t[:, None] * inv[None, :]).astype(np.float32).astype(np.float64)
    fr = np.concatenate([fr, fr], 1)
    base = (half.astype(np.float64) + 0.4 * DH) / (1.4 * DH)
    power = (t.astype(np.float64) - L // 2) / float(WIN // 2)
    sc = base[None, :] ** power[:, None]
    sc = np.concatenate([sc, sc], 1)
    sg = np.where(np.arange(DH) < DH // 2, -1.0, 1.0)
    for name, f in (("cos_q", np.cos(fr) * sc * 8.0), ("sin_q", np.sin(fr) * sc * 8.0 * sg),
                    ("cos_k", np.cos(fr) / sc), ("sin_k", np.sin(fr) / sc * sg)):
        put(name, np.tile(f.T, (2, 1)))
    theta = 1.0 / 10000.0 ** (2.0 * np.arange(HALF) / ROPE)
    theta = theta.astype(np.float32).astype(np.float64)
    sgn = np.where(p % ROPE < HALF, -1.0, 1.0)
    th = theta[p % HALF]
    pos = np.arange(L)
    for name, q in (("tab_a", pos), ("tab_b", np.where(pos < WIN, pos, 2 * pos - (WIN - 1)))):
        put(name + "_c", np.cos(th[:, None] * q[None, :]))
        put(name + "_s", np.sin(th[:, None] * q[None, :]) * sgn[:, None])
    m, s = (p % WIN)[:, None], np.arange(SLOTS)[None, :]
    first = (p < WIN)[:, None]
    f = (s >= m) & (s <= m + WIN)
    al = (s >= m + 1) & (s <= m + WIN)
    put("mask_f", np.where(f, 0.0, NEG))
    put("mask_f0", np.where(f & ~(first & (s < WIN)), 0.0, NEG))
    put("mask_a", np.where(al, 0.0, NEG))
    put("mask_a0", np.where(np.where(first, s >= WIN, al), 0.0, NEG))
    put("far_mask", np.where(p[None, :] <= p[:, None], 0.0, NEG))
    j = np.arange(FAR)[None, :]
    keep = j < (p[:, None] - (WIN - 1))
    put("keep0", keep)
    put("fill0", np.where(keep, 0, WIN + j))
    put("iota", p[:, None] + P * np.arange(TILES)[None, :])
    put("sgn", sgn[:, None])
    put("eps", 1e-5)
    put("tiny", 2.0 ** -62)
    put("shift", 0.5 * LN_SHIFT * np.log(2.0))
    put("negpi", -np.pi)
    rot = np.zeros((32, r.n), np.float32)
    ang = (WIN + np.arange(FAR))[:, None] * theta[None, :]
    rc = np.zeros((32, FAR, 32))
    rs = np.zeros((32, FAR, 32))
    for i in range(HALF):
        lo, hi = i, i + HALF
        rc[lo, :, lo] = rc[hi, :, hi] = np.cos(ang[:, i])
        rs[lo, :, lo] = rs[hi, :, hi] = -np.sin(ang[:, i])
        rc[hi, :, lo], rc[lo, :, hi] = -np.sin(ang[:, i]), np.sin(ang[:, i])
        rs[hi, :, lo], rs[lo, :, hi] = -np.cos(ang[:, i]), np.cos(ang[:, i])
    rot[:, r.at["rot_c"][0]:r.at["rot_c"][1]] = rc.reshape(32, -1)
    rot[:, r.at["rot_s"][0]:r.at["rot_s"][1]] = rs.reshape(32, -1)
    return a, rot


class Region:

    def __init__(self, full):
        self.full, self.jobs, self.read = full, {}, None

    def start(self, pe, job, read, count):
        assert job not in self.jobs, job
        self.jobs[job] = len(self.jobs) + 1
        if self.read:
            pe.wait_ge(*self.read)
        self.read = (read, count)

    def nth(self, job):
        return self.jobs[job]

class Signals:

    def __init__(self, sem):
        self.x_loaded = sem("x_loaded")
        self.dve_step = sem("dve_step")
        self.var_ready = sem("var_ready")
        self.lnv_ready = sem("lnv_ready")
        self.rstd_ready = sem("rstd_ready")
        self.xn_ready = sem("xn_ready")
        self.xnT_ready = sem("xnT_ready")
        self.qi_ready = sem("qi_ready")
        self.ki_ready = sem("ki_ready")
        self.relu_ready = sem("relu_ready")
        self.relu_used = sem("relu_used")
        self.far_idx_ready = sem("far_idx_ready")
        self.far_idx_stored = sem("far_idx_stored")
        self.hT_ready = sem("hT_ready")
        self.sq_ready = sem("sq_ready")
        self.ln_ready = sem("ln_ready")
        self.rn_ready = sem("rn_ready")
        self.parts_ready = sem("parts_ready")
        self.ab_ready = sem("ab_ready")
        self.qk_ready = sem("qk_ready")
        self.v_ready = sem("v_ready")
        self.masked_ready = sem("masked_ready")
        self.max_ready = sem("max_ready")
        self.prob_ready = sem("prob_ready")
        self.recip_ready = sem("recip_ready")
        self.prob_normed = sem("prob_normed")
        self.pT_ready = sem("pT_ready")
        self.o_ready = sem("o_ready")
        self.x1_ready = sem("x1_ready")
        self.hc_ready = sem("hc_ready")
        self.sqh_ready = sem("sqh_ready")
        self.lnh_ready = sem("lnh_ready")
        self.rstdh_ready = sem("rstdh_ready")
        self.hn_ready = sem("hn_ready")
        self.hng_ready = sem("hng_ready")
        self.gelu_ready = sem("gelu_ready")
        self.hid_ready = sem("hid_ready")
        self.x2_ready = sem("x2_ready")
        self.l_step = sem("l_step")
        self.cq_ready = sem("cq_ready")
        self.keys_zeroed = sem("keys_zeroed")
        self.ckvs_ready = sem("ckvs_ready")
        self.qc_ready = sem("qc_ready")
        self.abs_ready = sem("abs_ready")
        self.expn_ready = sem("expn_ready")
        self.log_ready = sem("log_ready")
        self.soft_ready = sem("soft_ready")
        self.krT_ready = sem("krT_ready")
        self.qb_ready = sem("qb_ready")
        self.qa_ready = sem("qa_ready")
        self.hi_ready = sem("hi_ready")
        self.rest_ready = sem("rest_ready")
        self.mid_ready = sem("mid_ready")
        self.lo_ready = sem("lo_ready")
        self.q3_stored = sem("q3_stored")
        self.pool_prod = sem("pool_prod")
        self.d_step = sem("d_step")
        self.idx_loaded0 = sem("idx_loaded0")
        self.idx_loaded1 = sem("idx_loaded1")
        self.q3_loaded = sem("q3_loaded")
        self.onehot_ready = sem("onehot_ready")
        self.kc_ready = sem("kc_ready")
        self.kr_far_ready = sem("kr_far_ready")
        self.lmasked = sem("lmasked")
        self.far_ready = sem("far_ready")
        self.vfar_ready = sem("vfar_ready")
        self.joined = sem("joined")
        self.jmax_ready = sem("jmax_ready")
        self.bias_ready = sem("bias_ready")
        self.jprob_ready = sem("jprob_ready")
        self.jrecip_ready = sem("jrecip_ready")
        self.jnormed = sem("jnormed")
        self.jpT_ready = sem("jpT_ready")
        self.blocks_ready = sem("blocks_ready")
        self.oT_ready = sem("oT_ready")
        self.fT_ready = sem("fT_ready")
        self.out_ready = sem("out_ready")
        self.out_stored = sem("out_stored")
        self.x_full = sem("x_full")
        self.y_full = sem("y_full")
        self.z_full = sem("z_full")
        self.w_full = sem("w_full")
        self.u_full = sem("u_full")
        self.regions = [self.x_full, self.y_full, self.z_full, self.w_full, self.u_full]


class Core:
    pass


def project(nc, b, k, scope):
    F, U32 = mybir.dt.float32, mybir.dt.uint32
    ALU, ACT, AX = mybir.AluOpType, mybir.ActivationFunctionType, mybir.AxisListType
    a, C, W = k.sems, k.C, k.W

    def sb(name, shape, dt=F):
        return k.sb(name, shape, dt, scope)
    xn = sb("xn", [P, TILES, D])
    stats, mv, lnv, rstd = sb("stats", [P, TILES, 6]), sb("mv", [P, TILES, 2]), sb("lnv", [P, TILES]), sb("rstd", [P, TILES])
    qiT, kiT = sb("qiT", [P, 2, L]), sb("kiT", [P, L])
    relu = sb("relu", [P, 2, 2, L])
    score, best = sb("score", [P, L]), sb("best", [P, FAR])
    idx_u, idx_f, idx_t = sb("idx_u", [P, FAR], U32), sb("idx_f", [P, FAR]), sb("idx_t", [P, FAR])
    hT = sb("hT", [P, WIN + L])
    sq, lnr, rn = sb("sq", [P, 2, L]), sb("lnr", [P, L]), sb("rn", [P, 2, L])
    pa, pb, ab = sb("pa", [P, 2, L]), sb("pb", [P, 2, L]), sb("ab", [P, 2, L])
    qT, kT = sb("qT", [P, PAIRS, L]), sb("kT", [P, PAIRS, WIN + L])
    v = sb("v", [P, NW_T, TILES, INNER])
    S = sb("S", [P, 2, HEADS, SLOTS])
    nmax, rsum, rrec = sb("nmax", [P, 2, HEADS]), sb("rsum", [P, 2, HEADS]), sb("rrec", [P, 2, HEADS])
    pT, oT = sb("pT", [P, 2, HEADS, P]), sb("oT", [P, PAIRS, L])
    x1, x2 = sb("x1", [P, 1 + L]), sb("x2", [P, 1 + L])
    hc, hn, hng = sb("hc", [P, L]), sb("hn", [P, L]), sb("hng", [P, L])
    gl, hid = sb("gl", [P, 2, L]), sb("hid", [P, 3, L])
    rX, rY, rZ = Region(a.x_full), Region(a.y_full), Region(a.z_full)
    rW, rU = Region(a.w_full), Region(a.u_full)

    def pair(n):
        return (k.X, rX) if n % 2 == 0 else (k.Y, rY)

    def place(h):
        return (h % 2) * PAIRS + h // 2

    def far_width(i):
        return WIN + P * i

    def tile(i):
        return slice(i * P, (i + 1) * P)

    with nc.Block() as block:
        @block.tensor
        def _(pe):
            mm = nc.tensor.matmul
            rZ.start(pe, "xnT", a.xnT_ready, 1)
            pe.wait_ge(a.xn_ready, TILES)
            for i in range(TILES):
                last = nc.tensor.transpose(k.Z[:, 0, tile(i)], xn[:, i, :], C("ident"))
            last.then_inc(rZ.full, 1)
            pe.wait_ge(a.xnT_ready, 1)
            rX.start(pe, "qi", a.qi_ready, 1)
            for c in range(2):
                last = mm(k.X[:, c, :], W("idxq", c * P, P), k.xnT[:, WIN:], start=True, stop=True)
            last.then_inc(rX.full, 1)
            rY.start(pe, "ki", a.ki_ready, 1)
            mm(k.Y[:, 0, :], W("idxk2"), k.xnT[:, WIN:], start=True, stop=True).then_inc(rY.full, 1)
            pe.wait_ge(a.qi_ready, 1)
            pe.wait_ge(a.ki_ready, 1)
            for i in range(TILES):
                for hp in range(2):
                    reg, r = pair(hp)
                    r.start(pe, f"idx{i}.{hp}", a.relu_ready, 2 * i + hp + 1)
                    for j in range(2):
                        last = mm(reg[:, j, 0:far_width(i)], qiT[64 * j:64 * j + 64, hp, tile(i)],
                                  kiT[64 * j:64 * j + 64, 0:far_width(i)], start=True, stop=True)
                    last.then_inc(r.full, 1)

            def qk(l, n):
                c, which = n // 2, n % 2
                reg, r = pair(n)
                r.start(pe, f"qk{l}.{n}", a.parts_ready, 8 * l + n + 1)
                mm(reg[:, 0, :], W("qkv", l * 3 * INNER + which * INNER + c * P, P), hT[:, WIN:], start=True, stop=True)
                mm(reg[:, 1, :], W("rot", l * 2 * INNER + which * INNER + c * P, P), hT[:, WIN:],
                   start=True, stop=True).then_inc(r.full, 1)

            def square_sums(l, n):
                reg, r = (k.Wb, rW) if n % 2 == 0 else (k.Ub, rU)
                r.start(pe, f"ss{l}.{n}", a.ln_ready, 8 * l + n + 1)
                pe.wait_ge(a.sq_ready, 8 * l + n + 1)
                mm(reg, C("pair_ones"), sq[:, n % 2, :], start=True, stop=True).then_inc(r.full, 1)

            def values(l, i):
                rZ.start(pe, f"v{l}.{i}", a.v_ready, TILES * l + i + 1)
                for par in range(2):
                    at = WIN + i * P - WIN * (1 - par)
                    last = mm(k.Z[:, par, :], hT[:, at:at + P], W("qkv", l * 3 * INNER + 2 * INNER, INNER),
                              start=True, stop=True)
                last.then_inc(rZ.full, 1)

            def scores(l, i):
                reg, r = pair(i)
                r.start(pe, f"s{l}.{i}", a.masked_ready, TILES * l + i + 1)
                pe.wait_ge(a.qk_ready, 8 * l + 8)
                for h in range(HEADS):
                    r0, c = 64 * (h % 2), h // 2
                    for w in range(NW_T):
                        t0 = i * P + w * WIN
                        last = mm(reg[64 * w:64 * w + 64, h % 2, c * P:(c + 1) * P],
                                  qT[r0:r0 + 64, c, t0:t0 + WIN], kT[r0:r0 + 64, c, t0:t0 + SLOTS],
                                  start=True, stop=True)
                last.then_inc(r.full, 1)

            def prob_T(l, i):
                rZ.start(pe, f"t{l}.{i}", a.pT_ready, TILES * l + i + 1)
                pe.wait_ge(a.prob_normed, TILES * l + i + 1)
                for u in range(HEADS):
                    last = nc.tensor.transpose(k.Z[:, u // 4, (u % 4) * P:(u % 4 + 1) * P], S[:, i % 2, u, :], C("ident"))
                last.then_inc(rZ.full, 1)

            def weigh_values(l, i):
                rW.start(pe, f"o{l}.{i}", a.o_ready, TILES * l + i + 1)
                pe.wait_ge(a.pT_ready, TILES * l + i + 1)
                for h in range(HEADS):
                    for w in range(NW_T):
                        last = mm(k.Wb[64 * (h % 2):64 * (h % 2) + 64, (h // 2) * P + w * WIN:(h // 2) * P + (w + 1) * WIN],
                                  v[:, w, i, h * DH:(h + 1) * DH], pT[:, i % 2, place(h), w * WIN:(w + 1) * WIN],
                                  start=True, stop=True)
                last.then_inc(rW.full, 1)

            for l in range(LAYERS):
                pe.wait_ge(a.hT_ready, 2 * l + 1)
                for n in range(8):
                    qk(l, n)
                    if n:
                        square_sums(l, n - 1)
                    if n % 2:
                        values(l, n // 2)
                square_sums(l, 7)
                pe.wait_ge(a.v_ready, TILES * (l + 1))
                scores(l, 0)
                for i in range(TILES):
                    if i + 1 < TILES:
                        scores(l, i + 1)
                    prob_T(l, i)
                    weigh_values(l, i)
                rU.start(pe, f"wo{l}", a.x1_ready, l + 1)
                pe.wait_ge(a.o_ready, TILES * (l + 1))
                for c in range(PAIRS):
                    last = mm(k.Ub, W("wo", (l * PAIRS + c) * D, D), oT[:, c, :], start=(c == 0), stop=(c == PAIRS - 1))
                last.then_inc(rU.full, 1)
                rX.start(pe, f"mean{l}", a.hc_ready, l + 1)
                pe.wait_ge(a.hT_ready, 2 * l + 2)
                mm(k.X[:, 0, :], C("mean_ones"), hT[:, WIN:], start=True, stop=True).then_inc(rX.full, 1)
                rY.start(pe, f"var{l}", a.lnh_ready, l + 1)
                pe.wait_ge(a.sqh_ready, l + 1)
                mm(k.Y[:, 0, :], C("mean_ones"), sq[:, 0, :], start=True, stop=True).then_inc(rY.full, 1)
                pe.wait_ge(a.hng_ready, l + 1)
                for j, (off, n) in enumerate(HCH):
                    reg, r = pair(j)
                    r.start(pe, f"up{l}.{j}", a.hid_ready, 3 * l + j + 1)
                    mm(reg[0:n, 0, :], W("w1", l * 2 * HID + HID + off, n), hng[:, :], start=True, stop=True)
                    mm(reg[0:n, 1, :], W("w1", l * 2 * HID + off, n), hng[:, :], start=True, stop=True).then_inc(r.full, 1)
                rU.start(pe, f"down{l}", a.x2_ready, l + 1)
                for j, (off, n) in enumerate(HCH):
                    pe.wait_ge(a.hid_ready, 3 * l + j + 1)
                    last = mm(k.Ub, W("w2", (l * 3 + j) * D, D, rows=n), hid[0:n, j, :], start=(j == 0), stop=(j == 2))
                last.then_inc(rU.full, 1)

        @block.sync
        def _(sp):
            sp.dma_start(k.x_in[:, :, :], k.x_d[bass.ds(b, 1), :, :].rearrange("a (i p) d -> p (a i) d", p=P)).then_inc(a.x_loaded, 16)
            sp.wait_ge(a.far_idx_ready, 1)
            for g in range(GR):
                sp.dma_start(k.scratch.rearrange("r (i g t) -> g r i t", g=GR, t=32)[g],
                             k.idx_h[32 * g:32 * g + 32, :, :]).then_inc(a.far_idx_stored, 16)
            sp.wait_ge(a.far_idx_stored, 16 * GR)

        @block.gpsimd
        def _(pool):
            for l in range(LAYERS):
                for n in range(8):
                    pool.wait_ge(a.parts_ready, 8 * l + n + 1)
                    nc.gpsimd.tensor_tensor(ab[:, n % 2, :], pa[:, n % 2, :], pb[:, n % 2, :], ALU.add).then_inc(a.ab_ready, 1)
                for i in range(TILES):
                    pool.wait_ge(a.recip_ready, TILES * l + i + 1)
                    nc.gpsimd.tensor_tensor(S[:, i % 2, :, :], S[:, i % 2, :, :],
                                            rrec[:, i % 2, :].unsqueeze(2).broadcast_to([P, HEADS, SLOTS]),
                                            ALU.mult).then_inc(a.prob_normed, 1)

        @block.scalar
        def _(act):
            op = nc.scalar.activation
            act.wait_ge(a.var_ready, 1)
            op(lnv[:, :], mv[:, :, 1], ACT.Ln, bias=C("eps")).then_inc(a.lnv_ready, 1)
            act.wait_ge(a.lnv_ready, 1)
            op(rstd[:, :], lnv[:, :], ACT.Exp, scale=-0.5).then_inc(a.rstd_ready, 1)
            act.wait_ge(rZ.full, rZ.nth("xnT"))
            op(k.xnT[:, WIN:], k.Z[:, 0, :], ACT.Copy).then_inc(a.xnT_ready, 1)
            act.wait_ge(rX.full, rX.nth("qi"))
            op(qiT[:, :, :], k.X, ACT.Copy).then_inc(a.qi_ready, 1)
            act.wait_ge(rY.full, rY.nth("ki"))
            op(kiT[:, :], k.Y[:, 0, :], ACT.Copy).then_inc(a.ki_ready, 1)
            for i in range(TILES):
                for hp in range(2):
                    reg, r = pair(hp)
                    act.wait_ge(r.full, r.nth(f"idx{i}.{hp}"))
                    if i:
                        act.wait_ge(a.relu_used, 2 * (i - 1) + hp + 1)
                    op(relu[:, hp, :, 0:far_width(i)], reg[:, :, 0:far_width(i)], ACT.Relu).then_inc(a.relu_ready, 1)

            def norm(l, n):
                reg, r = (k.Wb, rW) if n % 2 == 0 else (k.Ub, rU)
                act.wait_ge(r.full, r.nth(f"ss{l}.{n}"))
                if 8 * l + n:
                    act.wait_ge(a.rn_ready, 8 * l + n)
                op(lnr[:, :], reg, ACT.Ln, bias=C("tiny"), scale=float(2 ** LN_SHIFT)).then_inc(a.ln_ready, 1)
                act.wait_ge(a.ln_ready, 8 * l + n + 1)
                if 8 * l + n >= 2:
                    act.wait_ge(a.qk_ready, 8 * l + n - 1)
                op(rn[:, n % 2, :], lnr[:, :], ACT.Exp, bias=C("shift"), scale=-0.5).then_inc(a.rn_ready, 1)

            def exps(l, i):
                act.wait_ge(a.max_ready, TILES * l + i + 1)
                for h in range(HEADS):
                    last = op(S[:, i % 2, h, :], S[:, i % 2, h, :], ACT.Exp, bias=nmax[:, i % 2, h:h + 1],
                              accum_out=rsum[:, i % 2, h:h + 1])
                last.then_inc(a.prob_ready, 1)

            def copy_pT(l, i):
                act.wait_ge(rZ.full, rZ.nth(f"t{l}.{i}"))
                if i >= 2:
                    act.wait_ge(a.o_ready, TILES * l + i - 1)
                op(pT[:, i % 2, :, :], k.Z.rearrange("p a (h t) -> p (a h) t", h=4), ACT.Copy).then_inc(a.pT_ready, 1)

            for l in range(LAYERS):
                for n in range(8):
                    reg, r = pair(n)
                    act.wait_ge(r.full, r.nth(f"qk{l}.{n}"))
                    op(sq[:, n % 2, :], reg[:, 0, :], ACT.Square).then_inc(a.sq_ready, 1)
                    if n:
                        norm(l, n - 1)
                    if n % 2:
                        i = n // 2
                        act.wait_ge(rZ.full, rZ.nth(f"v{l}.{i}"))
                        op(v[:, :, i, :], k.Z, ACT.Copy).then_inc(a.v_ready, 1)
                norm(l, 7)
                exps(l, 0)
                exps(l, 1)
                copy_pT(l, 0)
                exps(l, 2)
                copy_pT(l, 1)
                exps(l, 3)
                copy_pT(l, 2)
                copy_pT(l, 3)
                act.wait_ge(a.hc_ready, l + 1)
                op(sq[:, 0, :], hc[:, :], ACT.Square).then_inc(a.sqh_ready, 1)
                act.wait_ge(rY.full, rY.nth(f"var{l}"))
                op(lnr[:, :], k.Y[:, 0, :], ACT.Ln, bias=C("eps")).then_inc(a.lnh_ready, 1)
                act.wait_ge(a.lnh_ready, l + 1)
                op(rn[:, 0, :], lnr[:, :], ACT.Exp, scale=-0.5).then_inc(a.rstdh_ready, 1)
                act.wait_ge(a.hn_ready, l + 1)
                op(hng[:, :], hn[:, :], ACT.Identity, bias=W("lnb", l, 1), scale=W("lng", l, 1)).then_inc(a.hng_ready, 1)
                for j, (off, n) in enumerate(HCH):
                    reg, r = pair(j)
                    act.wait_ge(r.full, r.nth(f"up{l}.{j}"))
                    if j >= 2:
                        act.wait_ge(a.hid_ready, 3 * l + j - 1)
                    op(gl[0:n, j % 2, :], reg[0:n, 0, :], ACT.Gelu, bias=W("b1g", 3 * l + j, 1, rows=n)).then_inc(a.gelu_ready, 1)

            act.wait_ge(a.x2_ready, LAYERS)
            op(k.gate[:, :], x2[:, 1:], ACT.Silu)

        @block.vector
        def _(dve):
            ve = nc.vector
            step = [0]

            def link(ins):
                step[0] += 1
                ins.then_inc(a.dve_step, 1)
                dve.wait_ge(a.dve_step, step[0])
            link(ve.memset(hT[:, 0:WIN], 0.0))
            link(ve.memset(kT[:, :, 0:WIN], 0.0))
            link(ve.memset(x1[:, 0:1], 0.0))
            link(ve.memset(x2[:, 0:1], 0.0))
            dve.wait_ge(a.x_loaded, 16)
            for i in range(TILES):
                link(ve.bn_stats(stats[:, i, :], k.x_in[:, i, :]))
                ins = ve.bn_aggr(mv[:, i, :], stats[:, i, :])
            ins.then_inc(a.var_ready, 1)
            dve.wait_ge(a.rstd_ready, 1)
            for i in range(TILES):
                ve.tensor_scalar(xn[:, i, :], k.x_in[:, i, :], mv[:, i, 0:1], rstd[:, i:i + 1], ALU.subtract,
                                 ALU.mult).then_inc(a.xn_ready, 1)
            for i in range(TILES):
                n = far_width(i)
                for hp in range(2):
                    dve.wait_ge(a.relu_ready, 2 * i + hp + 1)
                    for j in range(2):
                        h = 2 * hp + j
                        if h == 0:
                            link(ve.tensor_scalar(score[:, 0:n], relu[:, 0, 0, 0:n], W("idxw", 0, 1), None, ALU.mult))
                        elif j == 0:
                            link(ve.scalar_tensor_tensor(score[:, 0:n], relu[:, hp, j, 0:n], W("idxw", h, 1),
                                                         score[:, 0:n], ALU.mult, ALU.add))
                        else:
                            ve.scalar_tensor_tensor(score[:, 0:n], relu[:, hp, j, 0:n], W("idxw", h, 1),
                                                    score[:, 0:n], ALU.mult, ALU.add).then_inc(a.relu_used, 1)
                            dve.wait_ge(a.relu_used, 2 * i + hp + 1)
                c0 = max(n - P, 0)
                link(ve.tensor_tensor(score[:, c0:n], score[:, c0:n], C("far_mask")[:, P - (n - c0):], ALU.add))
                for q in range(FAR // 8):
                    e = slice(8 * q, 8 * q + 8)
                    link(ve.max(best[:, e], score[:, 0:n]))
                    link(ve.max_index(idx_u[:, e], best[:, e], score[:, 0:n]))
                    if q < FAR // 8 - 1:
                        link(ve.match_replace(score[:, 0:n], best[:, e], score[:, 0:n], -3.0e38))
                link(ve.tensor_copy(idx_f[:, :], idx_u[:, :]))
                if i == 0:
                    link(ve.tensor_tensor(idx_f[:, :], idx_f[:, :], C("keep0"), ALU.mult))
                    link(ve.tensor_tensor(idx_f[:, :], idx_f[:, :], C("fill0"), ALU.add))
                link(ve.transpose(idx_t[:, :], idx_f[:, :]))
                ins = ve.tensor_copy(k.idx_h[:, i, :], idx_t[:, :])
                if i < TILES - 1:
                    link(ins)
            ins.then_inc(a.far_idx_ready, 1)

            def shift_tokens(src, off):
                link(ve.tensor_copy(hT[0:64, WIN:], src[0:64, off:off + L]))
                ve.tensor_copy(hT[64:128, WIN:], src[64:128, off - 1:off - 1 + L]).then_inc(a.hT_ready, 1)

            def parts(l, n):
                reg, r = pair(n)
                cos, sin = (("cos_q", "sin_q"), ("cos_k", "sin_k"))[n % 2]
                dve.wait_ge(r.full, r.nth(f"qk{l}.{n}"))
                link(ve.scalar_tensor_tensor(pb[:, n % 2, :], reg[:, 1, :], W("qks", 4 * l + 2 * (n % 2) + 1, 1), C(sin),
                                             ALU.mult, ALU.mult))
                dve.wait_ge(a.sq_ready, 8 * l + n + 1)
                ve.scalar_tensor_tensor(pa[:, n % 2, :], reg[:, 0, :], W("qks", 4 * l + 2 * (n % 2), 1), C(cos),
                                        ALU.mult, ALU.mult).then_inc(a.parts_ready, 1)

            def normed(l, n):
                dve.wait_ge(a.ab_ready, 8 * l + n + 1)
                dve.wait_ge(a.rn_ready, 8 * l + n + 1)
                dst = qT[:, n // 2, :] if n % 2 == 0 else kT[:, n // 2, WIN:]
                ve.scalar_tensor_tensor(dst, rn[:, n % 2, :], 1.0e12, ab[:, n % 2, :], ALU.min,
                                        ALU.mult).then_inc(a.qk_ready, 1)

            def mask_max(l, i):
                reg, r = pair(i)
                dve.wait_ge(r.full, r.nth(f"s{l}.{i}"))
                ve.tensor_tensor(S[:, i % 2, :, :], reg.rearrange("p a (h s) -> p (a h) s", h=4),
                                 C("mask_f0" if i == 0 else "mask_f").unsqueeze(1).broadcast_to([P, HEADS, SLOTS]),
                                 ALU.add).then_inc(a.masked_ready, 1)
                dve.wait_ge(a.masked_ready, TILES * l + i + 1)
                ve.tensor_reduce(nmax[:, i % 2, :], S[:, i % 2, :, :], AX.X, ALU.max, negate=True).then_inc(a.max_ready, 1)

            def recips(l, i):
                dve.wait_ge(a.prob_ready, TILES * l + i + 1)
                ve.reciprocal(rrec[:, i % 2, :], rsum[:, i % 2, :]).then_inc(a.recip_ready, 1)

            def copy_o(l, i):
                dve.wait_ge(rW.full, rW.nth(f"o{l}.{i}"))
                ve.tensor_copy(oT[:, :, tile(i)], k.Wb.rearrange("p (c t) -> p c t", c=PAIRS)).then_inc(a.o_ready, 1)

            x, off = k.xnT, WIN
            for l in range(LAYERS):
                shift_tokens(x, off)
                for n in range(8):
                    parts(l, n)
                    if n:
                        normed(l, n - 1)
                normed(l, 7)
                mask_max(l, 0)
                recips(l, 0)
                mask_max(l, 1)
                recips(l, 1)
                copy_o(l, 0)
                mask_max(l, 2)
                recips(l, 2)
                copy_o(l, 1)
                mask_max(l, 3)
                recips(l, 3)
                copy_o(l, 2)
                copy_o(l, 3)
                dve.wait_ge(rU.full, rU.nth(f"wo{l}"))
                ve.tensor_tensor(x1[:, 1:], k.Ub, x[:, off:off + L], ALU.add).then_inc(a.x1_ready, 1)
                dve.wait_ge(a.x1_ready, l + 1)
                shift_tokens(x1, 1)
                dve.wait_ge(rX.full, rX.nth(f"mean{l}"))
                ve.tensor_tensor(hc[:, :], hT[:, WIN:], k.X[:, 0, :], ALU.subtract).then_inc(a.hc_ready, 1)
                dve.wait_ge(a.rstdh_ready, l + 1)
                ve.tensor_tensor(hn[:, :], hc[:, :], rn[:, 0, :], ALU.mult).then_inc(a.hn_ready, 1)
                for j, (o, n) in enumerate(HCH):
                    reg, r = pair(j)
                    dve.wait_ge(r.full, r.nth(f"up{l}.{j}"))
                    dve.wait_ge(a.gelu_ready, 3 * l + j + 1)
                    ve.scalar_tensor_tensor(hid[0:n, j, :], reg[0:n, 1, :], W("b1a", 3 * l + j, 1, rows=n),
                                            gl[0:n, j % 2, :], ALU.add, ALU.mult).then_inc(a.hid_ready, 1)
                dve.wait_ge(rU.full, rU.nth(f"down{l}"))
                ve.scalar_tensor_tensor(x2[:, 1:], k.Ub, W("b2", l, 1), x1[:, 1:], ALU.add, ALU.add).then_inc(a.x2_ready, 1)
                dve.wait_ge(a.x2_ready, l + 1)
                x, off = x2, 1


def latents(nc, b, k, scope):
    F, BF = mybir.dt.float32, mybir.dt.bfloat16
    ALU, ACT = mybir.AluOpType, mybir.ActivationFunctionType
    a, C, W = k.sems, k.C, k.W

    def sb(name, shape, dt=F):
        return k.sb(name, shape, dt, scope)
    cqT = sb("cqT", [CQ, L])
    mag, soft = sb("mag", [P, 2, L]), sb("soft", [P, 3, 2, L])
    prod = sb("prod", [P, 2, L])
    pprod = sb("pprod", [P, 2, L])
    qa, krot = sb("qa", [P, 2, L]), sb("krot", [P, L])
    q3s = sb("q3s", [P, 2, 2, 3, L], BF)
    rest = sb("rest", [P, 2, FAR * 32])
    rX, rY, rZ, rW = Region(a.x_full), Region(a.y_full), Region(a.z_full), Region(a.w_full)
    rU = Region(a.u_full)
    SOFT = ("kr", "qr0", "qr1")

    def tile(i):
        return slice(i * P, (i + 1) * P)

    def soft_region(n):
        return (k.X, rX) if n % 2 == 0 else (k.Y, rY)

    def rank_region(j):
        return (k.Y, rY) if j % 2 == 0 else (k.X, rX)

    def xr_parts(j):
        return [k.XR[:, j, :, 32 * q:32 * q + 32] for q in range(3)]
    jobs = [(k.ckvS[:, :, 1, :], [k.CX[:, :, 32 * q:32 * q + 32] for q in range(3)], "r i d")]
    jobs += [(rank_region(j)[0].rearrange("p a (r d) -> p (a r) d", d=32), xr_parts(j), None) for j in range(TILES)]
    jobs += [(k.qcT[:, c, :], [q3s[:, 0, c, q, :] for q in range(3)], None) for c in range(2)]
    jobs += [(qa[:, c, :], [q3s[:, 1, c, q, :] for q in range(3)], None) for c in range(2)]

    def rest_of(s):
        src = jobs[s][0]
        if s == 0:
            return rest[:, 0, 0:TILES * 32].rearrange("p (i d) -> p i d", d=32)
        if s <= TILES:
            return rest[:, s % 2, :].rearrange("p (r d) -> p r d", d=32)
        return rest[:, s % 2, 0:L]

    with nc.Block() as block:
        @block.tensor
        def _(pe):
            mm = nc.tensor.matmul
            xnT = k.xnT[:, WIN:]
            rX.start(pe, "kr", a.soft_ready, 1)
            mm(k.X[:, 0, :], W("kr4"), xnT, start=True, stop=True)
            mm(k.X[:, 1, :], W("kr4p"), xnT, start=True, stop=True).then_inc(rX.full, 1)
            rZ.start(pe, "ckv", a.cq_ready, 1)
            mm(k.Z[0:CQ, 1, :], W("dq"), xnT, start=True, stop=True)
            mm(k.Z[:, 0, :], W("dkv4"), xnT, start=True, stop=True).then_inc(rZ.full, 1)
            rW.start(pe, "ckvs", a.ckvs_ready, 1)
            for i in range(TILES):
                for w in range(NW_T):
                    at = i * P + WIN * w
                    last = mm(k.Wb[:, (NW_T * i + w) * 32:(NW_T * i + w + 1) * 32], k.xnT[:, at:at + P],
                              W("dkv4", 0, CKV), start=True, stop=True)
            last.then_inc(rW.full, 1)
            pe.wait_ge(a.cq_ready, 1)
            for c in range(2):
                reg, r = soft_region(c + 1)
                r.start(pe, f"qr{c}", a.soft_ready, c + 2)
                mm(reg[:, 0, :], W("qr", c * P, P, rows=CQ), cqT[:, :], start=True, stop=True)
                mm(reg[:, 1, :], W("qrp", c * P, P, rows=CQ), cqT[:, :], start=True, stop=True).then_inc(r.full, 1)
            rU.start(pe, "qc0", a.qc_ready, 1)
            mm(k.Ub, k.m1[:, 0:P], cqT[:, :], start=True, stop=True).then_inc(rU.full, 1)
            rU.start(pe, "qc1", a.qc_ready, 2)
            mm(k.Ub, k.m1[:, P:2 * P], cqT[:, :], start=True, stop=True).then_inc(rU.full, 1)
            pe.wait_ge(a.soft_ready, 1)
            for j in range(TILES):
                reg, r = rank_region(j)
                r.start(pe, f"xr{j}", a.rest_ready, j + 2)
                for e in range(2):
                    last = mm(reg[:, e, :], soft[0:32, 0, 0, tile(j)], k.rot_tab[:, e * 512:(e + 1) * 512],
                              start=True, stop=True)
                last.then_inc(r.full, 1)

        @block.scalar
        def _(act):
            op = nc.scalar.activation

            def softplus_log(n):
                reg, r = soft_region(n)
                act.wait_ge(r.full, r.nth(SOFT[n]))
                if n:
                    act.wait_ge(a.soft_ready, n)
                op(mag[:, :, :], reg, ACT.Abs).then_inc(a.abs_ready, 1)
                act.wait_ge(a.abs_ready, n + 1)
                op(mag[:, :, :], mag[:, :, :], ACT.Exp, scale=-1.0).then_inc(a.expn_ready, 1)
                act.wait_ge(a.expn_ready, n + 1)
                op(mag[:, :, :], mag[:, :, :], ACT.Ln, bias=1.0).then_inc(a.log_ready, 1)

            def hi(s):
                if s == 0:
                    act.wait_ge(a.ckvs_ready, 1)
                elif s <= TILES:
                    reg, r = rank_region(s - 1)
                    act.wait_ge(r.full, r.nth(f"xr{s - 1}"))
                elif s <= TILES + 2:
                    act.wait_ge(a.qc_ready, s - TILES)
                else:
                    act.wait_ge(a.qa_ready, s - TILES - 2)
                op(jobs[s][1][0], jobs[s][0], ACT.Copy).then_inc(a.hi_ready, 1)

            def mid(s):
                act.wait_ge(a.rest_ready, s + 1)
                op(jobs[s][1][1], rest_of(s), ACT.Copy).then_inc(a.mid_ready, 1)

            softplus_log(0)
            act.wait_ge(rZ.full, rZ.nth("ckv"))
            act.wait_ge(a.keys_zeroed, 1)
            for g in range(GR):
                rows = slice(32 * g, 32 * g + 32)
                op(k.key_c[rows, g, WIN:], k.Z[rows, 0, :], ACT.Copy)
            op(cqT[:, :], k.Z[0:CQ, 1, :], ACT.Copy).then_inc(a.cq_ready, 1)
            softplus_log(1)
            softplus_log(2)
            for c in range(2):
                act.wait_ge(rU.full, rU.nth(f"qc{c}"))
                op(k.qcT[:, c, :], k.Ub, ACT.Copy).then_inc(a.qc_ready, 1)
            hi(0)
            for s in range(1, len(jobs)):
                hi(s)
                mid(s - 1)
            mid(len(jobs) - 1)

        @block.gpsimd
        def _(pool):
            tt = nc.gpsimd.tensor_tensor
            for c in range(2):
                pool.wait_ge(a.soft_ready, c + 2)
                tt(pprod[:, 0, :], soft[:, c + 1, 0, :], C("tab_b_c"), ALU.mult).then_inc(a.pool_prod, 1)
                tt(pprod[:, 1, :], soft[:, c + 1, 1, :], C("tab_b_s"), ALU.mult).then_inc(a.pool_prod, 1)
                pool.wait_ge(a.pool_prod, 2 * c + 2)
                tt(k.qrB[:, c, :], pprod[:, 0, :], pprod[:, 1, :], ALU.add).then_inc(a.qb_ready, 1)
                pool.wait_ge(a.qb_ready, c + 1)

        @block.vector
        def _(dve):
            ve = nc.vector
            step = [0]

            def link(ins):
                step[0] += 1
                ins.then_inc(a.l_step, 1)
                dve.wait_ge(a.l_step, step[0])

            def softplus(n):
                reg, r = soft_region(n)
                dve.wait_ge(a.log_ready, n + 1)
                ve.scalar_tensor_tensor(soft[:, n, :, :], reg, 0.0, mag[:, :, :], ALU.max,
                                        ALU.add).then_inc(a.soft_ready, 1)
                dve.wait_ge(a.soft_ready, n + 1)

            def rotate(dst, n, done):
                link(ve.tensor_tensor(prod[:, 0, :], soft[:, n, 0, :], C("tab_a_c"), ALU.mult))
                link(ve.tensor_tensor(prod[:, 1, :], soft[:, n, 1, :], C("tab_a_s"), ALU.mult))
                ve.tensor_tensor(dst, prod[:, 0, :], prod[:, 1, :], ALU.add).then_inc(done, 1)

            def take_hi(s):
                dve.wait_ge(a.hi_ready, s + 1)
                if s >= 2:
                    dve.wait_ge(a.lo_ready, s - 1)
                ve.tensor_tensor(rest_of(s), jobs[s][0], jobs[s][1][0], ALU.subtract).then_inc(a.rest_ready, 1)

            def lo(s):
                dve.wait_ge(a.mid_ready, s + 1)
                ve.tensor_tensor(jobs[s][1][2], rest_of(s), jobs[s][1][1], ALU.subtract).then_inc(a.lo_ready, 1)

            link(ve.memset(k.key_r[:, :, :], 0.0))
            ve.memset(k.key_c[:, :, :], 0.0).then_inc(a.keys_zeroed, 1)
            softplus(0)
            rotate(krot[:, :], 0, a.krT_ready)
            dve.wait_ge(a.krT_ready, 1)
            for g in range(GR):
                rows = slice(32 * g, 32 * g + 32)
                link(ve.tensor_copy(k.key_r[rows, g, WIN:], krot[rows, :]))
            dve.wait_ge(rW.full, rW.nth("ckvs"))
            ve.tensor_copy(k.ckvS[:, :, :, :], k.Wb[:, 0:TILES * NW_T * 32].rearrange("p (i w d) -> p i w d", w=NW_T, d=32)).then_inc(a.ckvs_ready, 1)
            softplus(1)
            rotate(qa[:, 0, :], 1, a.qa_ready)
            softplus(2)
            rotate(qa[:, 1, :], 2, a.qa_ready)
            take_hi(0)
            for s in range(1, TILES + 1):
                take_hi(s)
                lo(s - 1)
            for s in range(TILES + 1, len(jobs)):
                take_hi(s)
                lo(s - 1)
            lo(len(jobs) - 1)

        @block.sync
        def _(sp):
            sp.wait_ge(a.lo_ready, len(jobs))
            for kind in range(2):
                for c in range(2):
                    sp.dma_start(k.q_scratch[kind, :, c * P:(c + 1) * P, :].rearrange("q p t -> p q t"),
                                 q3s[:, kind, c, :, :]).then_inc(a.q3_stored, 16)
            sp.wait_ge(a.q3_stored, 64)


def attend(nc, b, k, scope):
    F, BF, FH = mybir.dt.float32, mybir.dt.bfloat16, mybir.dt.float16
    ALU, ACT, AX = mybir.AluOpType, mybir.ActivationFunctionType, mybir.AxisListType
    a, C, W = k.sems, k.C, k.W

    def sb(name, shape, dt=F):
        return k.sb(name, shape, dt, scope)
    QTR = FAR // RB
    NF = TILES * QTR
    OCT = 4
    idxb = sb("idxb", [P, 2, RB * P], FH)
    onehot = sb("onehot", [P, 2, TILES, RB * P], BF)
    KC, KR = sb("KC", [96, 32, P], BF), sb("KR", [96, 32, P], BF)
    q3 = sb("q3", [96, 2, 24, P], BF)
    V = sb("V", [P, 32, CKV])
    J = SLOTS + FAR
    SC = sb("SC", [P, 2, HEADS, J])
    SN = sb("SN", [P, HEADS, 32])
    nmax, bias = sb("jmax", [P, HEADS]), sb("jbias", [P, HEADS])
    rsum, rrec = sb("jsum", [P, HEADS]), sb("jrec", [P, HEADS])
    PT, PN = sb("PT", [P, HEADS, P]), sb("PN", [P, HEADS, 32])
    PB = sb("PB", [P, 32, GR, HEADS])
    OT = sb("OT", [CKV, 2, 512])
    fT, o_sb = sb("fT", [P, P]), sb("o_sb", [P, 2, D])
    rX, rY, rZ, rW = Region(a.x_full), Region(a.y_full), Region(a.z_full), Region(a.w_full)
    O2 = k.PS[:, 6:8, :]

    def tile(i):
        return slice(i * P, (i + 1) * P)

    def quad_region(o):
        return (k.Y, rY) if o % 2 == 0 else (k.Z, rZ)

    with nc.Block() as block:
        @block.tensor
        def _(pe):
            mm = nc.tensor.matmul

            def fetch(n):
                i, q = n // QTR, n % QTR
                pe.wait_ge(a.onehot_ready, n + 1)
                rZ.start(pe, f"gc{n}", a.kc_ready, n + 1)
                for e in range(2):
                    for j in range(i + 1):
                        last = mm(k.Z[0:96, e, :], k.CX[:, j, :], onehot[:, n % 2, j, e * 512:(e + 1) * 512],
                                  start=(j == 0), stop=(j == i))
                last.then_inc(rZ.full, 1)
                rY.start(pe, f"gr{n}", a.kr_far_ready, n + 1)
                for r in range(RB):
                    for j in range(i + 1):
                        last = mm(k.Y[0:96, r // 4, (r % 4) * P:(r % 4 + 1) * P], k.XR[:, j, q * RB + r, :],
                                  onehot[:, n % 2, j, r * P:(r + 1) * P], start=(j == 0), stop=(j == i))
                last.then_inc(rY.full, 1)

            def local_scores(i):
                rX.start(pe, f"ls{i}", a.lmasked, i + 1)
                for h in range(HEADS):
                    c, s0 = h // 4, (h % 4) * P
                    for w in range(NW_T):
                        t0 = i * P + w * WIN
                        out = k.X[64 * w:64 * w + 64, c, s0:s0 + P]
                        mm(out, k.qcT[:, c, t0:t0 + WIN], k.key_c[:, h % 4, t0:t0 + SLOTS], start=True, stop=False)
                        last = mm(out, k.qrB[:, c, t0:t0 + WIN], k.key_r[:, h % 4, t0:t0 + SLOTS], start=False, stop=True)
                last.then_inc(rX.full, 1)

            def far_scores(i, o):
                reg, r = quad_region(o)
                r.start(pe, f"fs{i}.{o}", a.far_ready, OCT * i + o + 1)
                if o == 0:
                    pe.wait_ge(a.kc_ready, QTR * (i + 1))
                    pe.wait_ge(a.kr_far_ready, QTR * (i + 1))
                    pe.wait_ge(a.q3_loaded, 96 * (i + 1))
                for q in range(8):
                    t, out = 8 * o + q, reg[:, q // 4, (q % 4) * P:(q % 4 + 1) * P]
                    mm(out[:, 96:P], KC[:, t, :], k.istack[:, :], start=True, stop=True)
                    mm(out[:, 0:96], KC[:, t, :], q3[:, 0, :, t::32], start=True, stop=False)
                    last = mm(out[:, 0:96], KR[:, t, :], q3[:, 1, :, t::32], start=False, stop=True)
                last.then_inc(r.full, 1)

            def probs_T(i):
                rX.start(pe, f"lt{i}", a.jpT_ready, i + 1)
                pe.wait_ge(a.jnormed, i + 1)
                for h in range(HEADS):
                    last = nc.tensor.transpose(k.X[:, h // 4, (h % 4) * P:(h % 4 + 1) * P], SC[:, i % 2, h, 0:SLOTS], C("ident"))
                last.then_inc(rX.full, 1)

            def weigh(i):
                rW.start(pe, f"pv{i}", a.oT_ready, i + 1)
                pe.wait_ge(a.jpT_ready, i + 1)
                pe.wait_ge(a.blocks_ready, i + 1)
                for e in range(2):
                    for w in range(NW_T):
                        mm(O2[0:CKV, e, :].rearrange("p (t g h) -> p t g h", g=GR, h=HEADS)[:, :, 2 * w:2 * w + 2, :],
                           k.ckvS[:, i, w, :],
                           PT[:, :, :].rearrange("p h (g t) -> p t g h", g=GR)[:, 16 * e:16 * e + 16, 2 * w:2 * w + 2, :],
                           start=(w == 0), stop=False, skip_group_check=True)
                    for t in range(16 * e, 16 * e + 16):
                        last = mm(O2[0:CKV, e, (t % 16) * 32:(t % 16 + 1) * 32], V[:, t, :],
                                  PB[:, t, :, :].rearrange("p g h -> p (g h)"), start=False, stop=True,
                                  skip_group_check=True)
                last.then_inc(rW.full, 1)

            def project_out(i):
                rX.start(pe, f"so{i}", a.fT_ready, i + 1)
                pe.wait_ge(a.oT_ready, i + 1)
                heads = OT[:, :, :].rearrange("p a (t g h) -> p h g (a t)", g=GR, h=HEADS)
                for h in range(HEADS):
                    last = mm(k.X[:, 0, 0:P], k.mo[:, h * D:(h + 1) * D], heads[:, h, :, :],
                              start=(h == 0), stop=(h == HEADS - 1))
                last.then_inc(rX.full, 1)
                rX.start(pe, f"fin{i}", a.out_ready, i + 1)
                pe.wait_ge(a.fT_ready, i + 1)
                nc.tensor.transpose(k.X[:, 1, 0:P], fT[:, :], C("ident")).then_inc(rX.full, 1)

            for n in range(QTR):
                fetch(n)
            for i in range(TILES):
                local_scores(i)
                for o in range(OCT):
                    far_scores(i, o)
                if i + 1 < TILES:
                    for n in range(QTR * (i + 1), QTR * (i + 2)):
                        fetch(n)
                probs_T(i)
                weigh(i)
                project_out(i)

        @block.sync
        def _(sp):
            loads = (a.idx_loaded0, a.idx_loaded1)

            def load_q3(i):
                for kind in range(2):
                    for part in range(3):
                        sp.dma_start(q3[32 * part:32 * part + 32, kind, :, :],
                                     k.q_scratch[kind, :, :, tile(i)].rearrange("q (c d) t -> d (q c) t", d=32)
                                     ).then_inc(a.q3_loaded, 16)

            def load_idx(n):
                i, q = n // QTR, n % QTR
                if n >= 2:
                    sp.wait_ge(a.onehot_ready, n - 1)
                sp.dma_start(idxb[:, n % 2, :].rearrange("p (r t) -> p r t", r=RB),
                             k.scratch[q * RB:(q + 1) * RB, tile(i)].partition_broadcast(P)).then_inc(loads[n % 2], 16)
            load_idx(0)
            load_idx(1)
            load_q3(0)
            for n in range(2, QTR + 2):
                load_idx(n)
            for i in range(TILES):
                if i + 1 < TILES:
                    sp.wait_ge(a.far_ready, OCT * (i + 1))
                    load_q3(i + 1)
                    for n in range(QTR * (i + 1) + 2, min(QTR * (i + 2) + 2, NF)):
                        load_idx(n)
                sp.wait_ge(a.out_ready, i + 1)
                sp.dma_start(k.out_d[bass.ds(b, 1), tile(i), :].rearrange("a p d -> (a p) d"), o_sb[:, i % 2, :]).then_inc(a.out_stored, 16)
            sp.wait_ge(a.out_stored, 16 * TILES)

        @block.gpsimd
        def _(pool):
            for i in range(TILES):
                pool.wait_ge(a.jrecip_ready, i + 1)
                nc.gpsimd.tensor_tensor(SC[:, i % 2, :, :], SC[:, i % 2, :, :],
                                        rrec[:, :].unsqueeze(2).broadcast_to([P, HEADS, J]), ALU.mult).then_inc(a.jnormed, 1)

        @block.scalar
        def _(act):
            op = nc.scalar.activation

            def keep_content(n):
                q = n % QTR
                act.wait_ge(rZ.full, rZ.nth(f"gc{n}"))
                op(KC[:, :, :].rearrange("p t (g r) -> p r g t", g=GR)[:, q * RB:(q + 1) * RB, :, :],
                   k.Z[0:96, :, :].rearrange("p a (r g t) -> p (a r) g t", g=GR, t=32), ACT.Copy).then_inc(a.kc_ready, 1)

            for n in range(QTR):
                keep_content(n)
            for i in range(TILES):
                for o in range(OCT):
                    reg, r = quad_region(o)
                    act.wait_ge(r.full, r.nth(f"fs{i}.{o}"))
                    if o == 0 and i:
                        act.wait_ge(a.oT_ready, i)
                    op(V[:, 8 * o:8 * o + 8, :], reg.rearrange("p a (q c) -> p (a q) c", c=P)[:, :, 96:P],
                       ACT.Copy).then_inc(a.vfar_ready, 1)
                act.wait_ge(a.bias_ready, i + 1)
                for h in range(HEADS):
                    last = op(SC[:, i % 2, h, :], SC[:, i % 2, h, :], ACT.Exp, bias=bias[:, h:h + 1], scale=SCALE,
                              accum_out=rsum[:, h:h + 1])
                last.then_inc(a.jprob_ready, 1)
                if i + 1 < TILES:
                    for n in range(QTR * (i + 1), QTR * (i + 2)):
                        keep_content(n)
                act.wait_ge(rX.full, rX.nth(f"lt{i}"))
                op(PT[:, :, :], k.X.rearrange("p a (h t) -> p (a h) t", h=4), ACT.Copy).then_inc(a.jpT_ready, 1)
                act.wait_ge(rW.full, rW.nth(f"pv{i}"))
                op(OT[:, :, :], O2[0:CKV, :, :], ACT.Copy).then_inc(a.oT_ready, 1)

        @block.vector
        def _(dve):
            ve = nc.vector
            loads = (a.idx_loaded0, a.idx_loaded1)
            step = [0]

            def link(ins):
                step[0] += 1
                ins.then_inc(a.d_step, 1)
                dve.wait_ge(a.d_step, step[0])

            def one_hots(n):
                i = n // QTR
                dve.wait_ge(loads[n % 2], 16 * (n // 2 + 1))
                for j in range(i + 1):
                    last = ve.tensor_scalar(onehot[:, n % 2, j, :], idxb[:, n % 2, :], C("iota")[:, j:j + 1], None, ALU.is_equal)
                last.then_inc(a.onehot_ready, 1)

            def keep_rope(n):
                q = n % QTR
                dve.wait_ge(rY.full, rY.nth(f"gr{n}"))
                ve.tensor_copy(KR[:, :, :].rearrange("p t (g r) -> p r g t", g=GR)[:, q * RB:(q + 1) * RB, :, :],
                               k.Y[0:96, :, :].rearrange("p a (r g t) -> p (a r) g t", g=GR, t=32)).then_inc(a.kr_far_ready, 1)

            link(ve.memset(PB[:, :, :, :], 0.0))
            one_hots(0)
            one_hots(1)
            for n in range(QTR):
                keep_rope(n)
                one_hots(n + 2)
            for i in range(TILES):
                dve.wait_ge(rX.full, rX.nth(f"ls{i}"))
                ve.tensor_tensor(SC[:, i % 2, :, 0:SLOTS], k.X.rearrange("p a (h s) -> p (a h) s", h=4),
                                 C("mask_a0" if i == 0 else "mask_a").unsqueeze(1).broadcast_to([P, HEADS, SLOTS]),
                                 ALU.add).then_inc(a.lmasked, 1)
                for o in range(OCT):
                    reg, r = quad_region(o)
                    dve.wait_ge(r.full, r.nth(f"fs{i}.{o}"))
                    dve.wait_ge(a.vfar_ready, OCT * i + o + 1)
                    for g in range(GR):
                        part = reg[32 * g:32 * g + 32, :, :].rearrange("p a (q c) -> p (a q) c", c=P)[:, :, 0:96]
                        part = part.rearrange("p q (k h g) -> p q h k g", k=3, g=GR)[:, :, :, :, g]
                        last = ve.tensor_reduce(SN[32 * g:32 * g + 32, :, 8 * o:8 * o + 8].rearrange("p h t -> p t h"),
                                                part, AX.X, ALU.add)
                    last.then_inc(a.far_ready, 1)
                dve.wait_ge(a.far_ready, OCT * (i + 1))
                ve.transpose(SC[:, i % 2, :, SLOTS:J], SN[:, :, :]).then_inc(a.joined, 1)
                dve.wait_ge(a.joined, i + 1)
                dve.wait_ge(a.lmasked, i + 1)
                ve.tensor_reduce(nmax[:, :], SC[:, i % 2, :, :], AX.X, ALU.max, negate=True).then_inc(a.jmax_ready, 1)
                dve.wait_ge(a.jmax_ready, i + 1)
                ve.tensor_scalar(bias[:, :], nmax[:, :], SCALE, None, ALU.mult).then_inc(a.bias_ready, 1)
                nxt = range(QTR * (i + 1), QTR * (i + 2)) if i + 1 < TILES else []
                for m, n in enumerate(nxt):
                    keep_rope(n)
                    if n + 2 < NF:
                        one_hots(n + 2)
                    if m == 0:
                        dve.wait_ge(a.jprob_ready, i + 1)
                        ve.reciprocal(rrec[:, :], rsum[:, :]).then_inc(a.jrecip_ready, 1)
                if not nxt:
                    dve.wait_ge(a.jprob_ready, i + 1)
                    ve.reciprocal(rrec[:, :], rsum[:, :]).then_inc(a.jrecip_ready, 1)
                dve.wait_ge(a.jnormed, i + 1)
                link(ve.transpose(PN[:, :, :], SC[:, i % 2, :, SLOTS:J]))
                if i:
                    dve.wait_ge(a.oT_ready, i)
                for g in range(GR):
                    e = slice(32 * g, 32 * g + 32)
                    last = ve.tensor_copy(PB[e, :, g, :], PN[e, :, :].rearrange("p h t -> p t h"))
                last.then_inc(a.blocks_ready, 1)
                dve.wait_ge(rX.full, rX.nth(f"so{i}"))
                ve.tensor_tensor(fT[:, :], k.X[:, 0, 0:P], k.gate[:, tile(i)], ALU.mult).then_inc(a.fT_ready, 1)
                dve.wait_ge(rX.full, rX.nth(f"fin{i}"))
                if i >= 2:
                    dve.wait_ge(a.out_stored, 16 * (i - 1))
                ve.tensor_tensor(o_sb[:, i % 2, :], k.X[:, 1, 0:P], k.x_in[:, i, :], ALU.add).then_inc(a.out_ready, 1)


def build(nc, x_d, const_d, rot_d, weights_d, setup_d, scratch, q_scratch, out_d):
    F, BF, FH, U32 = mybir.dt.float32, mybir.dt.bfloat16, mybir.dt.float16, mybir.dt.uint32
    ALU, ACT, AX = mybir.AluOpType, mybir.ActivationFunctionType, mybir.AxisListType
    cc, rr, ww, ss = layout()
    top = ExitStack()
    with top:
        def sb(name, shape, dt=F, ctx=top):
            return ctx.enter_context(nc.sbuf_tensor(name, shape, dt))

        def sem(name):
            return top.enter_context(nc.semaphore(name))

        consts = sb("consts", [P, cc.n])
        wts = sb("wts", [P, ww.n])
        rot_tab = sb("rot_tab", [32, FAR * 32])
        istack = sb("istack_bf", [96, 32], BF)
        m1 = sb("m1", [CQ, HEADS * CKV])
        mo = sb("mo", [CKV, HEADS * D])
        x_in = sb("x_in", [P, TILES, D])
        xnT = sb("xnT", [P, WIN + L])
        gate = sb("gate", [P, L])
        idx_h = sb("idx_h", [P, TILES, 32], FH)

        def C(name, rows=P):
            return consts[0:rows, cc.at[name][0]:cc.at[name][1]]

        def W(name, lo=0, width=None, r0=0, rows=P):
            s = ww.at[name][0] + lo
            return wts[r0:r0 + rows, s:(ww.at[name][1] if width is None else s + width)]

        PS = top.enter_context(nc.psum_tensor("PS", [P, 8, 512], F))
        X, Y, Z, Wb, Ub = PS[:, 0:2, :], PS[:, 2:4, :], PS[:, 4:6, :], PS[:, 6, :], PS[:, 7, :]

        loaded, setup_pe, setup_act, setup_dve = (sem(n) for n in ("loaded", "setup_pe", "setup_act", "setup_dve"))
        with ExitStack() as scope:
            rots = sb("rots", [32, rr.n], F, scope)
            setw = sb("setw", [64, ss.n], F, scope)
            sig = sb("sig", [P, 8], F, scope)
            tmp_t = sb("tmp_t", [P, L], F, scope)

            def S(name, lo, width):
                s = ss.at[name][0] + lo
                return setw[0:64, s:s + width]

            with nc.Block() as block:
                @block.sync
                def _(sp):
                    sp.dma_start(consts[:, :], const_d).then_inc(loaded, 16)
                    sp.dma_start(wts[:, :], weights_d).then_inc(loaded, 16)
                    sp.dma_start(setw[:, :], setup_d).then_inc(loaded, 16)
                    sp.dma_start(rots[:, :], rot_d).then_inc(loaded, 16)

                @block.tensor
                def _(pe):
                    pe.wait_ge(loaded, 64)
                    for h in range(HEADS):
                        nc.tensor.matmul(PS[0:CQ, 0, h * CKV:(h + 1) * CKV], S("uqT", h * CQ, CQ),
                                         S("ukT", h * CKV, CKV), start=True, stop=True)
                        nc.tensor.matmul(PS[0:CKV, 2 + h // 4, (h % 4) * D:(h % 4 + 1) * D],
                                         S("uvT", h * CKV, CKV), S("out", h * D, D),
                                         start=True, stop=True).then_inc(setup_pe, 1)

                @block.scalar
                def _(act):
                    act.wait_ge(loaded, 64)
                    nc.scalar.activation(sig[:, 0:1], W("delta"), ACT.Sigmoid).then_inc(setup_act, 1)
                    act.wait_ge(setup_act, 1)
                    nc.scalar.activation(sig[:, 1:2], sig[:, 0:1], ACT.Sin, bias=C("negpi"),
                                         scale=float(2 * np.pi)).then_inc(setup_act, 1)
                    nc.scalar.activation(sig[:, 2:3], sig[:, 0:1], ACT.Sin, scale=float(np.pi)).then_inc(setup_act, 1)

                @block.vector
                def _(dve):
                    n = [0]

                    def link(ins):
                        n[0] += 1
                        ins.then_inc(setup_dve, 1)
                        dve.wait_ge(setup_dve, n[0])
                    dve.wait_ge(loaded, 64)
                    link(nc.vector.memset(xnT[:, 0:WIN], 0.0))
                    link(nc.vector.tensor_copy(istack[:, :], C("istack", 96)))
                    dve.wait_ge(setup_act, 3)
                    link(nc.vector.tensor_tensor(sig[:, 3:4], sig[:, 2:3], sig[:, 2:3], ALU.mult))
                    link(nc.vector.tensor_scalar(sig[:, 4:5], sig[:, 3:4], -2.0, 1.0, ALU.mult, ALU.add))
                    link(nc.vector.tensor_tensor(sig[:, 5:6], sig[:, 1:2], C("sgn"), ALU.mult))
                    link(nc.vector.tensor_scalar(sig[:, 6:7], sig[:, 5:6], -1.0, None, ALU.mult))
                    cosd, sins, neg_sins = sig[:, 4:5], sig[:, 5:6], sig[:, 6:7]
                    for tab in ("tab_a", "tab_b"):
                        tc, ts = C(tab + "_c"), C(tab + "_s")
                        link(nc.vector.tensor_scalar(tmp_t[:, :], tc, sins, None, ALU.mult))
                        link(nc.vector.tensor_scalar(tc, tc, cosd, None, ALU.mult))
                        link(nc.vector.scalar_tensor_tensor(tc, ts, neg_sins, tc, ALU.mult, ALU.add))
                        link(nc.vector.scalar_tensor_tensor(ts, ts, cosd, tmp_t[:, :], ALU.mult, ALU.add))
                    link(nc.vector.tensor_scalar(rot_tab[:, :], rots[:, 0:FAR * 32], sig[0:32, 4:5], None, ALU.mult))
                    link(nc.vector.scalar_tensor_tensor(rot_tab[:, :], rots[:, FAR * 32:], sig[0:32, 1:2],
                                                        rot_tab[:, :], ALU.mult, ALU.add))
                    dve.wait_ge(setup_pe, HEADS)
                    link(nc.vector.tensor_copy(m1[:, :], PS[0:CQ, 0, 0:HEADS * CKV]))
                    link(nc.vector.tensor_copy(mo[:, :], PS[0:CKV, 2:4, :].rearrange("p a b -> p (a b)")))
        nc.all_engine_barrier()

        k = Core()
        k.sb, k.C, k.W, k.PS, k.X, k.Y, k.Z, k.Wb, k.Ub = sb, C, W, PS, X, Y, Z, Wb, Ub
        k.x_in, k.xnT, k.gate, k.idx_h, k.istack, k.m1, k.mo, k.rot_tab = x_in, xnT, gate, idx_h, istack, m1, mo, rot_tab
        k.x_d, k.out_d, k.scratch, k.q_scratch = x_d, out_d, scratch, q_scratch
        every = []

        def loop_sem(name):
            every.append(sem(name))
            return every[-1]
        k.sems = Signals(loop_sem)

        def clear_regions():
            nc.all_engine_barrier()
            for s in k.sems.regions:
                nc.gpsimd.sem_clear(s)
            nc.all_engine_barrier()

        with nc.Fori(0, B) as b:
            with ExitStack() as scope:
                project(nc, b, k, scope)
            clear_regions()
            with ExitStack() as kept:
                k.key_c, k.key_r = sb("key_c", [P, GR, WIN + L], F, kept), sb("key_r", [P, GR, WIN + L], F, kept)
                k.qcT, k.qrB = sb("qcT", [P, 2, L], F, kept), sb("qrB", [P, 2, L], F, kept)
                k.CX, k.ckvS = sb("CX", [P, TILES, 96], BF, kept), sb("ckvS", [P, TILES, NW_T, CKV], F, kept)
                k.XR = sb("XR", [P, TILES, FAR, 96], BF, kept)
                with ExitStack() as scope:
                    latents(nc, b, k, scope)
                clear_regions()
                with ExitStack() as scope:
                    attend(nc, b, k, scope)
            nc.all_engine_barrier()
            for s in every:
                nc.gpsimd.sem_clear(s)
            nc.all_engine_barrier()


def kernel(**inputs):
    import concourse.bacc as bacc
    from concourse.bass_utils import run_bass_kernel_spmd

    v = {n: np.asarray(a) for n, a in inputs.items()}
    g = {n[len("L0_attn_"):]: a for n, a in v.items() if n.startswith("L0_attn_")}
    f = {n[len("L0_ffn_"):]: a for n, a in v.items() if n.startswith("L0_ffn_")}
    _, _, ww, ss = layout()
    consts, rots = constants()

    def rows(m, n=P):
        return np.concatenate([m, np.zeros((n - m.shape[0],) + m.shape[1:], np.float32)], 0) if m.shape[0] < n else m

    def swap(m, h):
        s = m.reshape(m.shape[:-1] + (-1, 2, h))
        return s[..., ::-1, :].reshape(m.shape)

    def col(m):
        return np.ascontiguousarray(m.T)

    def chunks(m):
        return rows(m, 3 * P).reshape(3, P).T

    qs, ks = f["q_scale"], f["k_scale"]
    qks = np.stack([np.concatenate([s, s]) for l in range(LAYERS)
                    for s in (qs[l], swap(qs[l], 32), ks[l], swap(ks[l], 32))], 1)
    pieces = {
        "dkv4": np.concatenate([g["W_dkv"]] * 4, 1), "dq": g["W_dq"],
        "kr4": np.concatenate([g["W_kr"]] * 4, 1), "kr4p": np.concatenate([swap(g["W_kr"], HALF)] * 4, 1),
        "idxq": g["idx_wq"], "idxk2": np.concatenate([g["idx_wk"]] * 2, 1),
        "qr": rows(g["W_qr"]), "qrp": rows(swap(g["W_qr"], HALF)),
        "qkv": np.concatenate(list(f["wqkv"]), 1),
        "rot": np.concatenate([swap(w[:, :2 * INNER], 32) for w in f["wqkv"]], 1),
        "wo": np.concatenate([w.reshape(PAIRS, P, D).transpose(1, 0, 2).reshape(P, -1) for w in f["wo"]], 1),
        "w1": np.concatenate(list(f["w1"]), 1),
        "w2": np.concatenate([rows(w, 3 * P).reshape(3, P, D).transpose(1, 0, 2).reshape(P, -1) for w in f["w2"]], 1),
        "qks": qks, "lng": col(f["ln_g"]), "lnb": col(f["ln_b"]),
        "b1a": np.concatenate([chunks(r[:HID]) for r in f["b1"]], 1),
        "b1g": np.concatenate([chunks(r[HID:]) for r in f["b1"]], 1),
        "b2": col(f["b2"]), "idxw": np.broadcast_to(g["idx_w"], (P, IDX_HEADS)),
        "delta": np.concatenate([g["raw_delta"]] * (P // HALF))[:, None],
    }
    weights = np.ascontiguousarray(np.concatenate([pieces[n] for n in ww.at], 1))

    def by_head(m, width):
        return m.reshape(m.shape[0], HEADS, width).transpose(2, 1, 0).reshape(width, -1)
    heads = {"uqT": by_head(g["W_uq"], DH), "ukT": by_head(g["W_uk"], DH), "uvT": by_head(g["W_uv"], DH),
             "out": g["W_out"].reshape(HEADS, DH, D).transpose(1, 0, 2).reshape(DH, -1)}
    setup = np.ascontiguousarray(np.concatenate([heads[n] for n in ss.at], 1))

    nc = bacc.Bacc("TRN2", target_bir_lowering=False, num_devices=1)
    dt = mybir.dt.float32
    arrays = {"x_dram": np.ascontiguousarray(g["x"]), "consts_dram": consts, "rots_dram": rots,
              "weights_dram": weights, "setup_dram": setup}
    aps = {n: nc.dram_tensor(n, m.shape, dt, kind="ExternalInput").ap() for n, m in arrays.items()}
    out = nc.dram_tensor("out", (B, L, D), dt, kind="ExternalOutput").ap()
    idx_scratch = nc.dram_tensor("idx_scratch", (FAR, L), mybir.dt.float16).ap()
    q_scratch = nc.dram_tensor("q_scratch", (2, 3, HEADS * 32, L), mybir.dt.bfloat16).ap()
    build(nc, *aps.values(), idx_scratch, q_scratch, out)
    r = run_bass_kernel_spmd(nc, [arrays], core_ids=[0])
    return r.results[0]["out"]
```

```python
from contextlib import ExitStack

import numpy as np

import concourse.bass as bass
from concourse import mybir

B, L, D = 4, 512, 128
P = 128
TILES = L // P
WIN = 64
NW_T = P // WIN
CKV, CQ, ROPE, HALF = 32, 64, 32, 16
HEADS, DH = 8, 64
IDX_HEADS = 4
TOPK = 96
FAR = TOPK - WIN
LAYERS = 2
INNER = HEADS * DH
HID = 341
HCH = [(0, 128), (128, 128), (256, HID - 256)]
PAIRS = HEADS // 2
SLOTS = 2 * WIN
SCALE = float((DH + ROPE) ** -0.5)
NEG = -1.0e30
RB = 8
GR = P // 32


class Columns:

    def __init__(self):
        self.at, self.n = {}, 0

    def add(self, name, width):
        self.at[name] = (self.n, self.n + width)
        self.n += width


def layout():
    c = Columns()
    for name, width in (("ident", P), ("pair_ones", 2), ("mean_ones", P), ("centre", P), ("istack", 32),
                        ("cos_q", L), ("sin_q", L), ("cos_k", L), ("sin_k", L),
                        ("tab_a_c", L), ("tab_a_s", L), ("tab_b_c", L), ("tab_b_s", L),
                        ("mask_f0", P), ("mask_f", P), ("mask_a0", P), ("mask_a", P), ("far_mask", P),
                        ("keep0", FAR), ("fill0", FAR), ("iota", TILES), ("sgn", 1), ("eps", 1),
                        ("negpi", 1)):
        c.add(name, width)
    r = Columns()
    for name, width in (("rot_c", FAR * 32), ("rot_s", FAR * 32)):
        r.add(name, width)
    w = Columns()
    for name, width in (("dkv4", 128), ("dq", CQ), ("kr4", 128), ("kr4p", 128), ("idxq", IDX_HEADS * DH),
                        ("idxk2", 128), ("qr", 256), ("qrp", 256), ("qkv", LAYERS * 3 * INNER),
                        ("rot", LAYERS * 2 * INNER), ("wo", LAYERS * 4 * D), ("w1", LAYERS * 2 * HID),
                        ("w2", LAYERS * 3 * D), ("qks", LAYERS * 4), ("lng", LAYERS), ("lnb", LAYERS),
                        ("b1a", LAYERS * 3), ("b1g", LAYERS * 3), ("b2", LAYERS), ("idxw", IDX_HEADS),
                        ("delta", 1)):
        w.add(name, width)
    s = Columns()
    for name, width in (("uqT", HEADS * CQ), ("ukT", HEADS * CKV), ("uvT", HEADS * CKV), ("out", HEADS * D)):
        s.add(name, width)
    return c, r, w, s


def constants():
    c, r, _, _ = layout()
    a = np.zeros((P, c.n), np.float32)

    def put(name, v):
        a[:, c.at[name][0]:c.at[name][1]] = v
    p = np.arange(P)
    put("ident", np.eye(P))
    put("pair_ones", (p[:, None] // DH == np.arange(2)[None, :]))
    put("mean_ones", 1.0 / D)
    put("centre", np.eye(P) - 1.0 / D)
    put("istack", (p[:, None] % 32 == np.arange(32)[None, :]) & (p[:, None] < 96))
    t = np.arange(L, dtype=np.float32)
    half = np.arange(0, DH, 2, dtype=np.float32)
    inv = (1.0 / np.float32(10000.0) ** (half / np.float32(DH))).astype(np.float32)
    fr = (t[:, None] * inv[None, :]).astype(np.float32).astype(np.float64)
    fr = np.concatenate([fr, fr], 1)
    base = (half.astype(np.float64) + 0.4 * DH) / (1.4 * DH)
    power = (t.astype(np.float64) - L // 2) / float(WIN // 2)
    sc = base[None, :] ** power[:, None]
    sc = np.concatenate([sc, sc], 1)
    sg = np.where(np.arange(DH) < DH // 2, -1.0, 1.0)
    for name, f in (("cos_q", np.cos(fr) * sc * 8.0), ("sin_q", np.sin(fr) * sc * 8.0 * sg),
                    ("cos_k", np.cos(fr) / sc), ("sin_k", np.sin(fr) / sc * sg)):
        put(name, np.tile(f.T, (2, 1)))
    theta = 1.0 / 10000.0 ** (2.0 * np.arange(HALF) / ROPE)
    theta = theta.astype(np.float32).astype(np.float64)
    sgn = np.where(p % ROPE < HALF, -1.0, 1.0)
    th = theta[p % HALF]
    pos = np.arange(L)
    for name, q in (("tab_a", pos), ("tab_b", np.where(pos < WIN, pos, 2 * pos - (WIN - 1)))):
        put(name + "_c", np.cos(th[:, None] * q[None, :]))
        put(name + "_s", np.sin(th[:, None] * q[None, :]) * sgn[:, None])
    m, s = (p % WIN)[:, None], np.arange(SLOTS)[None, :]
    first = (p < WIN)[:, None]
    f = (s >= m) & (s <= m + WIN)
    al = (s >= m + 1) & (s <= m + WIN)
    put("mask_f", np.where(f, 0.0, NEG))
    put("mask_f0", np.where(f & ~(first & (s < WIN)), 0.0, NEG))
    put("mask_a", np.where(al, 0.0, NEG))
    put("mask_a0", np.where(np.where(first, s >= WIN, al), 0.0, NEG))
    put("far_mask", np.where(p[None, :] <= p[:, None], 0.0, NEG))
    j = np.arange(FAR)[None, :]
    keep = j < (p[:, None] - (WIN - 1))
    put("keep0", keep)
    put("fill0", np.where(keep, 0, WIN + j))
    put("iota", p[:, None] + P * np.arange(TILES)[None, :])
    put("sgn", sgn[:, None])
    put("eps", 1e-5)
    put("negpi", -np.pi)
    rot = np.zeros((32, r.n), np.float32)
    ang = (WIN + np.arange(FAR))[:, None] * theta[None, :]
    rc = np.zeros((32, FAR, 32))
    rs = np.zeros((32, FAR, 32))
    for i in range(HALF):
        lo, hi = i, i + HALF
        rc[lo, :, lo] = rc[hi, :, hi] = np.cos(ang[:, i])
        rs[lo, :, lo] = rs[hi, :, hi] = -np.sin(ang[:, i])
        rc[hi, :, lo], rc[lo, :, hi] = -np.sin(ang[:, i]), np.sin(ang[:, i])
        rs[hi, :, lo], rs[lo, :, hi] = -np.cos(ang[:, i]), np.cos(ang[:, i])
    rot[:, r.at["rot_c"][0]:r.at["rot_c"][1]] = rc.reshape(32, -1)
    rot[:, r.at["rot_s"][0]:r.at["rot_s"][1]] = rs.reshape(32, -1)
    return a, rot


class Region:

    def __init__(self, full):
        self.full, self.jobs, self.read = full, {}, None

    def start(self, pe, job, read, count):
        assert job not in self.jobs, job
        self.jobs[job] = len(self.jobs) + 1
        if self.read:
            pe.wait_ge(*self.read)
        self.read = (read, count)

    def more(self, job):
        self.jobs[job] = len(self.jobs) + 1

    def nth(self, job):
        return self.jobs[job]


class Signals:

    def __init__(self, sem):
        self.x_loaded = sem("x_loaded")
        self.dve_step = sem("dve_step")
        self.var_ready = sem("var_ready")
        self.std_ready = sem("std_ready")
        self.xn_ready = sem("xn_ready")
        self.xnT_ready = sem("xnT_ready")
        self.qi_ready = sem("qi_ready")
        self.ki_ready = sem("ki_ready")
        self.relu_ready = sem("relu_ready")
        self.far_idx_ready = sem("far_idx_ready")
        self.far_idx_stored = sem("far_idx_stored")
        self.hT_ready = sem("hT_ready")
        self.sq_ready = sem("sq_ready")
        self.root_ready = sem("root_ready")
        self.rn_ready = sem("rn_ready")
        self.zeroed = sem("zeroed")
        self.parts_ready = sem("parts_ready")
        self.ab_ready = sem("ab_ready")
        self.k_ready = sem("k_ready")
        self.v_ready = sem("v_ready")
        self.masked_ready = sem("masked_ready")
        self.max_ready = sem("max_ready")
        self.nbias_ready = sem("nbias_ready")
        self.prob_ready = sem("prob_ready")
        self.recip_ready = sem("recip_ready")
        self.prob_normed = sem("prob_normed")
        self.pT_ready = sem("pT_ready")
        self.o_ready = sem("o_ready")
        self.x1_ready = sem("x1_ready")
        self.sqh_ready = sem("sqh_ready")
        self.lnh_ready = sem("lnh_ready")
        self.rstdh_ready = sem("rstdh_ready")
        self.hn_ready = sem("hn_ready")
        self.hng_ready = sem("hng_ready")
        self.gelu_ready = sem("gelu_ready")
        self.hid_ready = sem("hid_ready")
        self.x2_ready = sem("x2_ready")
        self.l_step = sem("l_step")
        self.cq_ready = sem("cq_ready")
        self.keys_zeroed = sem("keys_zeroed")
        self.ckvs_ready = sem("ckvs_ready")
        self.qc_ready = sem("qc_ready")
        self.abs_ready = sem("abs_ready")
        self.expn_ready = sem("expn_ready")
        self.log_ready = sem("log_ready")
        self.soft_ready = sem("soft_ready")
        self.krT_ready = sem("krT_ready")
        self.qb_ready = sem("qb_ready")
        self.qa_ready = sem("qa_ready")
        self.hi_ready = sem("hi_ready")
        self.rest_ready = sem("rest_ready")
        self.mid_ready = sem("mid_ready")
        self.lo_ready = sem("lo_ready")
        self.q3_stored = sem("q3_stored")
        self.pool_prod = sem("pool_prod")
        self.d_step = sem("d_step")
        self.idx_loaded0 = sem("idx_loaded0")
        self.idx_loaded1 = sem("idx_loaded1")
        self.q3_loaded = sem("q3_loaded")
        self.onehot_ready = sem("onehot_ready")
        self.kc_ready = sem("kc_ready")
        self.kr_far_ready = sem("kr_far_ready")
        self.lmasked = sem("lmasked")
        self.far_ready = sem("far_ready")
        self.vfar_ready = sem("vfar_ready")
        self.joined = sem("joined")
        self.jmax_ready = sem("jmax_ready")
        self.bias_ready = sem("bias_ready")
        self.jprob_ready = sem("jprob_ready")
        self.jrecip_ready = sem("jrecip_ready")
        self.jnormed = sem("jnormed")
        self.jpT_ready = sem("jpT_ready")
        self.blocks_zeroed = sem("blocks_zeroed")
        self.blocks_ready = sem("blocks_ready")
        self.oT_ready = sem("oT_ready")
        self.fT_ready = sem("fT_ready")
        self.out_ready = sem("out_ready")
        self.out_stored0 = sem("out_stored0")
        self.out_stored1 = sem("out_stored1")
        self.x_full = sem("x_full")
        self.y_full = sem("y_full")
        self.z_full = sem("z_full")
        self.w_full = sem("w_full")
        self.u_full = sem("u_full")
        self.regions = [self.x_full, self.y_full, self.z_full, self.w_full, self.u_full]


class Core:
    pass


def project(nc, b, k, scope):
    F, U32 = mybir.dt.float32, mybir.dt.uint32
    ALU, ACT, AX = mybir.AluOpType, mybir.ActivationFunctionType, mybir.AxisListType
    a, C, W = k.sems, k.C, k.W

    def sb(name, shape, dt=F):
        return k.sb(name, shape, dt, scope)
    def far_width(i):
        return WIN + P * i
    far_at = [sum(far_width(j) for j in range(i)) for i in range(TILES + 1)]
    stats, mv, std, rstd = sb("stats", [P, TILES, 6]), sb("mv", [P, TILES, 2]), sb("std", [P, TILES]), sb("rstd", [P, TILES])
    qiT, kiZ = sb("qiT", [P, 2, L]), sb("kiZ", [P, 2, L])
    relu = sb("relu", [P, 2, 2, far_at[TILES]])
    score, best = sb("score", [P, 2, L]), sb("best", [P, FAR])
    idx_u, idx_f, idx_t = sb("idx_u", [P, FAR], U32), sb("idx_f", [P, FAR]), sb("idx_t", [P, FAR])
    hT = sb("hT", [P, WIN + L])
    sq, lnr, rn = sb("sq", [P, 2, L]), sb("lnr", [P, L]), sb("rn", [P, L])
    root, rnorm = sb("root", [P, 2, PAIRS, TILES, 2]), sb("rnorm", [P, 2, PAIRS, TILES, 2])
    pa, pb = sb("pa", [P, 2, L]), sb("pb", [P, 2, L])
    ab, qT, kZ = sb("ab", [P, PAIRS, L]), sb("qT", [P, PAIRS, L]), sb("kZ", [P, PAIRS, 2, WIN + L])
    v = sb("v", [P, NW_T, TILES, INNER])
    S = sb("S", [P, TILES, HEADS, SLOTS])
    nmax, nbias = sb("nmax", [P, TILES, HEADS]), sb("nbias", [P, TILES, HEADS])
    rsum, rrec = sb("rsum", [P, TILES, HEADS]), sb("rrec", [P, TILES, HEADS])
    pT, oT = sb("pT", [P, 2, HEADS, P]), sb("oT", [P, PAIRS, L])
    x1, x2 = sb("x1", [P, 1 + L]), sb("x2", [P, 1 + L])
    xn = pT[:, 0, 0:TILES, :]
    spare = S[:, :, :, :].rearrange("p i h s -> p (i h s)").rearrange("p (n t) -> p n t", t=L)
    hn, hng, gl, hid = spare[:, 1, :], spare[:, 2, :], spare[:, 3:5, :], spare[:, 5:8, :]
    rX, rY, rZ = Region(a.x_full), Region(a.y_full), Region(a.z_full)
    rW, rU = Region(a.w_full), Region(a.u_full)

    rk_wide = S[:, 0:2, :, :].rearrange("p a h s -> p (a h s)").rearrange("p (c i f) -> p c i f", c=PAIRS, i=TILES)

    def pair(n):
        return (k.X, rX) if n % 2 == 0 else (k.Y, rY)

    def sums(n):
        return (k.Ub, rU) if n < PAIRS else (k.Z[:, 0, :], rZ)

    def half(par):
        return slice(DH * par, DH * par + DH)

    def tile(i):
        return slice(i * P, (i + 1) * P)
    K, Q = 0, 1

    with nc.Block() as block:
        @block.tensor
        def _(pe):
            mm = nc.tensor.matmul
            rZ.start(pe, "xnT", a.xnT_ready, 1)
            pe.wait_ge(a.xn_ready, TILES)
            for i in range(TILES):
                last = nc.tensor.transpose(k.Z[:, 0, tile(i)], xn[:, i, :], C("ident"))
            last.then_inc(rZ.full, 1)
            pe.wait_ge(a.xnT_ready, 1)
            rY.start(pe, "ki", a.ki_ready, 1)
            mm(k.Y[:, 0, :], W("idxk2"), k.xnT[:, WIN:], start=True, stop=True).then_inc(rY.full, 1)
            rX.start(pe, "qi", a.qi_ready, 1)
            for c in range(2):
                last = mm(k.X[:, c, :], W("idxq", c * P, P), k.xnT[:, WIN:], start=True, stop=True)
            last.then_inc(rX.full, 1)
            pe.wait_ge(a.zeroed, 1)
            pe.wait_ge(a.ki_ready, 1)
            pe.wait_ge(a.qi_ready, 1)
            for i in range(TILES):
                for hp in range(2):
                    reg, r = pair(hp)
                    r.start(pe, f"idx{i}.{hp}", a.relu_ready, 2 * i + hp + 1)
                    for j in range(2):
                        last = mm(reg[:, j, 0:far_width(i)], qiT[:, hp, tile(i)], kiZ[:, j, 0:far_width(i)],
                                  start=True, stop=True)
                    last.then_inc(r.full, 1)

            def qk(l, n):
                c, which = n % PAIRS, 1 - n // PAIRS
                reg, r = pair(n)
                r.start(pe, f"qk{l}.{n}", a.parts_ready, 8 * l + n + 1)
                mm(reg[:, 0, :], W("qkv", l * 3 * INNER + which * INNER + c * P, P), hT[:, WIN:], start=True, stop=True)
                mm(reg[:, 1, :], W("rot", l * 2 * INNER + which * INNER + c * P, P), hT[:, WIN:],
                   start=True, stop=True).then_inc(r.full, 1)

            def square_sums(l, n):
                reg, r = sums(n)
                if n % PAIRS == 0:
                    r.start(pe, f"ss{l}.{n}", a.root_ready, 2 * l + 1 + n // PAIRS)
                else:
                    r.more(f"ss{l}.{n}")
                pe.wait_ge(a.sq_ready, 8 * l + n + 1)
                for i in range(TILES):
                    at = (n % PAIRS * TILES + i) * 2
                    last = mm(reg[:, at:at + 2], sq[:, n % 2, tile(i)], C("pair_ones"), start=True, stop=True)
                last.then_inc(r.full, 1)

            def spread_k(l, c):
                rW.start(pe, f"rk{l}.{c}", a.k_ready, PAIRS * l + c + 1)
                pe.wait_ge(a.rn_ready, 2 * l + 1)
                for i in range(TILES):
                    last = mm(k.Wb[:, tile(i)], rk_wide[:, c, i, :], C("ident"),
                              start=True, stop=True)
                last.then_inc(rW.full, 1)

            def values(l, i):
                rZ.start(pe, f"v{l}.{i}", a.v_ready, TILES * l + i + 1)
                for par in range(2):
                    at = WIN + i * P - WIN * (1 - par)
                    last = mm(k.Z[:, par, :], hT[:, at:at + P], W("qkv", l * 3 * INNER + 2 * INNER, INNER),
                              start=True, stop=True)
                last.then_inc(rZ.full, 1)

            def scores(l, i):
                reg, r = pair(i)
                r.start(pe, f"s{l}.{i}", a.masked_ready, TILES * l + i + 1)
                for h in range(HEADS):
                    for w in range(NW_T):
                        t0 = i * P + w * WIN
                        last = mm(reg[64 * w:64 * w + 64, h // 4, (h % 4) * P:(h % 4 + 1) * P],
                                  qT[:, h // 2, t0:t0 + WIN], kZ[:, h // 2, h % 2, t0:t0 + SLOTS], start=True, stop=True)
                last.then_inc(r.full, 1)

            def prob_T(l, i):
                rZ.start(pe, f"t{l}.{i}", a.pT_ready, TILES * l + i + 1)
                pe.wait_ge(a.prob_normed, TILES * l + i + 1)
                for h in range(HEADS):
                    last = nc.tensor.transpose(k.Z[:, h // 4, (h % 4) * P:(h % 4 + 1) * P], S[:, i, h, :], C("ident"))
                last.then_inc(rZ.full, 1)

            def weigh_values(l, i):
                rW.start(pe, f"o{l}.{i}", a.o_ready, TILES * l + i + 1)
                pe.wait_ge(a.pT_ready, TILES * l + i + 1)
                for h in range(HEADS):
                    for w in range(NW_T):
                        last = mm(k.Wb[64 * (h % 2):64 * (h % 2) + 64, (h // 2) * P + w * WIN:(h // 2) * P + (w + 1) * WIN],
                                  v[:, w, i, h * DH:(h + 1) * DH], pT[:, i % 2, h, w * WIN:(w + 1) * WIN],
                                  start=True, stop=True)
                last.then_inc(rW.full, 1)

            for l in range(LAYERS):
                pe.wait_ge(a.hT_ready, 2 * l + 1)
                for n in range(8):
                    qk(l, n)
                    if n:
                        square_sums(l, n - 1)
                    if n > PAIRS:
                        spread_k(l, n - PAIRS - 1)
                square_sums(l, 7)
                spread_k(l, PAIRS - 1)
                pe.wait_ge(a.ab_ready, 8 * l + 8)
                pe.wait_ge(a.k_ready, PAIRS * (l + 1))
                scores(l, 0)
                scores(l, 1)
                values(l, 0)
                scores(l, 2)
                values(l, 1)
                scores(l, 3)
                values(l, 2)
                values(l, 3)
                prob_T(l, 0)
                for i in range(TILES):
                    if i + 1 < TILES:
                        prob_T(l, i + 1)
                    weigh_values(l, i)
                rU.start(pe, f"wo{l}", a.x1_ready, l + 1)
                pe.wait_ge(a.o_ready, TILES * (l + 1))
                for c in range(PAIRS):
                    last = mm(k.Ub, W("wo", (l * PAIRS + c) * D, D), oT[:, c, :], start=(c == 0), stop=(c == PAIRS - 1))
                last.then_inc(rU.full, 1)
                rX.start(pe, f"centred{l}", a.hn_ready, l + 1)
                pe.wait_ge(a.hT_ready, 2 * l + 2)
                mm(k.X[:, 0, :], C("centre"), hT[:, WIN:], start=True, stop=True).then_inc(rX.full, 1)
                rY.start(pe, f"var{l}", a.lnh_ready, l + 1)
                pe.wait_ge(a.sqh_ready, l + 1)
                mm(k.Y[:, 0, :], C("mean_ones"), sq[:, 0, :], start=True, stop=True).then_inc(rY.full, 1)
                pe.wait_ge(a.hng_ready, l + 1)
                for j, (off, n) in enumerate(HCH):
                    reg, r = pair(j)
                    r.start(pe, f"up{l}.{j}", a.hid_ready, 3 * l + j + 1)
                    mm(reg[0:n, 0, :], W("w1", l * 2 * HID + HID + off, n), hng[:, :], start=True, stop=True)
                    mm(reg[0:n, 1, :], W("w1", l * 2 * HID + off, n), hng[:, :], start=True, stop=True).then_inc(r.full, 1)
                rU.start(pe, f"down{l}", a.x2_ready, l + 1)
                for j, (off, n) in enumerate(HCH):
                    pe.wait_ge(a.hid_ready, 3 * l + j + 1)
                    last = mm(k.Ub, W("w2", (l * 3 + j) * D, D, rows=n), hid[0:n, j, :], start=(j == 0), stop=(j == 2))
                last.then_inc(rU.full, 1)

        @block.sync
        def _(sp):
            sp.dma_start(k.x_in[:, :, :], k.x_d[bass.ds(b, 1), :, :].rearrange("a (i p) d -> p (a i) d", p=P)).then_inc(a.x_loaded, 16)
            sp.wait_ge(a.far_idx_ready, 1)
            for g in range(GR):
                sp.dma_start(k.scratch.rearrange("r (i g t) -> g r i t", g=GR, t=32)[g],
                             k.idx_h[32 * g:32 * g + 32, :, :]).then_inc(a.far_idx_stored, 16)
            sp.wait_ge(a.far_idx_stored, 16 * GR)

        @block.gpsimd
        def _(pool):
            for par in range(2):
                nc.gpsimd.memset(kiZ[half(1 - par), par, :], 0.0)
            for par in range(2):
                nc.gpsimd.memset(kZ[half(1 - par), :, par, :], 0.0)
                last = nc.gpsimd.memset(kZ[half(par), :, par, 0:WIN], 0.0)
            last.then_inc(a.zeroed, 1)
            for l in range(LAYERS):
                for n in range(8):
                    pool.wait_ge(a.parts_ready, 8 * l + n + 1)
                    dst = ab[:, n, :] if n < PAIRS else qT[:, n - PAIRS, :]
                    nc.gpsimd.tensor_tensor(dst, pa[:, n % 2, :], pb[:, n % 2, :], ALU.add).then_inc(a.ab_ready, 1)
                for i in range(TILES):
                    pool.wait_ge(a.recip_ready, TILES * l + i + 1)
                    nc.gpsimd.tensor_tensor(S[:, i, :, :], S[:, i, :, :],
                                            rrec[:, i, :].unsqueeze(2).broadcast_to([P, HEADS, SLOTS]),
                                            ALU.mult).then_inc(a.prob_normed, 1)

        @block.scalar
        def _(act):
            op = nc.scalar.activation
            act.wait_ge(a.var_ready, 1)
            op(std[:, :], mv[:, :, 1], ACT.Sqrt, bias=C("eps")).then_inc(a.std_ready, 1)
            act.wait_ge(rZ.full, rZ.nth("xnT"))
            op(k.xnT[:, WIN:], k.Z[:, 0, :], ACT.Copy).then_inc(a.xnT_ready, 1)
            act.wait_ge(rY.full, rY.nth("ki"))
            act.wait_ge(a.zeroed, 1)
            for par in range(2):
                last = op(kiZ[half(par), par, :], k.Y[half(par), 0, :], ACT.Copy)
            last.then_inc(a.ki_ready, 1)
            act.wait_ge(rX.full, rX.nth("qi"))
            op(qiT[:, :, :], k.X, ACT.Copy).then_inc(a.qi_ready, 1)
            for i in range(TILES):
                for hp in range(2):
                    reg, r = pair(hp)
                    act.wait_ge(r.full, r.nth(f"idx{i}.{hp}"))
                    op(relu[:, hp, :, far_at[i]:far_at[i + 1]], reg[:, :, 0:far_width(i)], ACT.Relu).then_inc(a.relu_ready, 1)

            def squares(l, n):
                reg, r = pair(n)
                act.wait_ge(r.full, r.nth(f"qk{l}.{n}"))
                if n >= 2:
                    r = sums(n - 2)[1]
                    act.wait_ge(r.full, r.nth(f"ss{l}.{n - 2}"))
                elif l:
                    act.wait_ge(rZ.full, rZ.nth(f"ss{l - 1}.{6 + n}"))
                    act.wait_ge(rY.full, rY.nth(f"var{l - 1}"))
                op(sq[:, n % 2, :], reg[:, 0, :], ACT.Square).then_inc(a.sq_ready, 1)

            def norms(l, which):
                reg, r = sums(PAIRS * which)
                act.wait_ge(r.full, r.nth(f"ss{l}.{PAIRS * which + PAIRS - 1}"))
                if l:
                    act.wait_ge(a.rn_ready, 2 * (l - 1) + which + 1)
                op(root[:, which, :, :, :].rearrange("p c i e -> p (c i e)"), reg[:, 0:PAIRS * TILES * 2],
                   ACT.Sqrt).then_inc(a.root_ready, 1)

            def exps(l, i):
                act.wait_ge(a.nbias_ready, TILES * l + i + 1)
                for h in range(HEADS):
                    last = op(S[:, i, h, :], S[:, i, h, :], ACT.Exp, bias=nbias[:, i, h:h + 1],
                              scale=rnorm[:, Q, h // 2, i, h % 2:h % 2 + 1])
                last.then_inc(a.prob_ready, 1)

            def copy_v(l, i):
                act.wait_ge(rZ.full, rZ.nth(f"v{l}.{i}"))
                op(v[:, :, i, :], k.Z, ACT.Copy).then_inc(a.v_ready, 1)

            def copy_pT(l, i):
                act.wait_ge(rZ.full, rZ.nth(f"t{l}.{i}"))
                if i >= 2:
                    act.wait_ge(a.o_ready, TILES * l + i - 1)
                op(pT[:, i % 2, :, :], k.Z.rearrange("p a (h t) -> p (a h) t", h=4), ACT.Copy).then_inc(a.pT_ready, 1)

            for l in range(LAYERS):
                for n in range(8):
                    squares(l, n)
                    if n == PAIRS:
                        norms(l, K)
                norms(l, Q)
                exps(l, 0)
                copy_v(l, 0)
                exps(l, 1)
                copy_v(l, 1)
                exps(l, 2)
                copy_v(l, 2)
                copy_v(l, 3)
                exps(l, 3)
                for i in range(TILES):
                    copy_pT(l, i)
                act.wait_ge(rX.full, rX.nth(f"centred{l}"))
                op(sq[:, 0, :], k.X[:, 0, :], ACT.Square).then_inc(a.sqh_ready, 1)
                act.wait_ge(rY.full, rY.nth(f"var{l}"))
                op(lnr[:, :], k.Y[:, 0, :], ACT.Ln, bias=C("eps")).then_inc(a.lnh_ready, 1)
                act.wait_ge(a.lnh_ready, l + 1)
                op(rn[:, :], lnr[:, :], ACT.Exp, scale=-0.5).then_inc(a.rstdh_ready, 1)
                act.wait_ge(a.hn_ready, l + 1)
                op(hng[:, :], hn[:, :], ACT.Identity, bias=W("lnb", l, 1), scale=W("lng", l, 1)).then_inc(a.hng_ready, 1)
                for j, (off, n) in enumerate(HCH):
                    reg, r = pair(j)
                    act.wait_ge(r.full, r.nth(f"up{l}.{j}"))
                    if j >= 2:
                        act.wait_ge(a.hid_ready, 3 * l + j - 1)
                    op(gl[0:n, j % 2, :], reg[0:n, 0, :], ACT.Gelu, bias=W("b1g", 3 * l + j, 1, rows=n)).then_inc(a.gelu_ready, 1)
            act.wait_ge(a.x2_ready, LAYERS)
            op(k.gate[:, :], x2[:, 1:], ACT.Silu)

        @block.vector
        def _(dve):
            ve = nc.vector
            step = [0]

            def link(ins):
                step[0] += 1
                ins.then_inc(a.dve_step, 1)
                dve.wait_ge(a.dve_step, step[0])
            link(ve.memset(hT[:, 0:WIN], 0.0))
            link(ve.memset(x1[:, 0:1], 0.0))
            link(ve.memset(x2[:, 0:1], 0.0))
            dve.wait_ge(a.x_loaded, 16)
            for i in range(TILES):
                link(ve.bn_stats(stats[:, i, :], k.x_in[:, i, :]))
                ins = ve.bn_aggr(mv[:, i, :], stats[:, i, :])
            ins.then_inc(a.var_ready, 1)
            dve.wait_ge(a.std_ready, 1)
            link(ve.reciprocal(rstd[:, :], std[:, :]))
            for i in range(TILES):
                ve.tensor_scalar(xn[:, i, :], k.x_in[:, i, :], mv[:, i, 0:1], rstd[:, i:i + 1], ALU.subtract,
                                 ALU.mult).then_inc(a.xn_ready, 1)

            def sum_heads(i):
                n, at = far_width(i), slice(far_at[i], far_at[i + 1])
                out = score[:, i % 2, 0:n]
                dve.wait_ge(a.relu_ready, 2 * i + 2)
                link(ve.tensor_scalar(out, relu[:, 0, 0, at], W("idxw", 0, 1), None, ALU.mult))
                for h in range(1, IDX_HEADS):
                    link(ve.scalar_tensor_tensor(out, relu[:, h // 2, h % 2, at], W("idxw", h, 1), out, ALU.mult, ALU.add))
                c0 = max(n - P, 0)
                link(ve.tensor_tensor(score[:, i % 2, c0:n], score[:, i % 2, c0:n], C("far_mask")[:, P - (n - c0):], ALU.add))

            def next_best(i, q):
                n, e = far_width(i), slice(8 * q, 8 * q + 8)
                out = score[:, i % 2, 0:n]
                link(ve.max(best[:, e], out))
                link(ve.max_index(idx_u[:, e], best[:, e], out))
                if q < FAR // 8 - 1:
                    link(ve.match_replace(out, best[:, e], out, -3.0e38))

            def keep_indices(i):
                link(ve.tensor_copy(idx_f[:, :], idx_u[:, :]))
                if i == 0:
                    link(ve.tensor_tensor(idx_f[:, :], idx_f[:, :], C("keep0"), ALU.mult))
                    link(ve.tensor_tensor(idx_f[:, :], idx_f[:, :], C("fill0"), ALU.add))
                link(ve.transpose(idx_t[:, :], idx_f[:, :]))
                ins = ve.tensor_copy(k.idx_h[:, i, :], idx_t[:, :])
                if i < TILES - 1:
                    link(ins)
                else:
                    ins.then_inc(a.far_idx_ready, 1)

            def shift_tokens(src, off):
                link(ve.tensor_copy(hT[0:64, WIN:], src[0:64, off:off + L]))
                ve.tensor_copy(hT[64:128, WIN:], src[64:128, off - 1:off - 1 + L]).then_inc(a.hT_ready, 1)

            def parts(l, n):
                reg, r = pair(n)
                which = n // PAIRS
                cos, sin = (("cos_k", "sin_k"), ("cos_q", "sin_q"))[which]
                dve.wait_ge(r.full, r.nth(f"qk{l}.{n}"))
                if 8 * l + n >= 2:
                    dve.wait_ge(a.ab_ready, 8 * l + n - 1)
                link(ve.scalar_tensor_tensor(pb[:, n % 2, :], reg[:, 1, :], W("qks", 4 * l + 2 * (1 - which) + 1, 1), C(sin),
                                             ALU.mult, ALU.mult))
                dve.wait_ge(a.sq_ready, 8 * l + n + 1)
                ve.scalar_tensor_tensor(pa[:, n % 2, :], reg[:, 0, :], W("qks", 4 * l + 2 * (1 - which), 1), C(cos),
                                        ALU.mult, ALU.mult).then_inc(a.parts_ready, 1)

            def inverse_norms(l, which):
                dve.wait_ge(a.root_ready, 2 * l + which + 1)
                r = rnorm[:, which, :, :, :]
                link(ve.tensor_scalar(r, root[:, which, :, :, :], 1.0e-12, None, ALU.max))
                if which == Q:
                    ve.reciprocal(r, r).then_inc(a.rn_ready, 1)
                else:
                    link(ve.reciprocal(r, r))
                    ve.tensor_copy(rk_wide.rearrange("p c i (e f) -> p (c i e) f", e=2),
                                   r.rearrange("p c i e -> p (c i e)").unsqueeze(2).broadcast_to([P, PAIRS * TILES * 2, DH])
                                   ).then_inc(a.rn_ready, 1)

            def norm_k(l, c):
                dve.wait_ge(a.ab_ready, 8 * l + c + 1)
                dve.wait_ge(rW.full, rW.nth(f"rk{l}.{c}"))
                link(ve.tensor_tensor(kZ[half(0), c, 0, WIN:], ab[half(0), c, :], k.Wb[half(0), :], ALU.mult))
                ve.tensor_tensor(kZ[half(1), c, 1, WIN:], ab[half(1), c, :], k.Wb[half(1), :], ALU.mult).then_inc(a.k_ready, 1)

            def mask_max(l, i):
                reg, r = pair(i)
                dve.wait_ge(r.full, r.nth(f"s{l}.{i}"))
                ve.tensor_tensor(S[:, i, :, :], reg.rearrange("p a (h s) -> p (a h) s", h=4),
                                 C("mask_f0" if i == 0 else "mask_f").unsqueeze(1).broadcast_to([P, HEADS, SLOTS]),
                                 ALU.add).then_inc(a.masked_ready, 1)
                dve.wait_ge(a.masked_ready, TILES * l + i + 1)
                ve.tensor_reduce(nmax[:, i, :], S[:, i, :, :], AX.X, ALU.max, negate=True).then_inc(a.max_ready, 1)
                dve.wait_ge(a.max_ready, TILES * l + i + 1)
                ve.tensor_tensor(nbias[:, i, :].rearrange("p (c e) -> p c e", e=2),
                                 nmax[:, i, :].rearrange("p (c e) -> p c e", e=2), rnorm[:, Q, :, i, :],
                                 ALU.mult).then_inc(a.nbias_ready, 1)

            def recips(l, i):
                dve.wait_ge(a.prob_ready, TILES * l + i + 1)
                link(ve.tensor_reduce(rsum[:, i, :], S[:, i, :, :], AX.X, ALU.add))
                ve.reciprocal(rrec[:, i, :], rsum[:, i, :]).then_inc(a.recip_ready, 1)

            def copy_o(l, i):
                dve.wait_ge(rW.full, rW.nth(f"o{l}.{i}"))
                ve.tensor_copy(oT[:, :, tile(i)], k.Wb.rearrange("p (c t) -> p c t", c=PAIRS)).then_inc(a.o_ready, 1)

            x, off = k.xnT, WIN
            dve.wait_ge(a.xnT_ready, 1)
            for l in range(LAYERS):
                shift_tokens(x, off)
                for n in range(8):
                    parts(l, n)
                    if n == 0:
                        sum_heads(2 * l)
                    if n in (1, 2, 3):
                        next_best(2 * l, n - 1)
                    if n == 5:
                        next_best(2 * l, 3)
                    if n == 6:
                        keep_indices(2 * l)
                    if n == PAIRS:
                        inverse_norms(l, K)
                    if n > PAIRS:
                        norm_k(l, n - PAIRS - 1)
                norm_k(l, PAIRS - 1)
                inverse_norms(l, Q)
                dve.wait_ge(a.rn_ready, 2 * l + 2)
                mask_max(l, 0)
                mask_max(l, 1)
                recips(l, 0)
                mask_max(l, 2)
                recips(l, 1)
                mask_max(l, 3)
                recips(l, 2)
                recips(l, 3)
                sum_heads(2 * l + 1)
                copy_o(l, 0)
                next_best(2 * l + 1, 0)
                copy_o(l, 1)
                next_best(2 * l + 1, 1)
                copy_o(l, 2)
                next_best(2 * l + 1, 2)
                copy_o(l, 3)
                dve.wait_ge(rU.full, rU.nth(f"wo{l}"))
                ve.tensor_tensor(x1[:, 1:], k.Ub, x[:, off:off + L], ALU.add).then_inc(a.x1_ready, 1)
                dve.wait_ge(a.x1_ready, l + 1)
                shift_tokens(x1, 1)
                next_best(2 * l + 1, 3)
                keep_indices(2 * l + 1)
                dve.wait_ge(a.rstdh_ready, l + 1)
                ve.tensor_tensor(hn[:, :], k.X[:, 0, :], rn[:, :], ALU.mult).then_inc(a.hn_ready, 1)
                for j, (o, n) in enumerate(HCH):
                    reg, r = pair(j)
                    dve.wait_ge(r.full, r.nth(f"up{l}.{j}"))
                    dve.wait_ge(a.gelu_ready, 3 * l + j + 1)
                    ve.scalar_tensor_tensor(hid[0:n, j, :], reg[0:n, 1, :], W("b1a", 3 * l + j, 1, rows=n),
                                            gl[0:n, j % 2, :], ALU.add, ALU.mult).then_inc(a.hid_ready, 1)
                dve.wait_ge(rU.full, rU.nth(f"down{l}"))
                ve.scalar_tensor_tensor(x2[:, 1:], k.Ub, W("b2", l, 1), x1[:, 1:], ALU.add, ALU.add).then_inc(a.x2_ready, 1)
                dve.wait_ge(a.x2_ready, l + 1)
                x, off = x2, 1


def latents(nc, b, k, scope):
    F, BF = mybir.dt.float32, mybir.dt.bfloat16
    ALU, ACT = mybir.AluOpType, mybir.ActivationFunctionType
    a, C, W = k.sems, k.C, k.W

    def sb(name, shape, dt=F):
        return k.sb(name, shape, dt, scope)
    cqT, qcT = sb("cqT", [CQ, L]), sb("qcT", [P, 2, L])
    mag, soft = sb("mag", [P, 3, 2, L]), sb("soft", [P, 3, 2, L])
    prod = sb("prod", [P, 2, L])
    pprod = sb("pprod", [P, 2, L])
    qa, krot = sb("qa", [P, 2, L]), sb("krot", [P, L])
    q3s = sb("q3s", [P, 2, 2, 3, L], BF)
    rest = sb("rest", [P, 2, FAR * 32])
    rX, rY, rZ, rW = Region(a.x_full), Region(a.y_full), Region(a.z_full), Region(a.w_full)
    rU = Region(a.u_full)
    SOFT = ("kr", "qr0", "qr1")

    def tile(i):
        return slice(i * P, (i + 1) * P)

    def soft_region(n):
        return ((k.X, rX), (k.Y, rY), (k.Z, rZ))[n]

    def rank_region(j):
        return (k.X, rX) if j % 2 == 0 else (k.Y, rY)

    def split_job(kind, c):
        if kind == "value":
            return k.ckvS[:, :, 1, :], [k.CX[:, :, 32 * q:32 * q + 32] for q in range(3)], (a.ckvs_ready, 1)
        if kind == "rank":
            reg, r = rank_region(c)
            return (reg.rearrange("p a (r d) -> p (a r) d", d=32), [k.XR[:, c, :, 32 * q:32 * q + 32] for q in range(3)],
                    (r.full, r.nth(f"xr{c}")))
        if kind == "content":
            return qcT[:, c, :], [q3s[:, 0, c, q, :] for q in range(3)], (a.qc_ready, c + 1)
        return qa[:, c, :], [q3s[:, 1, c, q, :] for q in range(3)], (a.qa_ready, c + 1)
    order = [("value", 0), ("content", 0), ("content", 1), ("rank", 0), ("rope", 0), ("rank", 1), ("rope", 1),
             ("rank", 2), ("rank", 3)]

    def rest_of(s):
        kind = order[s][0]
        if kind == "value":
            return rest[:, s % 2, 0:TILES * 32].rearrange("p (i d) -> p i d", d=32)
        if kind == "rank":
            return rest[:, s % 2, :].rearrange("p (r d) -> p r d", d=32)
        return rest[:, s % 2, 0:L]

    with nc.Block() as block:
        @block.tensor
        def _(pe):
            mm = nc.tensor.matmul
            xnT = k.xnT[:, WIN:]
            rX.start(pe, "kr", a.soft_ready, 1)
            mm(k.X[:, 0, :], W("kr4"), xnT, start=True, stop=True)
            mm(k.X[:, 1, :], W("kr4p"), xnT, start=True, stop=True).then_inc(rX.full, 1)
            rZ.start(pe, "ckv", a.cq_ready, 1)
            mm(k.Z[0:CQ, 1, :], W("dq"), xnT, start=True, stop=True)
            mm(k.Z[:, 0, :], W("dkv4"), xnT, start=True, stop=True).then_inc(rZ.full, 1)
            rW.start(pe, "ckvs", a.ckvs_ready, 1)
            for i in range(TILES):
                for w in range(NW_T):
                    at = i * P + WIN * w
                    last = mm(k.Wb[:, (NW_T * i + w) * 32:(NW_T * i + w + 1) * 32], k.xnT[:, at:at + P],
                              W("dkv4", 0, CKV), start=True, stop=True)
            last.then_inc(rW.full, 1)
            pe.wait_ge(a.cq_ready, 1)
            for c in range(2):
                reg, r = soft_region(c + 1)
                r.start(pe, f"qr{c}", a.soft_ready, c + 2)
                mm(reg[:, 0, :], W("qr", c * P, P, rows=CQ), cqT[:, :], start=True, stop=True)
                mm(reg[:, 1, :], W("qrp", c * P, P, rows=CQ), cqT[:, :], start=True, stop=True).then_inc(r.full, 1)
            rU.start(pe, "qc0", a.qc_ready, 1)
            mm(k.Ub, k.m1[:, 0:P], cqT[:, :], start=True, stop=True).then_inc(rU.full, 1)
            rW.start(pe, "qc1", a.qc_ready, 2)
            mm(k.Wb, k.m1[:, P:2 * P], cqT[:, :], start=True, stop=True).then_inc(rW.full, 1)
            pe.wait_ge(a.soft_ready, 1)
            for j in range(TILES):
                reg, r = rank_region(j)
                r.start(pe, f"xr{j}", a.rest_ready, order.index(("rank", j)) + 1)
                for e in range(2):
                    last = mm(reg[:, e, :], soft[32:64, 0, 0, tile(j)], k.rot_tab[:, e * 512:(e + 1) * 512],
                              start=True, stop=True)
                last.then_inc(r.full, 1)

        @block.scalar
        def _(act):
            op = nc.scalar.activation

            def magnitude(n):
                reg, r = soft_region(n)
                act.wait_ge(r.full, r.nth(SOFT[n]))
                op(mag[:, n, :, :], reg, ACT.Abs).then_inc(a.abs_ready, 1)

            def exponential(n):
                act.wait_ge(a.abs_ready, n + 1)
                op(mag[:, n, :, :], mag[:, n, :, :], ACT.Exp, scale=-1.0).then_inc(a.expn_ready, 1)

            def logarithm(n):
                act.wait_ge(a.expn_ready, n + 1)
                op(mag[:, n, :, :], mag[:, n, :, :], ACT.Ln, bias=1.0).then_inc(a.log_ready, 1)

            def copy_content(c):
                bank, r = ((7, rU), (6, rW))[c]
                act.wait_ge(r.full, r.nth(f"qc{c}"))
                for e in range(2):
                    op(k.q_loc[0:64, 2 * c + e, :], k.PS[64 * e:64 * e + 64, bank, :], ACT.Copy)
                op(qcT[:, c, :], k.PS[:, bank, :], ACT.Copy).then_inc(a.qc_ready, 1)

            def hi(s):
                src, dst, ready = split_job(*order[s])
                act.wait_ge(*ready)
                op(dst[0], src, ACT.Copy).then_inc(a.hi_ready, 1)

            def mid(s):
                act.wait_ge(a.rest_ready, s + 1)
                op(split_job(*order[s])[1][1], rest_of(s), ACT.Copy).then_inc(a.mid_ready, 1)

            magnitude(0)
            act.wait_ge(rZ.full, rZ.nth("ckv"))
            op(cqT[:, :], k.Z[0:CQ, 1, :], ACT.Copy)
            act.wait_ge(a.keys_zeroed, 1)
            for e in range(2):
                rows = slice(32 * e, 32 * e + 32)
                last = op(k.key[rows, e, WIN:], k.Z[rows, 0, :], ACT.Copy)
            last.then_inc(a.cq_ready, 1)
            exponential(0)
            magnitude(1)
            exponential(1)
            magnitude(2)
            exponential(2)
            for n in range(3):
                logarithm(n)
            copy_content(0)
            copy_content(1)
            hi(0)
            for s in range(1, len(order)):
                hi(s)
                mid(s - 1)
            mid(len(order) - 1)

        @block.gpsimd
        def _(pool):
            tt = nc.gpsimd.tensor_tensor
            for c in range(2):
                pool.wait_ge(a.soft_ready, c + 2)
                tt(pprod[:, 0, :], soft[:, c + 1, 0, :], C("tab_b_c"), ALU.mult).then_inc(a.pool_prod, 1)
                tt(pprod[:, 1, :], soft[:, c + 1, 1, :], C("tab_b_s"), ALU.mult).then_inc(a.pool_prod, 1)
                pool.wait_ge(a.pool_prod, 2 * c + 2)
                for e in range(2):
                    rows = slice(64 * e, 64 * e + 64)
                    last = tt(k.q_loc[64:128, 2 * c + e, :], pprod[rows, 0, :], pprod[rows, 1, :], ALU.add)
                last.then_inc(a.qb_ready, 1)
                pool.wait_ge(a.qb_ready, c + 1)

        @block.vector
        def _(dve):
            ve = nc.vector
            step = [0]

            def link(ins):
                step[0] += 1
                ins.then_inc(a.l_step, 1)
                dve.wait_ge(a.l_step, step[0])

            def softplus(n):
                reg, r = soft_region(n)
                dve.wait_ge(a.log_ready, n + 1)
                ve.scalar_tensor_tensor(soft[:, n, :, :], reg, 0.0, mag[:, n, :, :], ALU.max,
                                        ALU.add).then_inc(a.soft_ready, 1)
                dve.wait_ge(a.soft_ready, n + 1)

            def rotate(dst, n, done):
                link(ve.tensor_tensor(prod[:, 0, :], soft[:, n, 0, :], C("tab_a_c"), ALU.mult))
                link(ve.tensor_tensor(prod[:, 1, :], soft[:, n, 1, :], C("tab_a_s"), ALU.mult))
                ve.tensor_tensor(dst, prod[:, 0, :], prod[:, 1, :], ALU.add).then_inc(done, 1)

            def take_hi(s):
                dve.wait_ge(a.hi_ready, s + 1)
                if s >= 2:
                    dve.wait_ge(a.lo_ready, s - 1)
                src, dst, _ = split_job(*order[s])
                ve.tensor_tensor(rest_of(s), src, dst[0], ALU.subtract).then_inc(a.rest_ready, 1)

            def lo(s):
                dve.wait_ge(a.mid_ready, s + 1)
                _, dst, _ = split_job(*order[s])
                ve.tensor_tensor(dst[2], rest_of(s), dst[1], ALU.subtract).then_inc(a.lo_ready, 1)

            ve.memset(k.key[:, :, :], 0.0).then_inc(a.keys_zeroed, 1)
            dve.wait_ge(a.keys_zeroed, 1)
            dve.wait_ge(rW.full, rW.nth("ckvs"))
            ve.tensor_copy(k.ckvS[:, :, :, :], k.Wb[:, 0:TILES * NW_T * 32].rearrange("p (i w d) -> p i w d", w=NW_T, d=32)).then_inc(a.ckvs_ready, 1)
            softplus(0)
            softplus(1)
            softplus(2)
            for c in range(2):
                rotate(qa[:, c, :], c + 1, a.qa_ready)
                dve.wait_ge(a.qa_ready, c + 1)
            take_hi(0)
            for s in range(1, len(order)):
                take_hi(s)
                lo(s - 1)
                if s == 4:
                    rotate(krot[:, :], 0, a.krT_ready)
                    dve.wait_ge(a.krT_ready, 1)
                    for e in range(2):
                        rows = slice(64 + 32 * e, 64 + 32 * e + 32)
                        link(ve.tensor_copy(k.key[rows, e, WIN:], krot[rows, :]))
            lo(len(order) - 1)

        @block.sync
        def _(sp):
            for n, loaded in enumerate((a.idx_loaded0, a.idx_loaded1)):
                sp.dma_start(k.idxb[:, n, :].rearrange("p (r t) -> p r t", r=RB),
                             k.scratch[n * RB:(n + 1) * RB, 0:P].partition_broadcast(P)).then_inc(loaded, 16)
            for kind, name in enumerate(("content", "rope")):
                for c in range(2):
                    sp.wait_ge(a.lo_ready, order.index((name, c)) + 1)
                    sp.dma_start(k.q_scratch[kind, :, c * P:(c + 1) * P, :].rearrange("q p t -> p q t"),
                                 q3s[:, kind, c, :, :]).then_inc(a.q3_stored, 16)
            sp.wait_ge(a.q3_stored, 64)


def attend(nc, b, k, scope):
    F, BF, FH = mybir.dt.float32, mybir.dt.bfloat16, mybir.dt.float16
    ALU, ACT, AX = mybir.AluOpType, mybir.ActivationFunctionType, mybir.AxisListType
    a, C, W = k.sems, k.C, k.W

    def sb(name, shape, dt=F):
        return k.sb(name, shape, dt, scope)
    QTR = FAR // RB
    NF = TILES * QTR
    OCT = 4
    idxb = k.idxb
    onehot = sb("onehot", [P, 2, TILES, RB * P], BF)
    KC, KR = sb("KC", [96, 2, 32, P], BF), sb("KR", [96, 2, 32, P], BF)
    q3 = sb("q3", [96, 2, 24, P], BF)
    V = sb("V", [P, 2, 32, CKV])
    J = SLOTS + FAR
    SC = sb("SC", [P, 2, HEADS, J])
    SN = sb("SN", [P, HEADS, 32])
    nmax, bias = sb("jmax", [P, 2, HEADS]), sb("jbias", [P, 2, HEADS])
    rsum, rrec = sb("jsum", [P, 2, HEADS]), sb("jrec", [P, 2, HEADS])
    PT, PN = sb("PT", [P, HEADS, P]), sb("PN", [P, HEADS, 32])
    PB = sb("PB", [P, 32, GR, HEADS])
    OT = sb("OT", [CKV, 2, 512])
    fT, o_sb = sb("fT", [P, P]), sb("o_sb", [P, 2, D])
    rX, rY, rZ, rW = Region(a.x_full), Region(a.y_full), Region(a.z_full), Region(a.w_full)
    O2 = k.PS[:, 6:8, :]

    def tile(i):
        return slice(i * P, (i + 1) * P)

    with nc.Block() as block:
        @block.tensor
        def _(pe):
            mm = nc.tensor.matmul

            def fetch(n):
                i, q = n // QTR, n % QTR
                pe.wait_ge(a.onehot_ready, n + 1)
                rZ.start(pe, f"gc{n}", a.kc_ready, n + 1)
                for e in range(2):
                    for j in range(i + 1):
                        last = mm(k.Z[0:96, e, :], k.CX[:, j, :], onehot[:, n % 2, j, e * 512:(e + 1) * 512],
                                  start=(j == 0), stop=(j == i))
                last.then_inc(rZ.full, 1)
                rY.start(pe, f"gr{n}", a.kr_far_ready, n + 1)
                for r in range(RB):
                    for j in range(i + 1):
                        last = mm(k.Y[0:96, r // 4, (r % 4) * P:(r % 4 + 1) * P], k.XR[:, j, q * RB + r, :],
                                  onehot[:, n % 2, j, r * P:(r + 1) * P], start=(j == 0), stop=(j == i))
                last.then_inc(rY.full, 1)

            def local_scores(i):
                rX.start(pe, f"ls{i}", a.lmasked, i + 1)
                for h in range(HEADS):
                    c, s0 = h // 4, (h % 4) * P
                    for w in range(NW_T):
                        t0 = i * P + w * WIN
                        out = k.X[64 * w:64 * w + 64, c, s0:s0 + P]
                        last = mm(out, k.q_loc[:, h // 2, t0:t0 + WIN], k.key[:, h % 2, t0:t0 + SLOTS], start=True, stop=True)
                last.then_inc(rX.full, 1)

            def far_scores(i, o):
                reg, r = k.X, rX
                r.start(pe, f"fs{i}.{o}", a.far_ready, OCT * i + o + 1)
                if o == 0:
                    pe.wait_ge(a.kc_ready, QTR * (i + 1))
                    pe.wait_ge(a.kr_far_ready, QTR * (i + 1))
                    pe.wait_ge(a.q3_loaded, 96 * (i + 1))
                for q in range(8):
                    t, out = 8 * o + q, reg[:, q // 4, (q % 4) * P:(q % 4 + 1) * P]
                    mm(out[:, 96:P], KC[:, i % 2, t, :], k.istack[:, :], start=True, stop=True)
                    mm(out[:, 0:96], KC[:, i % 2, t, :], q3[:, 0, :, t::32], start=True, stop=False)
                    last = mm(out[:, 0:96], KR[:, i % 2, t, :], q3[:, 1, :, t::32], start=False, stop=True)
                last.then_inc(r.full, 1)

            def probs_T(i):
                rX.start(pe, f"lt{i}", a.jpT_ready, i + 1)
                pe.wait_ge(a.jnormed, i + 1)
                for h in range(HEADS):
                    last = nc.tensor.transpose(k.X[:, h // 4, (h % 4) * P:(h % 4 + 1) * P], SC[:, i % 2, h, 0:SLOTS], C("ident"))
                last.then_inc(rX.full, 1)

            def weigh(i):
                rW.start(pe, f"pv{i}", a.oT_ready, i + 1)
                pe.wait_ge(a.jpT_ready, i + 1)
                pe.wait_ge(a.blocks_ready, i + 1)
                for e in range(2):
                    for w in range(NW_T):
                        mm(O2[0:CKV, e, :].rearrange("p (t g h) -> p t g h", g=GR, h=HEADS)[:, :, 2 * w:2 * w + 2, :],
                           k.ckvS[:, i, w, :],
                           PT[:, :, :].rearrange("p h (g t) -> p t g h", g=GR)[:, 16 * e:16 * e + 16, 2 * w:2 * w + 2, :],
                           start=(w == 0), stop=False, skip_group_check=True)
                    for t in range(16 * e, 16 * e + 16):
                        last = mm(O2[0:CKV, e, (t % 16) * 32:(t % 16 + 1) * 32], V[:, i % 2, t, :],
                                  PB[:, t, :, :].rearrange("p g h -> p (g h)"), start=False, stop=True,
                                  skip_group_check=True)
                last.then_inc(rW.full, 1)

            def project_out(i):
                rW.start(pe, f"so{i}", a.fT_ready, i + 1)
                pe.wait_ge(a.oT_ready, i + 1)
                heads = OT[:, :, :].rearrange("p a (t g h) -> p h g (a t)", g=GR, h=HEADS)
                for h in range(HEADS):
                    last = mm(k.Ub[:, 0:P], k.mo[:, h * D:(h + 1) * D], heads[:, h, :, :],
                              start=(h == 0), stop=(h == HEADS - 1))
                last.then_inc(rW.full, 1)

            def turn_back(i):
                rW.start(pe, f"fin{i}", a.out_ready, i + 1)
                pe.wait_ge(a.fT_ready, i + 1)
                nc.tensor.transpose(k.Wb[:, 0:P], fT[:, :], C("ident")).then_inc(rW.full, 1)

            for n in range(QTR):
                fetch(n)
            local_scores(0)
            for i in range(TILES):
                nxt = QTR * (i + 1)
                far_scores(i, 0)
                if i + 1 < TILES:
                    fetch(nxt)
                far_scores(i, 1)
                if i + 1 < TILES:
                    fetch(nxt + 1)
                if i:
                    probs_T(i - 1)
                far_scores(i, 2)
                if i + 1 < TILES:
                    fetch(nxt + 2)
                if i:
                    weigh(i - 1)
                far_scores(i, 3)
                if i:
                    project_out(i - 1)
                if i + 1 < TILES:
                    fetch(nxt + 3)
                if i:
                    turn_back(i - 1)
                if i + 1 < TILES:
                    local_scores(i + 1)
            probs_T(TILES - 1)
            weigh(TILES - 1)
            project_out(TILES - 1)
            turn_back(TILES - 1)

        @block.sync
        def _(sp):
            loads, stores = (a.idx_loaded0, a.idx_loaded1), (a.out_stored0, a.out_stored1)

            def load_q3(i):
                if i:
                    sp.wait_ge(a.far_ready, OCT * i)
                for kind in range(2):
                    for part in range(3):
                        sp.dma_start(q3[32 * part:32 * part + 32, kind, :, :],
                                     k.q_scratch[kind, :, :, tile(i)].rearrange("q (c d) t -> d (q c) t", d=32)
                                     ).then_inc(a.q3_loaded, 16)

            def load_idx(n):
                i, q = n // QTR, n % QTR
                if n >= 2:
                    sp.wait_ge(a.onehot_ready, n - 1)
                sp.dma_start(idxb[:, n % 2, :].rearrange("p (r t) -> p r t", r=RB),
                             k.scratch[q * RB:(q + 1) * RB, tile(i)].partition_broadcast(P)).then_inc(loads[n % 2], 16)
            def store(i):
                sp.wait_ge(a.out_ready, i + 1)
                sp.dma_start(k.out_d[bass.ds(b, 1), tile(i), :].rearrange("a p d -> (a p) d"), o_sb[:, i % 2, :]).then_inc(stores[i % 2], 16)

            load_idx(2)
            load_idx(3)
            load_q3(0)
            load_idx(4)
            load_idx(5)
            for i in range(TILES):
                for n in range(QTR * (i + 1) + 2, min(QTR * (i + 2) + 2, NF)):
                    load_idx(n)
                if i + 1 < TILES:
                    load_q3(i + 1)
                if i:
                    store(i - 1)
            store(TILES - 1)
            sp.wait_ge(a.out_stored0, 16 * TILES // 2)
            sp.wait_ge(a.out_stored1, 16 * TILES // 2)

        @block.gpsimd
        def _(pool):
            nc.gpsimd.memset(PB[:, :, :, :], 0.0).then_inc(a.blocks_zeroed, 1)
            for i in range(TILES):
                pool.wait_ge(a.jrecip_ready, i + 1)
                nc.gpsimd.tensor_tensor(SC[:, i % 2, :, :], SC[:, i % 2, :, :],
                                        rrec[:, i % 2, :].unsqueeze(2).broadcast_to([P, HEADS, J]), ALU.mult).then_inc(a.jnormed, 1)

        @block.scalar
        def _(act):
            op = nc.scalar.activation

            def keep_content(n):
                i, q = n // QTR, n % QTR
                act.wait_ge(rZ.full, rZ.nth(f"gc{n}"))
                op(KC[:, i % 2, :, :].rearrange("p t (g r) -> p r g t", g=GR)[:, q * RB:(q + 1) * RB, :, :],
                   k.Z[0:96, :, :].rearrange("p a (r g t) -> p (a r) g t", g=GR, t=32), ACT.Copy).then_inc(a.kc_ready, 1)

            def keep_values(i, o):
                reg, r = k.X, rX
                act.wait_ge(r.full, r.nth(f"fs{i}.{o}"))
                if o == 0 and i >= 2:
                    act.wait_ge(rW.full, rW.nth(f"pv{i - 2}"))
                op(V[:, i % 2, 8 * o:8 * o + 8, :], reg.rearrange("p a (q c) -> p (a q) c", c=P)[:, :, 96:P],
                   ACT.Copy).then_inc(a.vfar_ready, 1)

            def exps(i):
                act.wait_ge(a.bias_ready, i + 1)
                for h in range(HEADS):
                    last = op(SC[:, i % 2, h, :], SC[:, i % 2, h, :], ACT.Exp, bias=bias[:, i % 2, h:h + 1], scale=SCALE,
                              accum_out=rsum[:, i % 2, h:h + 1])
                last.then_inc(a.jprob_ready, 1)

            def copy_PT(i):
                act.wait_ge(rX.full, rX.nth(f"lt{i}"))
                op(PT[:, :, :], k.X.rearrange("p a (h t) -> p (a h) t", h=4), ACT.Copy).then_inc(a.jpT_ready, 1)

            def copy_OT(i):
                act.wait_ge(rW.full, rW.nth(f"pv{i}"))
                op(OT[:, :, :], O2[0:CKV, :, :], ACT.Copy).then_inc(a.oT_ready, 1)

            for n in range(QTR):
                keep_content(n)
            for i in range(TILES):
                for o in range(OCT):
                    keep_values(i, o)
                    if i + 1 < TILES:
                        keep_content(QTR * (i + 1) + o)
                    if i and o == 1:
                        copy_PT(i - 1)
                    if i and o == 2:
                        copy_OT(i - 1)
                exps(i)
            copy_PT(TILES - 1)
            copy_OT(TILES - 1)

        @block.vector
        def _(dve):
            ve = nc.vector
            loads, stores = (a.idx_loaded0, a.idx_loaded1), (a.out_stored0, a.out_stored1)
            step = [0]

            def link(ins):
                step[0] += 1
                ins.then_inc(a.d_step, 1)
                dve.wait_ge(a.d_step, step[0])

            def one_hots(n):
                i = n // QTR
                dve.wait_ge(loads[n % 2], 16 * (n // 2 + 1))
                for j in range(i + 1):
                    last = ve.tensor_scalar(onehot[:, n % 2, j, :], idxb[:, n % 2, :], C("iota")[:, j:j + 1], None, ALU.is_equal)
                last.then_inc(a.onehot_ready, 1)

            def keep_rope(n):
                i, q = n // QTR, n % QTR
                dve.wait_ge(rY.full, rY.nth(f"gr{n}"))
                ve.tensor_copy(KR[:, i % 2, :, :].rearrange("p t (g r) -> p r g t", g=GR)[:, q * RB:(q + 1) * RB, :, :],
                               k.Y[0:96, :, :].rearrange("p a (r g t) -> p (a r) g t", g=GR, t=32)).then_inc(a.kr_far_ready, 1)

            def mask_local(i):
                dve.wait_ge(rX.full, rX.nth(f"ls{i}"))
                ve.tensor_tensor(SC[:, i % 2, :, 0:SLOTS], k.X.rearrange("p a (h s) -> p (a h) s", h=4),
                                 C("mask_a0" if i == 0 else "mask_a").unsqueeze(1).broadcast_to([P, HEADS, SLOTS]),
                                 ALU.add).then_inc(a.lmasked, 1)

            def take_scores(i, o):
                reg, r = k.X, rX
                dve.wait_ge(r.full, r.nth(f"fs{i}.{o}"))
                dve.wait_ge(a.vfar_ready, OCT * i + o + 1)
                for g in range(GR):
                    part = reg[32 * g:32 * g + 32, :, :].rearrange("p a (q c) -> p (a q) c", c=P)[:, :, 0:96]
                    part = part.rearrange("p q (k h g) -> p q h k g", k=3, g=GR)[:, :, :, :, g]
                    last = ve.tensor_reduce(SN[32 * g:32 * g + 32, :, 8 * o:8 * o + 8].rearrange("p h t -> p t h"),
                                            part, AX.X, ALU.add)
                last.then_inc(a.far_ready, 1)

            def join_max(i):
                dve.wait_ge(a.far_ready, OCT * (i + 1))
                ve.transpose(SC[:, i % 2, :, SLOTS:J], SN[:, :, :]).then_inc(a.joined, 1)
                dve.wait_ge(a.joined, i + 1)
                dve.wait_ge(a.lmasked, i + 1)
                ve.tensor_reduce(nmax[:, i % 2, :], SC[:, i % 2, :, :], AX.X, ALU.max, negate=True).then_inc(a.jmax_ready, 1)
                dve.wait_ge(a.jmax_ready, i + 1)
                ve.tensor_scalar(bias[:, i % 2, :], nmax[:, i % 2, :], SCALE, None, ALU.mult).then_inc(a.bias_ready, 1)

            def recips(i):
                dve.wait_ge(a.jprob_ready, i + 1)
                ve.reciprocal(rrec[:, i % 2, :], rsum[:, i % 2, :]).then_inc(a.jrecip_ready, 1)

            def spread_blocks(i):
                dve.wait_ge(a.jnormed, i + 1)
                link(ve.transpose(PN[:, :, :], SC[:, i % 2, :, SLOTS:J]))
                if i:
                    dve.wait_ge(a.oT_ready, i)
                else:
                    dve.wait_ge(a.blocks_zeroed, 1)
                for g in range(GR):
                    e = slice(32 * g, 32 * g + 32)
                    last = ve.tensor_copy(PB[e, :, g, :], PN[e, :, :].rearrange("p h t -> p t h"))
                last.then_inc(a.blocks_ready, 1)

            def gate_out(i):
                dve.wait_ge(rW.full, rW.nth(f"so{i}"))
                ve.tensor_tensor(fT[:, :], k.Ub[:, 0:P], k.gate[:, tile(i)], ALU.mult).then_inc(a.fT_ready, 1)

            def add_residual(i):
                dve.wait_ge(rW.full, rW.nth(f"fin{i}"))
                if i >= 2:
                    dve.wait_ge(stores[i % 2], 16 * (i // 2))
                ve.tensor_tensor(o_sb[:, i % 2, :], k.Wb[:, 0:P], k.x_in[:, i, :], ALU.add).then_inc(a.out_ready, 1)

            one_hots(0)
            for n in range(QTR - 1):
                one_hots(n + 1)
                keep_rope(n)
            keep_rope(QTR - 1)
            mask_local(0)
            one_hots(QTR)
            for i in range(TILES):
                for o in range(OCT):
                    take_scores(i, o)
                    if i and o == 3:
                        gate_out(i - 1)
                    n = QTR * (i + 1) + o
                    if n + 1 < NF:
                        one_hots(n + 1)
                    if n < NF:
                        keep_rope(n)
                    if i and o == 0:
                        recips(i - 1)
                    if i and o == 1:
                        spread_blocks(i - 1)
                join_max(i)
                if i + 1 < TILES:
                    mask_local(i + 1)
                if i:
                    add_residual(i - 1)
            recips(TILES - 1)
            spread_blocks(TILES - 1)
            gate_out(TILES - 1)
            add_residual(TILES - 1)


def build(nc, x_d, const_d, rot_d, weights_d, setup_d, scratch, q_scratch, out_d):
    F, BF, FH, U32 = mybir.dt.float32, mybir.dt.bfloat16, mybir.dt.float16, mybir.dt.uint32
    ALU, ACT, AX = mybir.AluOpType, mybir.ActivationFunctionType, mybir.AxisListType
    cc, rr, ww, ss = layout()
    top = ExitStack()
    with top:
        def sb(name, shape, dt=F, ctx=top):
            return ctx.enter_context(nc.sbuf_tensor(name, shape, dt))

        def sem(name):
            return top.enter_context(nc.semaphore(name))

        consts = sb("consts", [P, cc.n])
        wts = sb("wts", [P, ww.n])
        istack = sb("istack_bf", [96, 32], BF)
        m1 = sb("m1", [CQ, HEADS * CKV])
        mo_rot = sb("mo_rot", [2 * CKV, HEADS * D])
        mo = mo_rot[0:CKV, :]
        rot_tab = mo_rot[CKV:2 * CKV, :]
        x_in = sb("x_in", [P, TILES, D])
        xnT = sb("xnT", [P, WIN + L])
        gate = sb("gate", [P, L])
        idx_h = sb("idx_h", [P, TILES, 32], FH)

        def C(name, rows=P):
            return consts[0:rows, cc.at[name][0]:cc.at[name][1]]

        def W(name, lo=0, width=None, r0=0, rows=P):
            s = ww.at[name][0] + lo
            return wts[r0:r0 + rows, s:(ww.at[name][1] if width is None else s + width)]

        PS = top.enter_context(nc.psum_tensor("PS", [P, 8, 512], F))
        X, Y, Z, Wb, Ub = PS[:, 0:2, :], PS[:, 2:4, :], PS[:, 4:6, :], PS[:, 6, :], PS[:, 7, :]

        loaded, setup_pe, setup_act, setup_dve = (sem(n) for n in ("loaded", "setup_pe", "setup_act", "setup_dve"))
        with ExitStack() as scope:
            rots = sb("rots", [2 * CKV, rr.n], F, scope)
            setw = sb("setw", [64, ss.n], F, scope)
            sig = sb("sig", [P, 8], F, scope)
            tmp_t = sb("tmp_t", [P, L], F, scope)

            def S(name, lo, width):
                s = ss.at[name][0] + lo
                return setw[0:64, s:s + width]

            with nc.Block() as block:
                @block.sync
                def _(sp):
                    sp.dma_start(consts[:, :], const_d).then_inc(loaded, 16)
                    sp.dma_start(wts[:, :], weights_d).then_inc(loaded, 16)
                    sp.dma_start(setw[:, :], setup_d).then_inc(loaded, 16)
                    sp.dma_start(rots[CKV:, :], rot_d).then_inc(loaded, 16)

                @block.tensor
                def _(pe):
                    pe.wait_ge(loaded, 64)
                    for h in range(HEADS):
                        nc.tensor.matmul(PS[0:CQ, 0, h * CKV:(h + 1) * CKV], S("uqT", h * CQ, CQ),
                                         S("ukT", h * CKV, CKV), start=True, stop=True)
                        nc.tensor.matmul(PS[0:CKV, 2 + h // 4, (h % 4) * D:(h % 4 + 1) * D],
                                         S("uvT", h * CKV, CKV), S("out", h * D, D),
                                         start=True, stop=True).then_inc(setup_pe, 1)

                @block.scalar
                def _(act):
                    act.wait_ge(loaded, 64)
                    nc.scalar.activation(sig[:, 0:1], W("delta"), ACT.Sigmoid).then_inc(setup_act, 1)
                    act.wait_ge(setup_act, 1)
                    nc.scalar.activation(sig[:, 1:2], sig[:, 0:1], ACT.Sin, bias=C("negpi"),
                                         scale=float(2 * np.pi)).then_inc(setup_act, 1)
                    nc.scalar.activation(sig[:, 2:3], sig[:, 0:1], ACT.Sin, scale=float(np.pi)).then_inc(setup_act, 1)

                @block.vector
                def _(dve):
                    n = [0]

                    def link(ins):
                        n[0] += 1
                        ins.then_inc(setup_dve, 1)
                        dve.wait_ge(setup_dve, n[0])
                    dve.wait_ge(loaded, 64)
                    link(nc.vector.memset(xnT[:, 0:WIN], 0.0))
                    link(nc.vector.tensor_copy(istack[:, :], C("istack", 96)))
                    dve.wait_ge(setup_act, 3)
                    link(nc.vector.tensor_tensor(sig[:, 3:4], sig[:, 2:3], sig[:, 2:3], ALU.mult))
                    link(nc.vector.tensor_scalar(sig[:, 4:5], sig[:, 3:4], -2.0, 1.0, ALU.mult, ALU.add))
                    link(nc.vector.tensor_tensor(sig[:, 5:6], sig[:, 1:2], C("sgn"), ALU.mult))
                    link(nc.vector.tensor_scalar(sig[:, 6:7], sig[:, 5:6], -1.0, None, ALU.mult))
                    cosd, sins, neg_sins = sig[:, 4:5], sig[:, 5:6], sig[:, 6:7]
                    for tab in ("tab_a", "tab_b"):
                        tc, ts = C(tab + "_c"), C(tab + "_s")
                        link(nc.vector.tensor_scalar(tmp_t[:, :], tc, sins, None, ALU.mult))
                        link(nc.vector.tensor_scalar(tc, tc, cosd, None, ALU.mult))
                        link(nc.vector.scalar_tensor_tensor(tc, ts, neg_sins, tc, ALU.mult, ALU.add))
                        link(nc.vector.scalar_tensor_tensor(ts, ts, cosd, tmp_t[:, :], ALU.mult, ALU.add))
                    link(nc.vector.tensor_scalar(rot_tab, rots[CKV:, 0:FAR * 32], sig[32:64, 4:5], None, ALU.mult))
                    link(nc.vector.scalar_tensor_tensor(rot_tab, rots[CKV:, FAR * 32:], sig[32:64, 1:2],
                                                        rot_tab, ALU.mult, ALU.add))
                    dve.wait_ge(setup_pe, HEADS)
                    link(nc.vector.tensor_copy(m1[:, :], PS[0:CQ, 0, 0:HEADS * CKV]))
                    link(nc.vector.tensor_copy(mo, PS[0:CKV, 2:4, :].rearrange("p a b -> p (a b)")))
        nc.all_engine_barrier()

        k = Core()
        k.sb, k.C, k.W, k.PS, k.X, k.Y, k.Z, k.Wb, k.Ub = sb, C, W, PS, X, Y, Z, Wb, Ub
        k.x_in, k.xnT, k.gate, k.idx_h, k.istack, k.m1, k.mo, k.rot_tab = x_in, xnT, gate, idx_h, istack, m1, mo, rot_tab
        k.x_d, k.out_d, k.scratch, k.q_scratch = x_d, out_d, scratch, q_scratch
        every = []

        def loop_sem(name):
            every.append(sem(name))
            return every[-1]
        k.sems = Signals(loop_sem)

        def clear_regions():
            nc.all_engine_barrier()
            for s in k.sems.regions:
                nc.gpsimd.sem_clear(s)
            nc.all_engine_barrier()

        with nc.Fori(0, B) as b:
            with ExitStack() as scope:
                project(nc, b, k, scope)
            clear_regions()
            with ExitStack() as kept:
                k.q_loc, k.key = sb("q_loc", [P, PAIRS, L], F, kept), sb("key", [P, 2, WIN + L], F, kept)
                k.CX, k.ckvS = sb("CX", [P, TILES, 96], BF, kept), sb("ckvS", [P, TILES, NW_T, CKV], F, kept)
                k.XR = sb("XR", [P, TILES, FAR, 96], BF, kept)
                k.idxb = sb("idxb", [P, 2, RB * P], FH, kept)
                with ExitStack() as scope:
                    latents(nc, b, k, scope)
                clear_regions()
                with ExitStack() as scope:
                    attend(nc, b, k, scope)
            nc.all_engine_barrier()
            for s in every:
                nc.gpsimd.sem_clear(s)
            nc.all_engine_barrier()


def kernel(**inputs):
    import concourse.bacc as bacc
    from concourse.bass_utils import run_bass_kernel_spmd

    v = {n: np.asarray(a) for n, a in inputs.items()}
    g = {n[len("L0_attn_"):]: a for n, a in v.items() if n.startswith("L0_attn_")}
    f = {n[len("L0_ffn_"):]: a for n, a in v.items() if n.startswith("L0_ffn_")}
    _, _, ww, ss = layout()
    consts, rots = constants()

    def rows(m, n=P):
        return np.concatenate([m, np.zeros((n - m.shape[0],) + m.shape[1:], np.float32)], 0) if m.shape[0] < n else m

    def swap(m, h):
        s = m.reshape(m.shape[:-1] + (-1, 2, h))
        return s[..., ::-1, :].reshape(m.shape)

    def col(m):
        return np.ascontiguousarray(m.T)

    def chunks(m):
        return rows(m, 3 * P).reshape(3, P).T

    qs, ks = f["q_scale"], f["k_scale"]
    qks = np.stack([np.concatenate([s, s]) for l in range(LAYERS)
                    for s in (qs[l], swap(qs[l], 32), ks[l], swap(ks[l], 32))], 1)
    pieces = {
        "dkv4": np.concatenate([g["W_dkv"]] * 4, 1), "dq": g["W_dq"],
        "kr4": np.concatenate([g["W_kr"]] * 4, 1), "kr4p": np.concatenate([swap(g["W_kr"], HALF)] * 4, 1),
        "idxq": g["idx_wq"], "idxk2": np.concatenate([g["idx_wk"]] * 2, 1),
        "qr": rows(g["W_qr"]), "qrp": rows(swap(g["W_qr"], HALF)),
        "qkv": np.concatenate(list(f["wqkv"]), 1),
        "rot": np.concatenate([swap(w[:, :2 * INNER], 32) for w in f["wqkv"]], 1),
        "wo": np.concatenate([w.reshape(PAIRS, P, D).transpose(1, 0, 2).reshape(P, -1) for w in f["wo"]], 1),
        "w1": np.concatenate(list(f["w1"]), 1),
        "w2": np.concatenate([rows(w, 3 * P).reshape(3, P, D).transpose(1, 0, 2).reshape(P, -1) for w in f["w2"]], 1),
        "qks": qks, "lng": col(f["ln_g"]), "lnb": col(f["ln_b"]),
        "b1a": np.concatenate([chunks(r[:HID]) for r in f["b1"]], 1),
        "b1g": np.concatenate([chunks(r[HID:]) for r in f["b1"]], 1),
        "b2": col(f["b2"]), "idxw": np.broadcast_to(g["idx_w"], (P, IDX_HEADS)),
        "delta": np.concatenate([g["raw_delta"]] * (P // HALF))[:, None],
    }
    weights = np.ascontiguousarray(np.concatenate([pieces[n] for n in ww.at], 1))

    def by_head(m, width):
        return m.reshape(m.shape[0], HEADS, width).transpose(2, 1, 0).reshape(width, -1)
    heads = {"uqT": by_head(g["W_uq"], DH), "ukT": by_head(g["W_uk"], DH), "uvT": by_head(g["W_uv"], DH),
             "out": g["W_out"].reshape(HEADS, DH, D).transpose(1, 0, 2).reshape(DH, -1)}
    setup = np.ascontiguousarray(np.concatenate([heads[n] for n in ss.at], 1))

    nc = bacc.Bacc("TRN2", target_bir_lowering=False, num_devices=1)
    dt = mybir.dt.float32
    arrays = {"x_dram": np.ascontiguousarray(g["x"]), "consts_dram": consts, "rots_dram": rots,
              "weights_dram": weights, "setup_dram": setup}
    aps = {n: nc.dram_tensor(n, m.shape, dt, kind="ExternalInput").ap() for n, m in arrays.items()}
    out = nc.dram_tensor("out", (B, L, D), dt, kind="ExternalOutput").ap()
    idx_scratch = nc.dram_tensor("idx_scratch", (FAR, L), mybir.dt.float16).ap()
    q_scratch = nc.dram_tensor("q_scratch", (2, 3, HEADS * 32, L), mybir.dt.bfloat16).ap()
    build(nc, *aps.values(), idx_scratch, q_scratch, out)
    r = run_bass_kernel_spmd(nc, [arrays], core_ids=[0])
    return r.results[0]["out"]
```

```python
from contextlib import ExitStack

import numpy as np

import concourse.bass as bass
from concourse import mybir

B, L, D = 4, 512, 128
P = 128
TILES = L // P
WIN = 64
NW_T = P // WIN
CKV, CQ, ROPE, HALF = 32, 64, 32, 16
HEADS, DH = 8, 64
IDX_HEADS = 4
TOPK = 96
FAR = TOPK - WIN
LAYERS = 2
INNER = HEADS * DH
HID = 341
HCH = [(0, 128), (128, 128), (256, HID - 256)]
PAIRS = HEADS // 2
SLOTS = 2 * WIN
SCALE = float((DH + ROPE) ** -0.5)
NEG = -1.0e30
RB = 8
GR = P // 32


class Columns:

    def __init__(self):
        self.at, self.n = {}, 0

    def add(self, name, width):
        self.at[name] = (self.n, self.n + width)
        self.n += width


def layout():
    c = Columns()
    for name, width in (("ident", P), ("pair_ones", 2), ("mean_ones", P), ("centre", P), ("istack", 32),
                        ("cos_q", L), ("sin_q", L), ("cos_k", L), ("sin_k", L),
                        ("tab_a_c", L), ("tab_a_s", L), ("tab_b_c", L), ("tab_b_s", L),
                        ("mask_f0", P), ("mask_f", P), ("mask_a0", P), ("mask_a", P), ("far_mask", P),
                        ("keep0", FAR), ("fill0", FAR), ("iota", TILES), ("sgn", 1), ("eps", 1),
                        ("negpi", 1)):
        c.add(name, width)
    r = Columns()
    for name, width in (("rot_c", FAR * 32), ("rot_s", FAR * 32)):
        r.add(name, width)
    w = Columns()
    for name, width in (("dkv4", 128), ("dq", CQ), ("kr4", 128), ("kr4p", 128), ("idxq", IDX_HEADS * DH),
                        ("idxk2", 128), ("qr", 256), ("qrp", 256), ("qkv", LAYERS * 3 * INNER),
                        ("rot", LAYERS * 2 * INNER), ("wo", LAYERS * 4 * D), ("w1", LAYERS * 2 * HID),
                        ("w2", LAYERS * 3 * D), ("qks", LAYERS * 4), ("lng", LAYERS), ("lnb", LAYERS),
                        ("b1a", LAYERS * 3), ("b1g", LAYERS * 3), ("b2", LAYERS), ("idxw", IDX_HEADS),
                        ("delta", 1)):
        w.add(name, width)
    s = Columns()
    for name, width in (("uqT", HEADS * CQ), ("ukT", HEADS * CKV), ("uvT", HEADS * CKV), ("out", HEADS * D)):
        s.add(name, width)
    return c, r, w, s


def constants():
    c, r, _, _ = layout()
    a = np.zeros((P, c.n), np.float32)

    def put(name, v):
        a[:, c.at[name][0]:c.at[name][1]] = v
    p = np.arange(P)
    put("ident", np.eye(P))
    put("pair_ones", (p[:, None] // DH == np.arange(2)[None, :]))
    put("mean_ones", 1.0 / D)
    put("centre", np.eye(P) - 1.0 / D)
    put("istack", (p[:, None] % 32 == np.arange(32)[None, :]) & (p[:, None] < 96))
    t = np.arange(L, dtype=np.float32)
    half = np.arange(0, DH, 2, dtype=np.float32)
    inv = (1.0 / np.float32(10000.0) ** (half / np.float32(DH))).astype(np.float32)
    fr = (t[:, None] * inv[None, :]).astype(np.float32).astype(np.float64)
    fr = np.concatenate([fr, fr], 1)
    base = (half.astype(np.float64) + 0.4 * DH) / (1.4 * DH)
    power = (t.astype(np.float64) - L // 2) / float(WIN // 2)
    sc = base[None, :] ** power[:, None]
    sc = np.concatenate([sc, sc], 1)
    sg = np.where(np.arange(DH) < DH // 2, -1.0, 1.0)
    for name, f in (("cos_q", np.cos(fr) * sc * 8.0), ("sin_q", np.sin(fr) * sc * 8.0 * sg),
                    ("cos_k", np.cos(fr) / sc), ("sin_k", np.sin(fr) / sc * sg)):
        put(name, np.tile(f.T, (2, 1)))
    theta = 1.0 / 10000.0 ** (2.0 * np.arange(HALF) / ROPE)
    theta = theta.astype(np.float32).astype(np.float64)
    sgn = np.where(p % ROPE < HALF, -1.0, 1.0)
    th = theta[p % HALF]
    pos = np.arange(L)
    for name, q in (("tab_a", pos), ("tab_b", np.where(pos < WIN, pos, 2 * pos - (WIN - 1)))):
        put(name + "_c", np.cos(th[:, None] * q[None, :]))
        put(name + "_s", np.sin(th[:, None] * q[None, :]) * sgn[:, None])
    m, s = (p % WIN)[:, None], np.arange(SLOTS)[None, :]
    first = (p < WIN)[:, None]
    f = (s >= m) & (s <= m + WIN)
    al = (s >= m + 1) & (s <= m + WIN)
    put("mask_f", np.where(f, 0.0, NEG))
    put("mask_f0", np.where(f & ~(first & (s < WIN)), 0.0, NEG))
    put("mask_a", np.where(al, 0.0, NEG))
    put("mask_a0", np.where(np.where(first, s >= WIN, al), 0.0, NEG))
    put("far_mask", np.where(p[None, :] <= p[:, None], 0.0, NEG))
    j = np.arange(FAR)[None, :]
    keep = j < (p[:, None] - (WIN - 1))
    put("keep0", keep)
    put("fill0", np.where(keep, 0, WIN + j))
    put("iota", p[:, None] + P * np.arange(TILES)[None, :])
    put("sgn", sgn[:, None])
    put("eps", 1e-5)
    put("negpi", -np.pi)
    rot = np.zeros((32, r.n), np.float32)
    ang = (WIN + np.arange(FAR))[:, None] * theta[None, :]
    rc = np.zeros((32, FAR, 32))
    rs = np.zeros((32, FAR, 32))
    for i in range(HALF):
        lo, hi = i, i + HALF
        rc[lo, :, lo] = rc[hi, :, hi] = np.cos(ang[:, i])
        rs[lo, :, lo] = rs[hi, :, hi] = -np.sin(ang[:, i])
        rc[hi, :, lo], rc[lo, :, hi] = -np.sin(ang[:, i]), np.sin(ang[:, i])
        rs[hi, :, lo], rs[lo, :, hi] = -np.cos(ang[:, i]), np.cos(ang[:, i])
    rot[:, r.at["rot_c"][0]:r.at["rot_c"][1]] = rc.reshape(32, -1)
    rot[:, r.at["rot_s"][0]:r.at["rot_s"][1]] = rs.reshape(32, -1)
    return a, rot


class Region:

    def __init__(self, full):
        self.full, self.jobs, self.read = full, {}, None

    def start(self, pe, job, read, count):
        assert job not in self.jobs, job
        self.jobs[job] = len(self.jobs) + 1
        if self.read:
            pe.wait_ge(*self.read)
        self.read = (read, count)

    def more(self, job):
        self.jobs[job] = len(self.jobs) + 1

    def nth(self, job):
        return self.jobs[job]


class Signals:

    def __init__(self, make):
        self.of_project, self.of_latents, self.of_attend = [], [], []
        group = self.of_project

        def sem(name):
            group.append(make(name))
            return group[-1]

        def full(program):
            return [sem(f"{program}_{r}_full") for r in "xyzwu"]
        self.project_full = full("project")
        self.x_kept = sem("x_kept")
        self.dve_step = sem("dve_step")
        self.var_ready = sem("var_ready")
        self.std_ready = sem("std_ready")
        self.xn_ready = sem("xn_ready")
        self.xnT_ready = sem("xnT_ready")
        self.qi_ready = sem("qi_ready")
        self.ki_ready = sem("ki_ready")
        self.relu_ready = sem("relu_ready")
        self.far_idx_ready = sem("far_idx_ready")
        self.far_idx_stored = sem("far_idx_stored")
        self.hT_ready = sem("hT_ready")
        self.sq_ready = sem("sq_ready")
        self.root_ready = sem("root_ready")
        self.rn_ready = sem("rn_ready")
        self.zeroed = sem("zeroed")
        self.parts_ready = sem("parts_ready")
        self.ab_ready = sem("ab_ready")
        self.k_ready = sem("k_ready")
        self.v_ready = sem("v_ready")
        self.masked_ready = sem("masked_ready")
        self.max_ready = sem("max_ready")
        self.nbias_ready = sem("nbias_ready")
        self.prob_ready = sem("prob_ready")
        self.recip_ready = sem("recip_ready")
        self.prob_normed = sem("prob_normed")
        self.pT_ready = sem("pT_ready")
        self.o_ready = sem("o_ready")
        self.x1_ready = sem("x1_ready")
        self.sqh_ready = sem("sqh_ready")
        self.lnh_ready = sem("lnh_ready")
        self.rstdh_ready = sem("rstdh_ready")
        self.hn_ready = sem("hn_ready")
        self.gelu_ready = sem("gelu_ready")
        self.hid_ready = sem("hid_ready")
        self.x2_ready = sem("x2_ready")
        self.kr_abs = sem("kr_abs")
        self.kr_exp = sem("kr_exp")
        self.kr_log = sem("kr_log")
        self.kr_soft = sem("kr_soft")
        group = self.of_latents
        self.latents_full = full("latents")
        self.l_step = sem("l_step")
        self.cq_ready = sem("cq_ready")
        self.keys_zeroed = sem("keys_zeroed")
        self.ckvs_ready = sem("ckvs_ready")
        self.qc_ready = sem("qc_ready")
        self.abs_ready = sem("abs_ready")
        self.expn_ready = sem("expn_ready")
        self.log_ready = sem("log_ready")
        self.soft_ready = sem("soft_ready")
        self.krT_ready = sem("krT_ready")
        self.qb_ready = sem("qb_ready")
        self.qa_ready = sem("qa_ready")
        self.hi_ready = sem("hi_ready")
        self.rest_ready = sem("rest_ready")
        self.mid_ready = sem("mid_ready")
        self.lo_ready = sem("lo_ready")
        self.lo_pool = sem("lo_pool")
        self.q3_stored = sem("q3_stored")
        self.pool_prod = sem("pool_prod")
        group = self.of_attend
        self.attend_full = full("attend")
        self.x_loaded = sem("x_loaded")
        self.d_step = sem("d_step")
        self.idx_loaded0 = sem("idx_loaded0")
        self.idx_loaded1 = sem("idx_loaded1")
        self.q3_loaded = sem("q3_loaded")
        self.onehot_ready = sem("onehot_ready")
        self.kc_ready = sem("kc_ready")
        self.kr_far_ready = sem("kr_far_ready")
        self.lmasked = sem("lmasked")
        self.far_ready = sem("far_ready")
        self.vfar_ready = sem("vfar_ready")
        self.joined = sem("joined")
        self.jmax_ready = sem("jmax_ready")
        self.bias_ready = sem("bias_ready")
        self.jprob_ready = sem("jprob_ready")
        self.jrecip_ready = sem("jrecip_ready")
        self.jnormed = sem("jnormed")
        self.jpT_ready = sem("jpT_ready")
        self.blocks_zeroed = sem("blocks_zeroed")
        self.blocks_ready = sem("blocks_ready")
        self.oT_ready = sem("oT_ready")
        self.fT_ready = sem("fT_ready")
        self.out_ready = sem("out_ready")
        self.out_stored0 = sem("out_stored0")
        self.out_stored1 = sem("out_stored1")


class Core:
    pass


def project(nc, b, k, scope):
    F, U32 = mybir.dt.float32, mybir.dt.uint32
    ALU, ACT, AX = mybir.AluOpType, mybir.ActivationFunctionType, mybir.AxisListType
    a, C, W = k.sems, k.C, k.W

    def sb(name, shape, dt=F):
        return k.sb(name, shape, dt, scope)
    def far_width(i):
        return WIN + P * i
    far_at = [sum(far_width(j) for j in range(i)) for i in range(TILES + 1)]
    stats, mv, std, rstd = sb("stats", [P, TILES, 6]), sb("mv", [P, TILES, 2]), sb("std", [P, TILES]), sb("rstd", [P, TILES])
    qiT, kiZ = sb("qiT", [P, 2, L]), sb("kiZ", [P, 2, L])
    relu = sb("relu", [P, 2, 2, far_at[TILES]])
    score, best = sb("score", [P, 2, L]), sb("best", [P, FAR])
    idx_u, idx_f, idx_t = sb("idx_u", [P, FAR], U32), sb("idx_f", [P, FAR]), sb("idx_t", [P, FAR])
    hT = sb("hT", [P, WIN + L])
    sq, rn = sb("sq", [P, 2, L]), sb("rn", [P, L])
    root, rnorm = sb("root", [P, 2, PAIRS, TILES, 2]), sb("rnorm", [P, 2, PAIRS, TILES, 2])
    pa, pb = sb("pa", [P, 2, L]), sb("pb", [P, 2, L])
    ab, qT, kZ = sb("ab", [P, PAIRS, L]), sb("qT", [P, PAIRS, L]), sb("kZ", [P, PAIRS, 2, WIN + L])
    v = sb("v", [P, NW_T, TILES, INNER])
    S = sb("S", [P, TILES, HEADS, SLOTS])
    nmax, nbias = sb("nmax", [P, TILES, HEADS]), sb("nbias", [P, TILES, HEADS])
    rsum, rrec = sb("rsum", [P, TILES, HEADS]), sb("rrec", [P, TILES, HEADS])
    pT, oT = sb("pT", [P, 2, HEADS, P]), sb("oT", [P, PAIRS, L])
    x1, x2 = sb("x1", [P, 1 + L]), sb("x2", [P, 1 + L])
    xn = pT[:, 0, 0:TILES, :]
    spare = S[:, :, :, :].rearrange("p i h s -> p (i h s)").rearrange("p (n t) -> p n t", t=L)
    lnr, hn, gl, hid = spare[:, 0, :], spare[:, 1, :], spare[:, 3:5, :], spare[:, 5:8, :]
    rX, rY, rZ, rW, rU = (Region(full) for full in a.project_full)

    rk_wide = S[:, 0:2, :, :].rearrange("p a h s -> p (a h s)").rearrange("p (c i f) -> p c i f", c=PAIRS, i=TILES)

    def pair(n):
        return (k.X, rX) if n % 2 == 0 else (k.Y, rY)

    def sums(n):
        return (k.Ub, rU) if n < PAIRS else (k.Z[:, 0, :], rZ)

    def spread(c):
        return (k.Wb, rW) if c % 2 == 0 else (k.Ub, rU)

    def half(par):
        return slice(DH * par, DH * par + DH)

    def tile(i):
        return slice(i * P, (i + 1) * P)
    K, Q = 0, 1

    with nc.Block() as block:
        @block.tensor
        def _(pe):
            mm = nc.tensor.matmul
            rZ.start(pe, "xnT", a.xnT_ready, 1)
            pe.wait_ge(a.xn_ready, TILES)
            for i in range(TILES):
                last = nc.tensor.transpose(k.Z[:, 0, tile(i)], xn[:, i, :], C("ident"))
            last.then_inc(rZ.full, 1)
            pe.wait_ge(a.xnT_ready, 1)
            rY.start(pe, "ki", a.ki_ready, 1)
            mm(k.Y[:, 0, :], W("idxk2"), k.xnT[:, WIN:], start=True, stop=True).then_inc(rY.full, 1)
            rX.start(pe, "qi", a.qi_ready, 1)
            for c in range(2):
                last = mm(k.X[:, c, :], W("idxq", c * P, P), k.xnT[:, WIN:], start=True, stop=True)
            last.then_inc(rX.full, 1)
            pe.wait_ge(a.zeroed, 1)
            pe.wait_ge(a.ki_ready, 1)
            pe.wait_ge(a.qi_ready, 1)
            for i in range(TILES):
                for hp in range(2):
                    reg, r = pair(hp)
                    r.start(pe, f"idx{i}.{hp}", a.relu_ready, 2 * i + hp + 1)
                    for j in range(2):
                        last = mm(reg[:, j, 0:far_width(i)], qiT[:, hp, tile(i)], kiZ[:, j, 0:far_width(i)],
                                  start=True, stop=True)
                    last.then_inc(r.full, 1)

            def qk(l, n):
                c, which = n % PAIRS, 1 - n // PAIRS
                reg, r = pair(n)
                r.start(pe, f"qk{l}.{n}", a.parts_ready, 8 * l + n + 1)
                mm(reg[:, 0, :], W("qkv", l * 3 * INNER + which * INNER + c * P, P), hT[:, WIN:], start=True, stop=True)
                mm(reg[:, 1, :], W("rot", l * 2 * INNER + which * INNER + c * P, P), hT[:, WIN:],
                   start=True, stop=True).then_inc(r.full, 1)

            def square_sums(l, n):
                reg, r = sums(n)
                if n % PAIRS == 0:
                    r.start(pe, f"ss{l}.{n}", a.root_ready, 2 * l + 1 + n // PAIRS)
                else:
                    r.more(f"ss{l}.{n}")
                pe.wait_ge(a.sq_ready, 8 * l + n + 1)
                for i in range(TILES):
                    at = (n % PAIRS * TILES + i) * 2
                    last = mm(reg[:, at:at + 2], sq[:, n % 2, tile(i)], C("pair_ones"), start=True, stop=True)
                last.then_inc(r.full, 1)

            def spread_k(l, c):
                reg, r = spread(c)
                r.start(pe, f"rk{l}.{c}", a.k_ready, PAIRS * l + c + 1)
                pe.wait_ge(a.rn_ready, 2 * l + 1)
                for i in range(TILES):
                    last = mm(reg[:, tile(i)], rk_wide[:, c, i, :], C("ident"), start=True, stop=True)
                last.then_inc(r.full, 1)

            def values(l, i):
                rZ.start(pe, f"v{l}.{i}", a.v_ready, TILES * l + i + 1)
                for par in range(2):
                    at = WIN + i * P - WIN * (1 - par)
                    last = mm(k.Z[:, par, :], hT[:, at:at + P], W("qkv", l * 3 * INNER + 2 * INNER, INNER),
                              start=True, stop=True)
                last.then_inc(rZ.full, 1)

            def scores(l, i):
                reg, r = pair(i)
                r.start(pe, f"s{l}.{i}", a.masked_ready, TILES * l + i + 1)
                for h in range(HEADS):
                    for w in range(NW_T):
                        t0 = i * P + w * WIN
                        last = mm(reg[64 * w:64 * w + 64, h // 4, (h % 4) * P:(h % 4 + 1) * P],
                                  qT[:, h // 2, t0:t0 + WIN], kZ[:, h // 2, h % 2, t0:t0 + SLOTS], start=True, stop=True)
                last.then_inc(r.full, 1)

            def prob_T(l, i):
                rZ.start(pe, f"t{l}.{i}", a.pT_ready, TILES * l + i + 1)
                pe.wait_ge(a.prob_normed, TILES * l + i + 1)
                for h in range(HEADS):
                    last = nc.tensor.transpose(k.Z[:, h // 4, (h % 4) * P:(h % 4 + 1) * P], S[:, i, h, :], C("ident"))
                last.then_inc(rZ.full, 1)

            def weigh_values(l, i):
                rW.start(pe, f"o{l}.{i}", a.o_ready, TILES * l + i + 1)
                pe.wait_ge(a.pT_ready, TILES * l + i + 1)
                for h in range(HEADS):
                    for w in range(NW_T):
                        last = mm(k.Wb[64 * (h % 2):64 * (h % 2) + 64, (h // 2) * P + w * WIN:(h // 2) * P + (w + 1) * WIN],
                                  v[:, w, i, h * DH:(h + 1) * DH], pT[:, i % 2, h, w * WIN:(w + 1) * WIN],
                                  start=True, stop=True)
                last.then_inc(rW.full, 1)

            def project_heads(l, i):
                if i == 0:
                    rU.start(pe, f"wo{l}.{i}", a.x1_ready, l + 1)
                else:
                    rU.more(f"wo{l}.{i}")
                pe.wait_ge(a.o_ready, TILES * l + i + 1)
                for c in range(PAIRS):
                    last = mm(k.Ub[:, tile(i)], W("wo", (l * PAIRS + c) * D, D), oT[:, c, tile(i)],
                              start=(c == 0), stop=(c == PAIRS - 1))
                last.then_inc(rU.full, 1)

            for l in range(LAYERS):
                pe.wait_ge(a.hT_ready, 2 * l + 1)
                for n in range(8):
                    qk(l, n)
                    if n:
                        square_sums(l, n - 1)
                    if n > PAIRS:
                        spread_k(l, n - PAIRS - 1)
                square_sums(l, 7)
                spread_k(l, PAIRS - 1)
                values(l, 0)
                pe.wait_ge(a.ab_ready, 8 * l + 8)
                pe.wait_ge(a.k_ready, PAIRS * (l + 1))
                scores(l, 0)
                scores(l, 1)
                values(l, 1)
                scores(l, 2)
                values(l, 2)
                scores(l, 3)
                values(l, 3)
                prob_T(l, 0)
                for i in range(TILES):
                    if i + 1 < TILES:
                        prob_T(l, i + 1)
                    weigh_values(l, i)
                    if i:
                        project_heads(l, i - 1)
                if l == LAYERS - 1:
                    rZ.start(pe, "kr", a.kr_soft, 1)
                    mm(k.Z[:, 0, :], W("kr4"), k.xnT[:, WIN:], start=True, stop=True)
                    mm(k.Z[:, 1, :], W("kr4p"), k.xnT[:, WIN:], start=True, stop=True).then_inc(rZ.full, 1)
                project_heads(l, TILES - 1)
                rX.start(pe, f"centred{l}", a.hn_ready, l + 1)
                pe.wait_ge(a.hT_ready, 2 * l + 2)
                mm(k.X[:, 0, :], C("centre"), hT[:, WIN:], start=True, stop=True).then_inc(rX.full, 1)
                rY.start(pe, f"var{l}", a.lnh_ready, l + 1)
                pe.wait_ge(a.sqh_ready, l + 1)
                mm(k.Y[:, 0, :], C("mean_ones"), sq[:, 0, :], start=True, stop=True).then_inc(rY.full, 1)
                pe.wait_ge(a.hn_ready, l + 1)
                for j, (off, n) in enumerate(HCH):
                    reg, r = pair(j)
                    r.start(pe, f"up{l}.{j}", a.hid_ready, 3 * l + j + 1)
                    mm(reg[0:n, 0, :], W("w1", l * 2 * HID + HID + off, n), hn,
                       start=True, stop=True).then_inc(r.full, 1)
                    r.more(f"up{l}.{j} linear")
                    mm(reg[0:n, 1, :], W("w1", l * 2 * HID + off, n), hn, start=True, stop=True).then_inc(r.full, 1)
                rU.start(pe, f"down{l}", a.x2_ready, l + 1)
                for j, (off, n) in enumerate(HCH):
                    pe.wait_ge(a.hid_ready, 3 * l + j + 1)
                    last = mm(k.Ub, W("w2", (l * 3 + j) * D, D, rows=n), hid[0:n, j, :], start=(j == 0), stop=(j == 2))
                last.then_inc(rU.full, 1)

        @block.sync
        def _(sp):
            sp.wait_ge(a.far_idx_ready, 1)
            for g in range(GR):
                sp.dma_start(k.scratch.rearrange("r (i g t) -> g r i t", g=GR, t=32)[g],
                             k.idx_h[32 * g:32 * g + 32, :, :]).then_inc(a.far_idx_stored, 16)
            sp.wait_ge(a.far_idx_stored, 16 * GR)

        @block.gpsimd
        def _(pool):
            for s in a.of_attend:
                nc.gpsimd.sem_clear(s)
            for par in range(2):
                nc.gpsimd.memset(kiZ[half(1 - par), par, :], 0.0)
            for par in range(2):
                nc.gpsimd.memset(kZ[half(1 - par), :, par, :], 0.0)
                last = nc.gpsimd.memset(kZ[half(par), :, par, 0:WIN], 0.0)
            last.then_inc(a.zeroed, 1)
            pool.wait_ge(a.zeroed, 1)
            nc.gpsimd.tensor_copy(k.x_in[:, :, :], k.x_next[:, :, :]).then_inc(a.x_kept, 1)
            pool.wait_ge(a.x_kept, 1)
            for l in range(LAYERS):
                for n in range(8):
                    pool.wait_ge(a.parts_ready, 8 * l + n + 1)
                    dst = ab[:, n, :] if n < PAIRS else qT[:, n - PAIRS, :]
                    nc.gpsimd.tensor_tensor(dst, pa[:, n % 2, :], pb[:, n % 2, :], ALU.add).then_inc(a.ab_ready, 1)
                for i in range(TILES):
                    pool.wait_ge(a.recip_ready, TILES * l + i + 1)
                    nc.gpsimd.tensor_tensor(S[:, i, :, :], S[:, i, :, :],
                                            rrec[:, i, :].unsqueeze(2).broadcast_to([P, HEADS, SLOTS]),
                                            ALU.mult).then_inc(a.prob_normed, 1)

        @block.scalar
        def _(act):
            op = nc.scalar.activation
            act.wait_ge(a.var_ready, 1)
            op(std[:, :], mv[:, :, 1], ACT.Sqrt, bias=C("eps")).then_inc(a.std_ready, 1)
            act.wait_ge(rZ.full, rZ.nth("xnT"))
            op(k.xnT[:, WIN:], k.Z[:, 0, :], ACT.Copy).then_inc(a.xnT_ready, 1)
            act.wait_ge(rY.full, rY.nth("ki"))
            act.wait_ge(a.zeroed, 1)
            for par in range(2):
                last = op(kiZ[half(par), par, :], k.Y[half(par), 0, :], ACT.Copy)
            last.then_inc(a.ki_ready, 1)
            act.wait_ge(rX.full, rX.nth("qi"))
            op(qiT[:, :, :], k.X, ACT.Copy).then_inc(a.qi_ready, 1)
            for i in range(TILES):
                for hp in range(2):
                    reg, r = pair(hp)
                    act.wait_ge(r.full, r.nth(f"idx{i}.{hp}"))
                    op(relu[:, hp, :, far_at[i]:far_at[i + 1]], reg[:, :, 0:far_width(i)], ACT.Relu).then_inc(a.relu_ready, 1)

            def squares(l, n):
                reg, r = pair(n)
                act.wait_ge(r.full, r.nth(f"qk{l}.{n}"))
                if n >= 2:
                    r = sums(n - 2)[1]
                    act.wait_ge(r.full, r.nth(f"ss{l}.{n - 2}"))
                elif l:
                    act.wait_ge(rZ.full, rZ.nth(f"ss{l - 1}.{6 + n}"))
                    act.wait_ge(rY.full, rY.nth(f"var{l - 1}"))
                op(sq[:, n % 2, :], reg[:, 0, :], ACT.Square).then_inc(a.sq_ready, 1)

            def norms(l, which):
                reg, r = sums(PAIRS * which)
                act.wait_ge(r.full, r.nth(f"ss{l}.{PAIRS * which + PAIRS - 1}"))
                if l:
                    act.wait_ge(a.rn_ready, 2 * (l - 1) + which + 1)
                op(root[:, which, :, :, :].rearrange("p c i e -> p (c i e)"), reg[:, 0:PAIRS * TILES * 2],
                   ACT.Sqrt).then_inc(a.root_ready, 1)

            def exps(l, i):
                act.wait_ge(a.nbias_ready, TILES * l + i + 1)
                for h in range(HEADS):
                    last = op(S[:, i, h, :], S[:, i, h, :], ACT.Exp, bias=nbias[:, i, h:h + 1],
                              scale=rnorm[:, Q, h // 2, i, h % 2:h % 2 + 1], accum_out=rsum[:, i, h:h + 1])
                last.then_inc(a.prob_ready, 1)

            def copy_v(l, i):
                act.wait_ge(rZ.full, rZ.nth(f"v{l}.{i}"))
                op(v[:, :, i, :], k.Z, ACT.Copy).then_inc(a.v_ready, 1)

            def copy_pT(l, i):
                act.wait_ge(rZ.full, rZ.nth(f"t{l}.{i}"))
                if i >= 2:
                    act.wait_ge(a.o_ready, TILES * l + i - 1)
                op(pT[:, i % 2, :, :], k.Z.rearrange("p a (h t) -> p (a h) t", h=4), ACT.Copy).then_inc(a.pT_ready, 1)

            for l in range(LAYERS):
                for n in range(8):
                    squares(l, n)
                    if n == PAIRS:
                        norms(l, K)
                norms(l, Q)
                copy_v(l, 0)
                for i in range(TILES - 1):
                    exps(l, i)
                copy_pT(l, 0)
                exps(l, TILES - 1)
                for i in range(1, TILES):
                    copy_pT(l, i)
                if l == LAYERS - 1:
                    act.wait_ge(rZ.full, rZ.nth("kr"))
                    op(k.soft_kr[:, :, :], k.Z, ACT.Abs).then_inc(a.kr_abs, 1)
                    act.wait_ge(a.kr_abs, 1)
                    op(k.soft_kr[:, :, :], k.soft_kr[:, :, :], ACT.Exp, scale=-1.0).then_inc(a.kr_exp, 1)
                    act.wait_ge(a.kr_exp, 1)
                    op(k.soft_kr[:, :, :], k.soft_kr[:, :, :], ACT.Ln, bias=1.0).then_inc(a.kr_log, 1)
                act.wait_ge(rX.full, rX.nth(f"centred{l}"))
                op(sq[:, 0, :], k.X[:, 0, :], ACT.Square).then_inc(a.sqh_ready, 1)
                act.wait_ge(rY.full, rY.nth(f"var{l}"))
                op(lnr, k.Y[:, 0, :], ACT.Ln, bias=C("eps")).then_inc(a.lnh_ready, 1)
                act.wait_ge(a.lnh_ready, l + 1)
                op(rn[:, :], lnr, ACT.Exp, scale=-0.5).then_inc(a.rstdh_ready, 1)
                for j, (off, n) in enumerate(HCH):
                    reg, r = pair(j)
                    act.wait_ge(r.full, r.nth(f"up{l}.{j}"))
                    if j >= 2:
                        act.wait_ge(a.hid_ready, 3 * l + j - 1)
                    op(gl[0:n, j % 2, :], reg[0:n, 0, :], ACT.Gelu, bias=W("b1g", 3 * l + j, 1, rows=n)).then_inc(a.gelu_ready, 1)
            act.wait_ge(a.x2_ready, LAYERS)
            op(k.gate[:, :], x2[:, 1:], ACT.Silu)

        @block.vector
        def _(dve):
            ve = nc.vector
            step = [0]

            def link(ins):
                step[0] += 1
                ins.then_inc(a.dve_step, 1)
                dve.wait_ge(a.dve_step, step[0])
            for i in range(TILES):
                ins = ve.bn_stats(stats[:, i, :], k.x_next[:, i, :])
            link(ins)
            for i in range(TILES):
                ins = ve.bn_aggr(mv[:, i, :], stats[:, i, :])
            ins.then_inc(a.var_ready, 1)
            link(ve.memset(hT[:, 0:WIN], 0.0))
            link(ve.memset(x1[:, 0:1], 0.0))
            link(ve.memset(x2[:, 0:1], 0.0))
            dve.wait_ge(a.var_ready, 1)
            dve.wait_ge(a.std_ready, 1)
            link(ve.reciprocal(rstd[:, :], std[:, :]))
            for i in range(TILES):
                ve.tensor_scalar(xn[:, i, :], k.x_next[:, i, :], mv[:, i, 0:1], rstd[:, i:i + 1], ALU.subtract,
                                 ALU.mult).then_inc(a.xn_ready, 1)

            def sum_heads(i):
                n, at = far_width(i), slice(far_at[i], far_at[i + 1])
                out = score[:, i % 2, 0:n]
                dve.wait_ge(a.relu_ready, 2 * i + 2)
                link(ve.tensor_scalar(out, relu[:, 0, 0, at], W("idxw", 0, 1), None, ALU.mult))
                for h in range(1, IDX_HEADS):
                    link(ve.scalar_tensor_tensor(out, relu[:, h // 2, h % 2, at], W("idxw", h, 1), out, ALU.mult, ALU.add))
                c0 = max(n - P, 0)
                link(ve.tensor_tensor(score[:, i % 2, c0:n], score[:, i % 2, c0:n], C("far_mask")[:, P - (n - c0):], ALU.add))

            def next_best(i, q):
                n, e = far_width(i), slice(8 * q, 8 * q + 8)
                out = score[:, i % 2, 0:n]
                link(ve.max(best[:, e], out))
                link(ve.max_index(idx_u[:, e], best[:, e], out))
                if q < FAR // 8 - 1:
                    link(ve.match_replace(out, best[:, e], out, -3.0e38))

            def keep_indices(i):
                link(ve.tensor_copy(idx_f[:, :], idx_u[:, :]))
                if i == 0:
                    link(ve.tensor_tensor(idx_f[:, :], idx_f[:, :], C("keep0"), ALU.mult))
                    link(ve.tensor_tensor(idx_f[:, :], idx_f[:, :], C("fill0"), ALU.add))
                link(ve.transpose(idx_t[:, :], idx_f[:, :]))
                ins = ve.tensor_copy(k.idx_h[:, i, :], idx_t[:, :])
                if i < TILES - 1:
                    link(ins)
                else:
                    ins.then_inc(a.far_idx_ready, 1)

            def shift_tokens(src, off):
                link(ve.tensor_copy(hT[0:64, WIN:], src[0:64, off:off + L]))
                ve.tensor_copy(hT[64:128, WIN:], src[64:128, off - 1:off - 1 + L]).then_inc(a.hT_ready, 1)

            def parts(l, n):
                reg, r = pair(n)
                which = n // PAIRS
                cos, sin = (("cos_k", "sin_k"), ("cos_q", "sin_q"))[which]
                dve.wait_ge(r.full, r.nth(f"qk{l}.{n}"))
                if 8 * l + n >= 2:
                    dve.wait_ge(a.ab_ready, 8 * l + n - 1)
                link(ve.scalar_tensor_tensor(pb[:, n % 2, :], reg[:, 1, :], W("qks", 4 * l + 2 * (1 - which) + 1, 1), C(sin),
                                             ALU.mult, ALU.mult))
                dve.wait_ge(a.sq_ready, 8 * l + n + 1)
                ve.scalar_tensor_tensor(pa[:, n % 2, :], reg[:, 0, :], W("qks", 4 * l + 2 * (1 - which), 1), C(cos),
                                        ALU.mult, ALU.mult).then_inc(a.parts_ready, 1)

            def inverse_norms(l, which):
                dve.wait_ge(a.root_ready, 2 * l + which + 1)
                r = rnorm[:, which, :, :, :]
                link(ve.tensor_scalar(r, root[:, which, :, :, :], 1.0e-12, None, ALU.max))
                if which == Q:
                    ve.reciprocal(r, r).then_inc(a.rn_ready, 1)
                else:
                    link(ve.reciprocal(r, r))
                    ve.tensor_copy(rk_wide.rearrange("p c i (e f) -> p (c i e) f", e=2),
                                   r.rearrange("p c i e -> p (c i e)").unsqueeze(2).broadcast_to([P, PAIRS * TILES * 2, DH])
                                   ).then_inc(a.rn_ready, 1)

            def norm_k(l, c):
                dve.wait_ge(a.ab_ready, 8 * l + c + 1)
                reg, r = spread(c)
                dve.wait_ge(r.full, r.nth(f"rk{l}.{c}"))
                link(ve.tensor_tensor(kZ[half(0), c, 0, WIN:], ab[half(0), c, :], reg[half(0), :], ALU.mult))
                ve.tensor_tensor(kZ[half(1), c, 1, WIN:], ab[half(1), c, :], reg[half(1), :], ALU.mult).then_inc(a.k_ready, 1)

            def mask_max(l, i):
                reg, r = pair(i)
                dve.wait_ge(r.full, r.nth(f"s{l}.{i}"))
                ve.tensor_tensor(S[:, i, :, :], reg.rearrange("p a (h s) -> p (a h) s", h=4),
                                 C("mask_f0" if i == 0 else "mask_f").unsqueeze(1).broadcast_to([P, HEADS, SLOTS]),
                                 ALU.add).then_inc(a.masked_ready, 1)
                dve.wait_ge(a.masked_ready, TILES * l + i + 1)
                ve.tensor_reduce(nmax[:, i, :], S[:, i, :, :], AX.X, ALU.max, negate=True).then_inc(a.max_ready, 1)
                dve.wait_ge(a.max_ready, TILES * l + i + 1)
                ve.tensor_tensor(nbias[:, i, :].rearrange("p (c e) -> p c e", e=2),
                                 nmax[:, i, :].rearrange("p (c e) -> p c e", e=2), rnorm[:, Q, :, i, :],
                                 ALU.mult).then_inc(a.nbias_ready, 1)

            def recips(l, i):
                dve.wait_ge(a.prob_ready, TILES * l + i + 1)
                ve.reciprocal(rrec[:, i, :], rsum[:, i, :]).then_inc(a.recip_ready, 1)

            def copy_v(l, i):
                dve.wait_ge(rZ.full, rZ.nth(f"v{l}.{i}"))
                ve.tensor_copy(v[:, :, i, :], k.Z).then_inc(a.v_ready, 1)

            def copy_o(l, i):
                dve.wait_ge(rW.full, rW.nth(f"o{l}.{i}"))
                ve.tensor_copy(oT[:, :, tile(i)], k.Wb.rearrange("p (c t) -> p c t", c=PAIRS)).then_inc(a.o_ready, 1)

            x, off = k.xnT, WIN
            dve.wait_ge(a.xnT_ready, 1)
            for l in range(LAYERS):
                shift_tokens(x, off)
                for n in range(8):
                    parts(l, n)
                    if n == 0:
                        sum_heads(2 * l)
                    if n in (1, 2, 3):
                        next_best(2 * l, n - 1)
                    if n == 5:
                        next_best(2 * l, 3)
                    if n == 6:
                        keep_indices(2 * l)
                    if n == PAIRS:
                        inverse_norms(l, K)
                    if n > PAIRS:
                        norm_k(l, n - PAIRS - 1)
                norm_k(l, PAIRS - 1)
                inverse_norms(l, Q)
                dve.wait_ge(a.rn_ready, 2 * l + 2)
                mask_max(l, 0)
                mask_max(l, 1)
                copy_v(l, 1)
                recips(l, 0)
                mask_max(l, 2)
                copy_v(l, 2)
                recips(l, 1)
                mask_max(l, 3)
                copy_v(l, 3)
                recips(l, 2)
                recips(l, 3)
                sum_heads(2 * l + 1)
                copy_o(l, 0)
                next_best(2 * l + 1, 0)
                copy_o(l, 1)
                next_best(2 * l + 1, 1)
                copy_o(l, 2)
                next_best(2 * l + 1, 2)
                copy_o(l, 3)
                dve.wait_ge(rU.full, rU.nth(f"wo{l}.{TILES - 1}"))
                ve.tensor_tensor(x1[:, 1:], k.Ub, x[:, off:off + L], ALU.add).then_inc(a.x1_ready, 1)
                dve.wait_ge(a.x1_ready, l + 1)
                shift_tokens(x1, 1)
                next_best(2 * l + 1, 3)
                keep_indices(2 * l + 1)
                if l == LAYERS - 1:
                    dve.wait_ge(a.kr_log, 1)
                    ve.scalar_tensor_tensor(k.soft_kr[:, :, :], k.Z, 0.0, k.soft_kr[:, :, :], ALU.max,
                                            ALU.add).then_inc(a.kr_soft, 1)
                dve.wait_ge(a.rstdh_ready, l + 1)
                ve.tensor_tensor(hn, k.X[:, 0, :], rn[:, :], ALU.mult).then_inc(a.hn_ready, 1)
                for j, (o, n) in enumerate(HCH):
                    reg, r = pair(j)
                    dve.wait_ge(r.full, r.nth(f"up{l}.{j} linear"))
                    dve.wait_ge(a.gelu_ready, 3 * l + j + 1)
                    ve.scalar_tensor_tensor(hid[0:n, j, :], reg[0:n, 1, :], W("b1a", 3 * l + j, 1, rows=n),
                                            gl[0:n, j % 2, :], ALU.add, ALU.mult).then_inc(a.hid_ready, 1)
                dve.wait_ge(rU.full, rU.nth(f"down{l}"))
                ve.scalar_tensor_tensor(x2[:, 1:], k.Ub, W("b2", l, 1), x1[:, 1:], ALU.add, ALU.add).then_inc(a.x2_ready, 1)
                dve.wait_ge(a.x2_ready, l + 1)
                x, off = x2, 1


def latents(nc, b, k, scope):
    F, BF = mybir.dt.float32, mybir.dt.bfloat16
    ALU, ACT = mybir.AluOpType, mybir.ActivationFunctionType
    a, C, W = k.sems, k.C, k.W

    def sb(name, shape, dt=F):
        return k.sb(name, shape, dt, scope)
    cqT, qcT = sb("cqT", [CQ, L]), sb("qcT", [P, 2, L])
    mag, soft = sb("mag", [P, 2, 2, L]), sb("soft", [P, 2, 2, L])
    prod = sb("prod", [P, 2, L])
    pprod = sb("pprod", [P, 2, L])
    qa = sb("qa", [P, 2, L])
    q3s = sb("q3s", [P, 2, 2, 3, L], BF)
    rest = sb("rest", [P, 9, FAR * 32])
    rX, rY, rZ, rW, rU = (Region(full) for full in a.latents_full)


    def tile(i):
        return slice(i * P, (i + 1) * P)

    def soft_region(n):
        return ((k.Z, rZ), (k.Y, rY))[n]

    def rank_region(j):
        return (k.Y, rY) if j == 2 else (k.X, rX)

    def split_job(kind, c):
        if kind == "value":
            return k.ckvS[:, :, 1, :], [k.CX[:, :, 32 * q:32 * q + 32] for q in range(3)], (a.ckvs_ready, 1)
        if kind == "rank":
            reg, r = rank_region(c)
            return (reg.rearrange("p a (r d) -> p (a r) d", d=32), [k.XR[:, c, :, 32 * q:32 * q + 32] for q in range(3)],
                    (r.full, r.nth(f"xr{c}")))
        if kind == "content":
            return qcT[:, c, :], [q3s[:, 0, c, q, :] for q in range(3)], (a.qc_ready, c + 1)
        return qa[:, c, :], [q3s[:, 1, c, q, :] for q in range(3)], (a.qa_ready, c + 1)
    order = [("value", 0), ("rank", 0), ("rank", 1), ("content", 0), ("content", 1), ("rope", 0), ("rope", 1),
             ("rank", 2), ("rank", 3)]

    pool_lo = [order.index(("rank", j)) for j in range(TILES - 1)]

    def lo_count(s):
        return len([i for i in range(s + 1) if i not in pool_lo])

    def rest_of(s):
        kind = order[s][0]
        if kind == "value":
            return rest[:, s, 0:TILES * 32].rearrange("p (i d) -> p i d", d=32)
        if kind == "rank":
            return rest[:, s, :].rearrange("p (r d) -> p r d", d=32)
        return rest[:, s, 0:L]

    with nc.Block() as block:
        @block.tensor
        def _(pe):
            mm = nc.tensor.matmul
            xnT = k.xnT[:, WIN:]
            def turn_ranks(j):
                reg, r = rank_region(j)
                r.start(pe, f"xr{j}", a.rest_ready, order.index(("rank", j)) + 1)
                for e in range(2):
                    last = mm(reg[:, e, :], k.soft_kr[32:64, 0, tile(j)], k.rot_tab[:, e * 512:(e + 1) * 512],
                              start=True, stop=True)
                last.then_inc(r.full, 1)

            rZ.start(pe, "ckv", a.cq_ready, 1)
            mm(k.Z[0:CQ, 1, :], W("dq"), xnT, start=True, stop=True)
            mm(k.Z[:, 0, :], W("dkv4"), xnT, start=True, stop=True).then_inc(rZ.full, 1)
            rW.start(pe, "ckvs", a.ckvs_ready, 1)
            for i in range(TILES):
                for w in range(NW_T):
                    at = i * P + WIN * w
                    last = mm(k.Wb[:, (NW_T * i + w) * 32:(NW_T * i + w + 1) * 32], k.xnT[:, at:at + P],
                              W("dkv4", 0, CKV), start=True, stop=True)
            last.then_inc(rW.full, 1)
            pe.wait_ge(a.cq_ready, 1)
            for c in range(2):
                reg, r = soft_region(c)
                r.start(pe, f"qr{c}", a.soft_ready, c + 1)
                mm(reg[:, 0, :], W("qr", c * P, P, rows=CQ), cqT[:, :], start=True, stop=True)
                mm(reg[:, 1, :], W("qrp", c * P, P, rows=CQ), cqT[:, :], start=True, stop=True).then_inc(r.full, 1)
                if c == 0:
                    turn_ranks(0)
            rU.start(pe, "qc0", a.qc_ready, 1)
            mm(k.Ub, k.m1[:, 0:P], cqT[:, :], start=True, stop=True).then_inc(rU.full, 1)
            rW.start(pe, "qc1", a.qc_ready, 2)
            mm(k.Wb, k.m1[:, P:2 * P], cqT[:, :], start=True, stop=True).then_inc(rW.full, 1)
            for j in range(1, TILES):
                turn_ranks(j)

        @block.scalar
        def _(act):
            op = nc.scalar.activation

            def magnitude(n):
                reg, r = soft_region(n)
                act.wait_ge(r.full, r.nth(f"qr{n}"))
                op(mag[:, n, :, :], reg, ACT.Abs).then_inc(a.abs_ready, 1)

            def exponential(n):
                act.wait_ge(a.abs_ready, n + 1)
                op(mag[:, n, :, :], mag[:, n, :, :], ACT.Exp, scale=-1.0).then_inc(a.expn_ready, 1)

            def logarithm(n):
                act.wait_ge(a.expn_ready, n + 1)
                op(mag[:, n, :, :], mag[:, n, :, :], ACT.Ln, bias=1.0).then_inc(a.log_ready, 1)

            def hi(s):
                src, dst, ready = split_job(*order[s])
                act.wait_ge(*ready)
                op(dst[0], src, ACT.Copy).then_inc(a.hi_ready, 1)

            def mid(s):
                act.wait_ge(a.rest_ready, s + 1)
                op(split_job(*order[s])[1][1], rest_of(s), ACT.Copy).then_inc(a.mid_ready, 1)

            act.wait_ge(rZ.full, rZ.nth("ckv"))
            op(cqT[:, :], k.Z[0:CQ, 1, :], ACT.Copy)
            act.wait_ge(a.keys_zeroed, 1)
            for e in range(2):
                rows = slice(32 * e, 32 * e + 32)
                last = op(k.key[rows, e, WIN:], k.Z[rows, 0, :], ACT.Copy)
            last.then_inc(a.cq_ready, 1)
            hi(0)
            magnitude(0)
            exponential(0)
            hi(1)
            magnitude(1)
            exponential(1)
            mid(0)
            mid(1)
            logarithm(0)
            logarithm(1)
            hi(2)
            for s in range(3, len(order)):
                hi(s)
                mid(s - 1)
            mid(len(order) - 1)

        @block.gpsimd
        def _(pool):
            tt = nc.gpsimd.tensor_tensor
            def products(values, tab):
                tt(pprod[:, :, :], values, k.C2(tab), ALU.mult).then_inc(a.pool_prod, 1)
            pool.wait_ge(a.keys_zeroed, 1)
            products(k.soft_kr[:, :, :], "tab_a")
            pool.wait_ge(a.pool_prod, 1)
            for e in range(2):
                rows = slice(64 + 32 * e, 64 + 32 * e + 32)
                last = tt(k.key[rows, e, WIN:], pprod[rows, 0, :], pprod[rows, 1, :], ALU.add)
            last.then_inc(a.krT_ready, 1)
            pool.wait_ge(a.krT_ready, 1)

            def lo(s):
                pool.wait_ge(a.mid_ready, s + 1)
                _, dst, _ = split_job(*order[s])
                tt(dst[2], rest_of(s), dst[1], ALU.subtract).then_inc(a.lo_pool, 1)
                pool.wait_ge(a.lo_pool, pool_lo.index(s) + 1)
            lo(pool_lo[0])
            for c in range(2):
                pool.wait_ge(a.soft_ready, c + 1)
                products(soft[:, c, :, :], "tab_b")
                pool.wait_ge(a.pool_prod, c + 2)
                for e in range(2):
                    rows = slice(64 * e, 64 * e + 64)
                    last = tt(k.q_loc[64:128, 2 * c + e, :], pprod[rows, 0, :], pprod[rows, 1, :], ALU.add)
                last.then_inc(a.qb_ready, 1)
                pool.wait_ge(a.qb_ready, c + 1)
            for s in pool_lo[1:]:
                lo(s)

        @block.vector
        def _(dve):
            ve = nc.vector
            step = [0]

            def link(ins):
                step[0] += 1
                ins.then_inc(a.l_step, 1)
                dve.wait_ge(a.l_step, step[0])

            def copy_content(c):
                bank, r = ((7, rU), (6, rW))[c]
                dve.wait_ge(r.full, r.nth(f"qc{c}"))
                for e in range(2):
                    ve.tensor_copy(k.q_loc[0:64, 2 * c + e, :], k.PS[64 * e:64 * e + 64, bank, :])
                ve.tensor_copy(qcT[:, c, :], k.PS[:, bank, :]).then_inc(a.qc_ready, 1)

            def softplus(n):
                reg, r = soft_region(n)
                dve.wait_ge(a.log_ready, n + 1)
                ve.scalar_tensor_tensor(soft[:, n, :, :], reg, 0.0, mag[:, n, :, :], ALU.max,
                                        ALU.add).then_inc(a.soft_ready, 1)
                dve.wait_ge(a.soft_ready, n + 1)

            def rotate(dst, n, done):
                link(ve.tensor_tensor(prod[:, :, :], soft[:, n, :, :], k.C2("tab_a"), ALU.mult))
                ve.tensor_tensor(dst, prod[:, 0, :], prod[:, 1, :], ALU.add).then_inc(done, 1)

            def take_hi(s):
                dve.wait_ge(a.hi_ready, s + 1)
                src, dst, _ = split_job(*order[s])
                ve.tensor_tensor(rest_of(s), src, dst[0], ALU.subtract).then_inc(a.rest_ready, 1)

            def lo(s):
                if s in pool_lo:
                    return
                dve.wait_ge(a.mid_ready, s + 1)
                _, dst, _ = split_job(*order[s])
                ve.tensor_tensor(dst[2], rest_of(s), dst[1], ALU.subtract).then_inc(a.lo_ready, 1)

            ve.memset(k.key[:, :, :], 0.0).then_inc(a.keys_zeroed, 1)
            dve.wait_ge(a.keys_zeroed, 1)
            dve.wait_ge(rW.full, rW.nth("ckvs"))
            ve.tensor_copy(k.ckvS[:, :, :, :], k.Wb[:, 0:TILES * NW_T * 32].rearrange("p (i w d) -> p i w d", w=NW_T, d=32)).then_inc(a.ckvs_ready, 1)
            take_hi(0)
            take_hi(1)
            copy_content(0)
            copy_content(1)
            lo(0)
            lo(1)
            softplus(0)
            softplus(1)
            take_hi(2)
            for s in range(3, len(order)):
                if s - 3 < 2:
                    rotate(qa[:, s - 3, :], s - 3, a.qa_ready)
                    dve.wait_ge(a.qa_ready, s - 2)
                if order[s][0] == "content":
                    dve.wait_ge(a.qc_ready, 2)
                take_hi(s)
                lo(s - 1)
            lo(len(order) - 1)

        @block.sync
        def _(sp):
            for n, loaded in enumerate((a.idx_loaded0, a.idx_loaded1)):
                sp.dma_start(k.idxb[:, n, :].rearrange("p (r t) -> p r t", r=RB),
                             k.scratch[n * RB:(n + 1) * RB, 0:P].partition_broadcast(P)).then_inc(loaded, 16)
            for kind, name in enumerate(("content", "rope")):
                for c in range(2):
                    sp.wait_ge(a.lo_ready, lo_count(order.index((name, c))))
                    sp.dma_start(k.q_scratch[kind, :, c * P:(c + 1) * P, :].rearrange("q p t -> p q t"),
                                 q3s[:, kind, c, :, :]).then_inc(a.q3_stored, 16)
            sp.wait_ge(a.q3_stored, 64)


def attend(nc, b, k, scope):
    F, BF, FH = mybir.dt.float32, mybir.dt.bfloat16, mybir.dt.float16
    ALU, ACT, AX = mybir.AluOpType, mybir.ActivationFunctionType, mybir.AxisListType
    a, C, W = k.sems, k.C, k.W

    def sb(name, shape, dt=F):
        return k.sb(name, shape, dt, scope)
    QTR = FAR // RB
    NF = TILES * QTR
    OCT = 4
    idxb = k.idxb
    onehot = sb("onehot", [P, 2, TILES, RB * P], BF)
    KC, KR = sb("KC", [96, 2, 32, P], BF), sb("KR", [96, 2, 32, P], BF)
    q3 = sb("q3", [96, 2, 24, P], BF)
    V = sb("V", [P, 2, 32, CKV])
    J = SLOTS + FAR
    SC = sb("SC", [P, 2, HEADS, J])
    SN = k.xnT[:, WIN:WIN + 256].rearrange("p (h t) -> p h t", h=HEADS)
    PN = k.xnT[:, WIN + 256:WIN + 512].rearrange("p (h t) -> p h t", h=HEADS)
    nmax, bias = sb("jmax", [P, 2, HEADS]), sb("jbias", [P, 2, HEADS])
    rsum, rrec = sb("jsum", [P, 2, HEADS]), sb("jrec", [P, 2, HEADS])
    PT = sb("PT", [P, HEADS, P])
    PB = sb("PB", [P, 32, GR, HEADS])
    OT = k.soft_kr[0:CKV, :, :]
    fT, o_sb = sb("fT", [P, P]), sb("o_sb", [P, 2, D])
    rX, rY, rZ, rW, _ = (Region(full) for full in a.attend_full)
    O2 = k.PS[:, 6:8, :]

    def quad_region(i, o):
        if i < TILES - 1:
            return k.X, rX
        return (k.Y, rY) if o % 2 == 0 else (k.Z, rZ)

    def tile(i):
        return slice(i * P, (i + 1) * P)

    with nc.Block() as block:
        @block.tensor
        def _(pe):
            mm = nc.tensor.matmul

            def fetch(n):
                i, q = n // QTR, n % QTR
                pe.wait_ge(a.onehot_ready, n + 1)
                rZ.start(pe, f"gc{n}", a.kc_ready, n + 1)
                for e in range(2):
                    for j in range(i + 1):
                        last = mm(k.Z[0:96, e, :], k.CX[:, j, :], onehot[:, n % 2, j, e * 512:(e + 1) * 512],
                                  start=(j == 0), stop=(j == i))
                last.then_inc(rZ.full, 1)
                rY.start(pe, f"gr{n}", a.kr_far_ready, n + 1)
                for r in range(RB):
                    for j in range(i + 1):
                        last = mm(k.Y[0:96, r // 4, (r % 4) * P:(r % 4 + 1) * P], k.XR[:, j, q * RB + r, :],
                                  onehot[:, n % 2, j, r * P:(r + 1) * P], start=(j == 0), stop=(j == i))
                last.then_inc(rY.full, 1)

            def local_scores(i):
                rX.start(pe, f"ls{i}", a.lmasked, i + 1)
                for h in range(HEADS):
                    c, s0 = h // 4, (h % 4) * P
                    for w in range(NW_T):
                        t0 = i * P + w * WIN
                        out = k.X[64 * w:64 * w + 64, c, s0:s0 + P]
                        last = mm(out, k.q_loc[:, h // 2, t0:t0 + WIN], k.key[:, h % 2, t0:t0 + SLOTS], start=True, stop=True)
                last.then_inc(rX.full, 1)

            def far_scores(i, o):
                reg, r = quad_region(i, o)
                r.start(pe, f"fs{i}.{o}", a.far_ready, OCT * i + o + 1)
                if o == 0:
                    pe.wait_ge(a.kc_ready, QTR * (i + 1))
                    pe.wait_ge(a.kr_far_ready, QTR * (i + 1))
                    pe.wait_ge(a.q3_loaded, 96 * (i + 1))
                for q in range(8):
                    t, out = 8 * o + q, reg[:, q // 4, (q % 4) * P:(q % 4 + 1) * P]
                    mm(out[:, 96:P], KC[:, i % 2, t, :], k.istack[:, :], start=True, stop=True)
                    mm(out[:, 0:96], KC[:, i % 2, t, :], q3[:, 0, :, t::32], start=True, stop=False)
                    last = mm(out[:, 0:96], KR[:, i % 2, t, :], q3[:, 1, :, t::32], start=False, stop=True)
                last.then_inc(r.full, 1)

            def probs_T(i):
                rX.start(pe, f"lt{i}", a.jpT_ready, i + 1)
                pe.wait_ge(a.jnormed, i + 1)
                for h in range(HEADS):
                    last = nc.tensor.transpose(k.X[:, h // 4, (h % 4) * P:(h % 4 + 1) * P], SC[:, i % 2, h, 0:SLOTS], C("ident"))
                last.then_inc(rX.full, 1)

            def weigh(i):
                rW.start(pe, f"pv{i}", a.oT_ready, i + 1)
                pe.wait_ge(a.jpT_ready, i + 1)
                pe.wait_ge(a.blocks_ready, i + 1)
                for e in range(2):
                    for w in range(NW_T):
                        mm(O2[0:CKV, e, :].rearrange("p (t g h) -> p t g h", g=GR, h=HEADS)[:, :, 2 * w:2 * w + 2, :],
                           k.ckvS[:, i, w, :],
                           PT[:, :, :].rearrange("p h (g t) -> p t g h", g=GR)[:, 16 * e:16 * e + 16, 2 * w:2 * w + 2, :],
                           start=(w == 0), stop=False, skip_group_check=True)
                    for t in range(16 * e, 16 * e + 16):
                        last = mm(O2[0:CKV, e, (t % 16) * 32:(t % 16 + 1) * 32], V[:, i % 2, t, :],
                                  PB[:, t, :, :].rearrange("p g h -> p (g h)"), start=False, stop=True,
                                  skip_group_check=True)
                last.then_inc(rW.full, 1)

            def project_out(i):
                rW.start(pe, f"so{i}", a.fT_ready, i + 1)
                pe.wait_ge(a.oT_ready, i + 1)
                heads = OT[:, :, :].rearrange("p a (t g h) -> p h g (a t)", g=GR, h=HEADS)
                for h in range(HEADS):
                    last = mm(k.Ub[:, 0:P], k.mo[:, h * D:(h + 1) * D], heads[:, h, :, :],
                              start=(h == 0), stop=(h == HEADS - 1))
                last.then_inc(rW.full, 1)

            def turn_back(i):
                rW.start(pe, f"fin{i}", a.out_ready, i + 1)
                pe.wait_ge(a.fT_ready, i + 1)
                nc.tensor.transpose(k.Wb[:, 0:P], fT[:, :], C("ident")).then_inc(rW.full, 1)

            for n in range(QTR):
                fetch(n)
            local_scores(0)
            for i in range(TILES):
                nxt = QTR * (i + 1)
                for o in range(OCT):
                    if i + 1 < TILES:
                        fetch(nxt + o)
                    if i and o == 2:
                        probs_T(i - 1)
                    if i and o == 3:
                        weigh(i - 1)
                    far_scores(i, o)
                if i:
                    project_out(i - 1)
                if i + 1 < TILES:
                    local_scores(i + 1)
                if i:
                    turn_back(i - 1)
            probs_T(TILES - 1)
            weigh(TILES - 1)
            project_out(TILES - 1)
            turn_back(TILES - 1)

        @block.sync
        def _(sp):
            loads, stores = (a.idx_loaded0, a.idx_loaded1), (a.out_stored0, a.out_stored1)

            def load_q3(i, kinds=(0, 1)):
                if i:
                    sp.wait_ge(a.far_ready, OCT * i)
                for kind in kinds:
                    for part in range(3):
                        sp.dma_start(q3[32 * part:32 * part + 32, kind, :, :],
                                     k.q_scratch[kind, :, :, tile(i)].rearrange("q (c d) t -> d (q c) t", d=32)
                                     ).then_inc(a.q3_loaded, 16)

            def load_idx(n):
                i, q = n // QTR, n % QTR
                if n >= 2:
                    sp.wait_ge(a.onehot_ready, n - 1)
                sp.dma_start(idxb[:, n % 2, :].rearrange("p (r t) -> p r t", r=RB),
                             k.scratch[q * RB:(q + 1) * RB, tile(i)].partition_broadcast(P)).then_inc(loads[n % 2], 16)
            def store(i):
                sp.wait_ge(a.out_ready, i + 1)
                sp.dma_start(k.out_d[bass.ds(b, 1), tile(i), :].rearrange("a p d -> (a p) d"), o_sb[:, i % 2, :]).then_inc(stores[i % 2], 16)

            load_idx(2)
            load_idx(3)
            load_q3(0, (0,))
            load_idx(4)
            load_q3(0, (1,))
            load_idx(5)
            sp.dma_start(k.x_next[:, :, :], k.x_d[bass.ds(b + 1, 1), :, :].rearrange("a (i p) d -> p (a i) d", p=P)
                         ).then_inc(a.x_loaded, 16)
            for i in range(TILES):
                for n in range(QTR * (i + 1) + 2, min(QTR * (i + 2) + 2, NF)):
                    load_idx(n)
                if i + 1 < TILES:
                    load_q3(i + 1)
                if i:
                    store(i - 1)
            store(TILES - 1)
            sp.wait_ge(a.out_stored0, 16 * TILES // 2)
            sp.wait_ge(a.out_stored1, 16 * TILES // 2)
            sp.wait_ge(a.x_loaded, 16)

        @block.gpsimd
        def _(pool):
            for s in a.of_project + a.of_latents:
                nc.gpsimd.sem_clear(s)
            nc.gpsimd.memset(PB[:, :, :, :], 0.0).then_inc(a.blocks_zeroed, 1)
            for i in range(TILES - 1):
                pool.wait_ge(a.jrecip_ready, i + 1)
                nc.gpsimd.tensor_tensor(SC[:, i % 2, :, :], SC[:, i % 2, :, :],
                                        rrec[:, i % 2, :].unsqueeze(2).broadcast_to([P, HEADS, J]), ALU.mult).then_inc(a.jnormed, 1)

        @block.scalar
        def _(act):
            op = nc.scalar.activation

            def keep_content(n):
                i, q = n // QTR, n % QTR
                act.wait_ge(rZ.full, rZ.nth(f"gc{n}"))
                op(KC[:, i % 2, :, :].rearrange("p t (g r) -> p r g t", g=GR)[:, q * RB:(q + 1) * RB, :, :],
                   k.Z[0:96, :, :].rearrange("p a (r g t) -> p (a r) g t", g=GR, t=32), ACT.Copy).then_inc(a.kc_ready, 1)

            def keep_values(i, o):
                reg, r = quad_region(i, o)
                act.wait_ge(r.full, r.nth(f"fs{i}.{o}"))
                if o == 0 and i >= 2:
                    act.wait_ge(rW.full, rW.nth(f"pv{i - 2}"))
                op(V[:, i % 2, 8 * o:8 * o + 8, :], reg.rearrange("p a (q c) -> p (a q) c", c=P)[:, :, 96:P],
                   ACT.Copy).then_inc(a.vfar_ready, 1)

            def exps(i):
                act.wait_ge(a.bias_ready, i + 1)
                for h in range(HEADS):
                    last = op(SC[:, i % 2, h, :], SC[:, i % 2, h, :], ACT.Exp, bias=bias[:, i % 2, h:h + 1], scale=SCALE,
                              accum_out=rsum[:, i % 2, h:h + 1])
                last.then_inc(a.jprob_ready, 1)

            def copy_PT(i):
                act.wait_ge(rX.full, rX.nth(f"lt{i}"))
                op(PT[:, :, :], k.X.rearrange("p a (h t) -> p (a h) t", h=4), ACT.Copy).then_inc(a.jpT_ready, 1)

            def copy_OT(i):
                act.wait_ge(rW.full, rW.nth(f"pv{i}"))
                op(OT[:, :, :], O2[0:CKV, :, :], ACT.Copy).then_inc(a.oT_ready, 1)

            for n in range(QTR):
                keep_content(n)
            for i in range(TILES):
                for o in range(OCT):
                    if i + 1 < TILES:
                        keep_content(QTR * (i + 1) + o)
                    if i and o == 2:
                        copy_PT(i - 1)
                    if i and o == 3:
                        copy_OT(i - 1)
                    keep_values(i, o)
                exps(i)
            copy_PT(TILES - 1)
            copy_OT(TILES - 1)

        @block.vector
        def _(dve):
            ve = nc.vector
            loads, stores = (a.idx_loaded0, a.idx_loaded1), (a.out_stored0, a.out_stored1)
            step = [0]

            def link(ins):
                step[0] += 1
                ins.then_inc(a.d_step, 1)
                dve.wait_ge(a.d_step, step[0])

            def one_hots(n):
                i = n // QTR
                dve.wait_ge(loads[n % 2], 16 * (n // 2 + 1))
                for j in range(i + 1):
                    last = ve.tensor_scalar(onehot[:, n % 2, j, :], idxb[:, n % 2, :], C("iota")[:, j:j + 1], None, ALU.is_equal)
                last.then_inc(a.onehot_ready, 1)

            def keep_rope(n):
                i, q = n // QTR, n % QTR
                dve.wait_ge(rY.full, rY.nth(f"gr{n}"))
                ve.tensor_copy(KR[:, i % 2, :, :].rearrange("p t (g r) -> p r g t", g=GR)[:, q * RB:(q + 1) * RB, :, :],
                               k.Y[0:96, :, :].rearrange("p a (r g t) -> p (a r) g t", g=GR, t=32)).then_inc(a.kr_far_ready, 1)

            def mask_local(i):
                dve.wait_ge(rX.full, rX.nth(f"ls{i}"))
                ve.tensor_tensor(SC[:, i % 2, :, 0:SLOTS], k.X.rearrange("p a (h s) -> p (a h) s", h=4),
                                 C("mask_a0" if i == 0 else "mask_a").unsqueeze(1).broadcast_to([P, HEADS, SLOTS]),
                                 ALU.add).then_inc(a.lmasked, 1)

            def take_scores(i, o):
                reg, r = quad_region(i, o)
                dve.wait_ge(r.full, r.nth(f"fs{i}.{o}"))
                dve.wait_ge(a.vfar_ready, OCT * i + o + 1)
                for g in range(GR):
                    part = reg[32 * g:32 * g + 32, :, :].rearrange("p a (q c) -> p (a q) c", c=P)[:, :, 0:96]
                    part = part.rearrange("p q (k h g) -> p q h k g", k=3, g=GR)[:, :, :, :, g]
                    last = ve.tensor_reduce(SN[32 * g:32 * g + 32, :, 8 * o:8 * o + 8].rearrange("p h t -> p t h"),
                                            part, AX.X, ALU.add)
                last.then_inc(a.far_ready, 1)

            def join_max(i):
                dve.wait_ge(a.far_ready, OCT * (i + 1))
                ve.transpose(SC[:, i % 2, :, SLOTS:J], SN).then_inc(a.joined, 1)
                dve.wait_ge(a.joined, i + 1)
                dve.wait_ge(a.lmasked, i + 1)
                ve.tensor_reduce(nmax[:, i % 2, :], SC[:, i % 2, :, :], AX.X, ALU.max, negate=True).then_inc(a.jmax_ready, 1)
                dve.wait_ge(a.jmax_ready, i + 1)
                ve.tensor_scalar(bias[:, i % 2, :], nmax[:, i % 2, :], SCALE, None, ALU.mult).then_inc(a.bias_ready, 1)

            def recips(i):
                dve.wait_ge(a.jprob_ready, i + 1)
                ve.reciprocal(rrec[:, i % 2, :], rsum[:, i % 2, :]).then_inc(a.jrecip_ready, 1)

            def spread_blocks(i):
                dve.wait_ge(a.jnormed, i + 1)
                link(ve.transpose(PN, SC[:, i % 2, :, SLOTS:J]))
                if i:
                    dve.wait_ge(a.oT_ready, i)
                else:
                    dve.wait_ge(a.blocks_zeroed, 1)
                for g in range(GR):
                    e = slice(32 * g, 32 * g + 32)
                    last = ve.tensor_copy(PB[e, :, g, :], PN[e, :, :].rearrange("p h t -> p t h"))
                last.then_inc(a.blocks_ready, 1)

            def gate_out(i):
                dve.wait_ge(rW.full, rW.nth(f"so{i}"))
                ve.tensor_tensor(fT[:, :], k.Ub[:, 0:P], k.gate[:, tile(i)], ALU.mult).then_inc(a.fT_ready, 1)

            def add_residual(i):
                dve.wait_ge(rW.full, rW.nth(f"fin{i}"))
                if i >= 2:
                    dve.wait_ge(stores[i % 2], 16 * (i // 2))
                ve.tensor_tensor(o_sb[:, i % 2, :], k.Wb[:, 0:P], k.x_in[:, i, :], ALU.add).then_inc(a.out_ready, 1)

            one_hots(0)
            for n in range(QTR - 1):
                one_hots(n + 1)
                keep_rope(n)
            keep_rope(QTR - 1)
            mask_local(0)
            one_hots(QTR)
            for i in range(TILES):
                for o in range(OCT):
                    n = QTR * (i + 1) + o
                    if n + 1 < NF:
                        one_hots(n + 1)
                    if n < NF:
                        keep_rope(n)
                    if i and o == 0:
                        recips(i - 1)
                    if i and o == 2:
                        spread_blocks(i - 1)
                    take_scores(i, o)
                join_max(i)
                if i:
                    gate_out(i - 1)
                if i + 1 < TILES:
                    mask_local(i + 1)
                if i:
                    add_residual(i - 1)
            recips(TILES - 1)
            dve.wait_ge(a.jrecip_ready, TILES)
            ve.tensor_tensor(SC[:, (TILES - 1) % 2, :, :], SC[:, (TILES - 1) % 2, :, :],
                             rrec[:, (TILES - 1) % 2, :].unsqueeze(2).broadcast_to([P, HEADS, J]), ALU.mult).then_inc(a.jnormed, 1)
            spread_blocks(TILES - 1)
            gate_out(TILES - 1)
            add_residual(TILES - 1)


def build(nc, x_d, const_d, rot_d, weights_d, setup_d, scratch, q_scratch, out_d):
    F, BF, FH, U32 = mybir.dt.float32, mybir.dt.bfloat16, mybir.dt.float16, mybir.dt.uint32
    ALU, ACT, AX = mybir.AluOpType, mybir.ActivationFunctionType, mybir.AxisListType
    cc, rr, ww, ss = layout()
    top = ExitStack()
    with top:
        def sb(name, shape, dt=F, ctx=top):
            return ctx.enter_context(nc.sbuf_tensor(name, shape, dt))

        def sem(name):
            return top.enter_context(nc.semaphore(name))

        consts = sb("consts", [P, cc.n])
        wts = sb("wts", [P, ww.n])
        istack = sb("istack_bf", [96, 32], BF)
        m1 = sb("m1", [CQ, HEADS * CKV])
        mo_rot = sb("mo_rot", [2 * CKV, HEADS * D])
        mo = mo_rot[0:CKV, :]
        rot_tab = mo_rot[CKV:2 * CKV, :]
        x_in, x_next = sb("x_in", [P, TILES, D]), sb("x_next", [P, TILES, D])
        xnT = sb("xnT", [P, WIN + L])
        soft_kr = sb("soft_kr", [P, 2, L])
        gate = sb("gate", [P, L])
        idx_h = sb("idx_h", [P, TILES, 32], FH)

        def C(name, rows=P):
            return consts[0:rows, cc.at[name][0]:cc.at[name][1]]

        def C2(tab):
            s = cc.at[tab + "_c"][0]
            return consts[:, s:s + 2 * L].rearrange("p (a t) -> p a t", a=2)

        def W(name, lo=0, width=None, r0=0, rows=P):
            s = ww.at[name][0] + lo
            return wts[r0:r0 + rows, s:(ww.at[name][1] if width is None else s + width)]

        PS = top.enter_context(nc.psum_tensor("PS", [P, 8, 512], F))
        X, Y, Z, Wb, Ub = PS[:, 0:2, :], PS[:, 2:4, :], PS[:, 4:6, :], PS[:, 6, :], PS[:, 7, :]

        loaded, setup_pe, setup_act, setup_dve = (sem(n) for n in ("loaded", "setup_pe", "setup_act", "setup_dve"))
        with ExitStack() as scope:
            rots = sb("rots", [2 * CKV, rr.n], F, scope)
            setw = sb("setw", [64, ss.n], F, scope)
            sig = sb("sig", [P, 8], F, scope)
            tmp_t = sb("tmp_t", [P, L], F, scope)

            def S(name, lo, width):
                s = ss.at[name][0] + lo
                return setw[0:64, s:s + width]

            with nc.Block() as block:
                @block.sync
                def _(sp):
                    sp.dma_start(consts[:, :], const_d).then_inc(loaded, 16)
                    sp.dma_start(wts[:, :], weights_d).then_inc(loaded, 16)
                    sp.dma_start(setw[:, :], setup_d).then_inc(loaded, 16)
                    sp.dma_start(rots[CKV:, :], rot_d).then_inc(loaded, 16)
                    sp.dma_start(x_next[:, :, :], x_d[0:1, :, :].rearrange("a (i p) d -> p (a i) d", p=P)).then_inc(loaded, 16)

                @block.tensor
                def _(pe):
                    pe.wait_ge(loaded, 80)
                    for h in range(HEADS):
                        nc.tensor.matmul(PS[0:CQ, 0, h * CKV:(h + 1) * CKV], S("uqT", h * CQ, CQ),
                                         S("ukT", h * CKV, CKV), start=True, stop=True)
                        nc.tensor.matmul(PS[0:CKV, 2 + h // 4, (h % 4) * D:(h % 4 + 1) * D],
                                         S("uvT", h * CKV, CKV), S("out", h * D, D),
                                         start=True, stop=True).then_inc(setup_pe, 1)
                    for l in range(LAYERS):
                        for j, (off, n) in enumerate(HCH):
                            for half in range(2):
                                at = (3 * l + j) * 2 + half
                                last = nc.tensor.matmul(PS[0:n, 1, at:at + 1],
                                                        W("w1", l * 2 * HID + half * HID + off, n), W("lnb", l, 1),
                                                        start=True, stop=True)
                    last.then_inc(setup_pe, 1)

                @block.scalar
                def _(act):
                    act.wait_ge(loaded, 80)
                    nc.scalar.activation(sig[:, 0:1], W("delta"), ACT.Sigmoid).then_inc(setup_act, 1)
                    act.wait_ge(setup_act, 1)
                    nc.scalar.activation(sig[:, 1:2], sig[:, 0:1], ACT.Sin, bias=C("negpi"),
                                         scale=float(2 * np.pi)).then_inc(setup_act, 1)
                    nc.scalar.activation(sig[:, 2:3], sig[:, 0:1], ACT.Sin, scale=float(np.pi)).then_inc(setup_act, 1)

                @block.vector
                def _(dve):
                    n = [0]

                    def link(ins):
                        n[0] += 1
                        ins.then_inc(setup_dve, 1)
                        dve.wait_ge(setup_dve, n[0])
                    dve.wait_ge(loaded, 80)
                    link(nc.vector.memset(xnT[:, 0:WIN], 0.0))
                    link(nc.vector.tensor_copy(istack[:, :], C("istack", 96)))
                    dve.wait_ge(setup_act, 3)
                    link(nc.vector.tensor_tensor(sig[:, 3:4], sig[:, 2:3], sig[:, 2:3], ALU.mult))
                    link(nc.vector.tensor_scalar(sig[:, 4:5], sig[:, 3:4], -2.0, 1.0, ALU.mult, ALU.add))
                    link(nc.vector.tensor_tensor(sig[:, 5:6], sig[:, 1:2], C("sgn"), ALU.mult))
                    link(nc.vector.tensor_scalar(sig[:, 6:7], sig[:, 5:6], -1.0, None, ALU.mult))
                    cosd, sins, neg_sins = sig[:, 4:5], sig[:, 5:6], sig[:, 6:7]
                    for tab in ("tab_a", "tab_b"):
                        tc, ts = C(tab + "_c"), C(tab + "_s")
                        link(nc.vector.tensor_scalar(tmp_t[:, :], tc, sins, None, ALU.mult))
                        link(nc.vector.tensor_scalar(tc, tc, cosd, None, ALU.mult))
                        link(nc.vector.scalar_tensor_tensor(tc, ts, neg_sins, tc, ALU.mult, ALU.add))
                        link(nc.vector.scalar_tensor_tensor(ts, ts, cosd, tmp_t[:, :], ALU.mult, ALU.add))
                    link(nc.vector.tensor_scalar(rot_tab, rots[CKV:, 0:FAR * 32], sig[32:64, 4:5], None, ALU.mult))
                    link(nc.vector.scalar_tensor_tensor(rot_tab, rots[CKV:, FAR * 32:], sig[32:64, 1:2],
                                                        rot_tab, ALU.mult, ALU.add))
                    dve.wait_ge(setup_pe, HEADS + 1)
                    for l in range(LAYERS):
                        w1 = W("w1", l * 2 * HID, 2 * HID)
                        link(nc.vector.tensor_scalar(w1, w1, W("lng", l, 1), None, ALU.mult))
                        for j, (_, rows) in enumerate(HCH):
                            for half, name in enumerate(("b1a", "b1g")):
                                bias, at = W(name, 3 * l + j, 1, rows=rows), (3 * l + j) * 2 + half
                                link(nc.vector.tensor_tensor(bias, bias, PS[0:rows, 1, at:at + 1], ALU.add))
                    link(nc.vector.tensor_copy(m1[:, :], PS[0:CQ, 0, 0:HEADS * CKV]))
                    link(nc.vector.tensor_copy(mo, PS[0:CKV, 2:4, :].rearrange("p a b -> p (a b)")))
        nc.all_engine_barrier()

        k = Core()
        k.sb, k.C, k.W, k.PS, k.X, k.Y, k.Z, k.Wb, k.Ub = sb, C, W, PS, X, Y, Z, Wb, Ub
        k.x_next, k.C2, k.soft_kr = x_next, C2, soft_kr
        k.x_in, k.xnT, k.gate, k.idx_h, k.istack, k.m1, k.mo, k.rot_tab = x_in, xnT, gate, idx_h, istack, m1, mo, rot_tab
        k.x_d, k.out_d, k.scratch, k.q_scratch = x_d, out_d, scratch, q_scratch
        k.sems = Signals(sem)

        with nc.Fori(0, B) as b:
            with ExitStack() as scope:
                project(nc, b, k, scope)
            nc.all_engine_barrier()
            with ExitStack() as kept:
                k.q_loc, k.key = sb("q_loc", [P, PAIRS, L], F, kept), sb("key", [P, 2, WIN + L], F, kept)
                k.CX, k.ckvS = sb("CX", [P, TILES, 96], BF, kept), sb("ckvS", [P, TILES, NW_T, CKV], F, kept)
                k.XR = sb("XR", [P, TILES, FAR, 96], BF, kept)
                k.idxb = sb("idxb", [P, 2, RB * P], FH, kept)
                with ExitStack() as scope:
                    latents(nc, b, k, scope)
                nc.all_engine_barrier()
                with ExitStack() as scope:
                    attend(nc, b, k, scope)
            nc.all_engine_barrier()


def kernel(**inputs):
    import concourse.bacc as bacc
    from concourse.bass_utils import run_bass_kernel_spmd

    v = {n: np.asarray(a) for n, a in inputs.items()}
    g = {n[len("L0_attn_"):]: a for n, a in v.items() if n.startswith("L0_attn_")}
    f = {n[len("L0_ffn_"):]: a for n, a in v.items() if n.startswith("L0_ffn_")}
    _, _, ww, ss = layout()
    consts, rots = constants()

    def rows(m, n=P):
        return np.concatenate([m, np.zeros((n - m.shape[0],) + m.shape[1:], np.float32)], 0) if m.shape[0] < n else m

    def swap(m, h):
        s = m.reshape(m.shape[:-1] + (-1, 2, h))
        return s[..., ::-1, :].reshape(m.shape)

    def col(m):
        return np.ascontiguousarray(m.T)

    def chunks(m):
        return rows(m, 3 * P).reshape(3, P).T

    qs, ks = f["q_scale"], f["k_scale"]
    qks = np.stack([np.concatenate([s, s]) for l in range(LAYERS)
                    for s in (qs[l], swap(qs[l], 32), ks[l], swap(ks[l], 32))], 1)
    pieces = {
        "dkv4": np.concatenate([g["W_dkv"]] * 4, 1), "dq": g["W_dq"],
        "kr4": np.concatenate([g["W_kr"]] * 4, 1), "kr4p": np.concatenate([swap(g["W_kr"], HALF)] * 4, 1),
        "idxq": g["idx_wq"], "idxk2": np.concatenate([g["idx_wk"]] * 2, 1),
        "qr": rows(g["W_qr"]), "qrp": rows(swap(g["W_qr"], HALF)),
        "qkv": np.concatenate(list(f["wqkv"]), 1),
        "rot": np.concatenate([swap(w[:, :2 * INNER], 32) for w in f["wqkv"]], 1),
        "wo": np.concatenate([w.reshape(PAIRS, P, D).transpose(1, 0, 2).reshape(P, -1) for w in f["wo"]], 1),
        "w1": np.concatenate(list(f["w1"]), 1),
        "w2": np.concatenate([rows(w, 3 * P).reshape(3, P, D).transpose(1, 0, 2).reshape(P, -1) for w in f["w2"]], 1),
        "qks": qks, "lng": col(f["ln_g"]), "lnb": col(f["ln_b"]),
        "b1a": np.concatenate([chunks(r[:HID]) for r in f["b1"]], 1),
        "b1g": np.concatenate([chunks(r[HID:]) for r in f["b1"]], 1),
        "b2": col(f["b2"]), "idxw": np.broadcast_to(g["idx_w"], (P, IDX_HEADS)),
        "delta": np.concatenate([g["raw_delta"]] * (P // HALF))[:, None],
    }
    weights = np.ascontiguousarray(np.concatenate([pieces[n] for n in ww.at], 1))

    def by_head(m, width):
        return m.reshape(m.shape[0], HEADS, width).transpose(2, 1, 0).reshape(width, -1)
    heads = {"uqT": by_head(g["W_uq"], DH), "ukT": by_head(g["W_uk"], DH), "uvT": by_head(g["W_uv"], DH),
             "out": g["W_out"].reshape(HEADS, DH, D).transpose(1, 0, 2).reshape(DH, -1)}
    setup = np.ascontiguousarray(np.concatenate([heads[n] for n in ss.at], 1))

    nc = bacc.Bacc("TRN2", target_bir_lowering=False, num_devices=1)
    dt = mybir.dt.float32
    arrays = {"x_dram": np.concatenate([g["x"], g["x"][:1]]), "consts_dram": consts, "rots_dram": rots,
              "weights_dram": weights, "setup_dram": setup}
    aps = {n: nc.dram_tensor(n, m.shape, dt, kind="ExternalInput").ap() for n, m in arrays.items()}
    out = nc.dram_tensor("out", (B, L, D), dt, kind="ExternalOutput").ap()
    idx_scratch = nc.dram_tensor("idx_scratch", (FAR, L), mybir.dt.float16).ap()
    q_scratch = nc.dram_tensor("q_scratch", (2, 3, HEADS * 32, L), mybir.dt.bfloat16).ap()
    build(nc, *aps.values(), idx_scratch, q_scratch, out)
    r = run_bass_kernel_spmd(nc, [arrays], core_ids=[0])
    return r.results[0]["out"]
```
